# Optimizing a Trainium2 kernel written in Bass

```python
import numpy as np
import jax
import jax.numpy as jnp

def _softmax(x, axis=-1):
    return jax.nn.softmax(x, axis=axis)

def _gelu(x):
    return jax.nn.gelu(x, approximate=True)

def _silu(x):
    return jax.nn.silu(x)

def _sigmoid(x):
    return jax.nn.sigmoid(x)

def _layernorm(x, axis=-1, eps=1e-05):
    m = jnp.mean(x, axis=axis, keepdims=True)
    v = jnp.var(x, axis=axis, keepdims=True)
    return (x - m) / jnp.sqrt(v + eps)

def _scatter_add(tgt, idx, src, axis=0):
    return tgt.at[idx].add(src)

def _segment_sum(src, seg, n):
    return jax.ops.segment_sum(src, seg, n)
kernel_name = 'mk_macaron_d2_jaxref_r8_b66eca'

def setup_inputs(seed: int=0):
    np.random.seed(seed)
    _w = jnp.asarray

    def _L0_attn_setup():
        import jax, jax.numpy as jnp
        import numpy as np
        B, N, E, D = (2, 512, 128, 128)
        H = E // D
        LN_EPS = 1e-05

        def _gla_scan(q, k, v, g):

            def step(S, inp):
                qt, kt, vt, gt = inp
                S = jnp.exp(gt)[..., None] * S + kt[..., None] * vt[..., None, :]
                ot = jnp.einsum('bhd,bhde->bhe', qt, S)
                return (S, ot)
            xs = tuple((jnp.moveaxis(a, 2, 0) for a in (q, k, v, g)))
            S0 = jnp.zeros(q.shape[:2] + (q.shape[-1], v.shape[-1]), q.dtype)
            _, o = jax.lax.scan(step, S0, xs)
            return jnp.moveaxis(o, 0, 2)
        key = jax.random.key(seed)
        ks = jax.random.split(key, 6)
        s = 0.02
        return {'x': jax.random.normal(ks[0], (B, N, E), jnp.float32), 'W_in': jax.random.normal(ks[1], (3 * E, E), jnp.float32) * s, 'W_out': jax.random.normal(ks[2], (E, E), jnp.float32) * s, 'W_g1': jax.random.normal(ks[3], (D, E), jnp.float32) * s, 'W_g2': jax.random.normal(ks[4], (E, D), jnp.float32) * s, 'ln_w': jnp.ones((E,), jnp.float32)}
    _L0_attn_in = _L0_attn_setup()

    def _L0_ffn_setup():
        import jax, jax.numpy as jnp
        import numpy as np
        B, S, D, M, E, K = (2, 256, 128, 176, 8, 2)
        key = jax.random.key(seed)
        k0, k1, k2, k3, k4 = jax.random.split(key, 5)
        scale = 0.02
        return {'x': jax.random.normal(k0, (B, S, D), dtype=jnp.float32), 'w_gate': jax.random.normal(k1, (D, E), dtype=jnp.float32) * scale, 'w_g': jax.random.normal(k2, (E, D, M), dtype=jnp.float32) * scale, 'w_u': jax.random.normal(k3, (E, D, M), dtype=jnp.float32) * scale, 'w_d': jax.random.normal(k4, (E, M, D), dtype=jnp.float32) * scale}
    _L0_ffn_in = _L0_ffn_setup()

    def _L1_attn_setup():
        import jax, jax.numpy as jnp
        import numpy as np
        D_MODEL = 128
        N_HEADS = 16
        D_HEAD = D_MODEL // N_HEADS
        EPS = 1e-05

        @jax.custom_vjp
        def spike(x):
            return (x >= 0).astype(x.dtype)

        def _spike_fwd(x):
            return (spike(x), x)

        def _spike_bwd(x, g):
            return (g / (1.0 + (jnp.pi * x) ** 2),)
        spike.defvjp(_spike_fwd, _spike_bwd)

        def lif(x, v_th):
            return spike(x - v_th)

        def layer_norm(x, g, b):
            mu = jnp.mean(x, axis=-1, keepdims=True)
            var = jnp.mean((x - mu) ** 2, axis=-1, keepdims=True)
            return (x - mu) * jax.lax.rsqrt(var + EPS) * g + b

        def log_pe_bias(n_q, n_k):
            pos_q = jnp.arange(n_q)[:, None]
            pos_k = jnp.arange(n_k)[None, :]
            dist = jnp.abs(pos_q - pos_k).astype(jnp.float32)
            max_len = max(n_q, n_k)
            bias = jnp.ceil(jnp.log2((max_len - 1) / (dist + 1.0)))
            return jnp.maximum(bias, 0.0)
        key = jax.random.key(seed)
        ks = jax.random.split(key, 16)
        D = D_MODEL
        std = 1.0 / np.sqrt(D)
        inp = {'query': jax.random.normal(ks[0], (2, 256, D), dtype=jnp.float32), 'Wq': jax.random.normal(ks[1], (D, D), dtype=jnp.float32) * std, 'bq': jnp.zeros((D,), jnp.float32), 'Wk': jax.random.normal(ks[2], (D, D), dtype=jnp.float32) * std, 'bk': jnp.zeros((D,), jnp.float32), 'Wv': jax.random.normal(ks[3], (D, D), dtype=jnp.float32) * std, 'bv': jnp.zeros((D,), jnp.float32), 'Wo': jax.random.normal(ks[4], (D, D), dtype=jnp.float32) * std, 'bo': jnp.zeros((D,), jnp.float32), 'gq': jnp.ones((D,), jnp.float32), 'betaq': jnp.zeros((D,), jnp.float32), 'gk': jnp.ones((D,), jnp.float32), 'betak': jnp.zeros((D,), jnp.float32), 'gv': jnp.ones((D,), jnp.float32), 'betav': jnp.zeros((D,), jnp.float32), 'go': jnp.ones((D,), jnp.float32), 'betao': jnp.zeros((D,), jnp.float32), 'scale': jnp.asarray(np.sqrt(1.0 / D_HEAD), jnp.float32)}
        return inp
    _L1_attn_in = _L1_attn_setup()

    def _L1_ffn_setup():
        import jax, jax.numpy as jnp
        import numpy as np
        D_MODEL, HIDDEN, N_EXPERTS, TOP_K = (128, 512, 8, 2)
        key = jax.random.key(seed)
        ks = jax.random.split(key, 7)
        s_d = 1.0 / np.sqrt(D_MODEL)
        s_h = 1.0 / np.sqrt(HIDDEN)
        return {'x': jax.random.normal(ks[0], (4, 256, D_MODEL), dtype=jnp.float32), 'gate_w': jax.random.uniform(ks[1], (D_MODEL, N_EXPERTS), minval=-s_d, maxval=s_d), 'gate_b': jax.random.uniform(ks[2], (N_EXPERTS,), minval=-s_d, maxval=s_d), 'w1': jax.random.uniform(ks[3], (N_EXPERTS, D_MODEL, HIDDEN), minval=-s_d, maxval=s_d), 'b1': jax.random.uniform(ks[4], (N_EXPERTS, HIDDEN), minval=-s_d, maxval=s_d), 'w2': jax.random.uniform(ks[5], (N_EXPERTS, HIDDEN, D_MODEL), minval=-s_h, maxval=s_h), 'b2': jax.random.uniform(ks[6], (N_EXPERTS, D_MODEL), minval=-s_h, maxval=s_h)}
    _L1_ffn_in = _L1_ffn_setup()
    _d = {'L0_attn_x': _L0_attn_in['x'], 'L0_attn_W_in': _L0_attn_in['W_in'], 'L0_attn_W_out': _L0_attn_in['W_out'], 'L0_attn_W_g1': _L0_attn_in['W_g1'], 'L0_attn_W_g2': _L0_attn_in['W_g2'], 'L0_attn_ln_w': _L0_attn_in['ln_w'], 'L0_ffn_w_gate': _L0_ffn_in['w_gate'], 'L0_ffn_w_g': _L0_ffn_in['w_g'], 'L0_ffn_w_u': _L0_ffn_in['w_u'], 'L0_ffn_w_d': _L0_ffn_in['w_d'], 'L1_attn_Wq': _L1_attn_in['Wq'], 'L1_attn_bq': _L1_attn_in['bq'], 'L1_attn_Wk': _L1_attn_in['Wk'], 'L1_attn_bk': _L1_attn_in['bk'], 'L1_attn_Wv': _L1_attn_in['Wv'], 'L1_attn_bv': _L1_attn_in['bv'], 'L1_attn_Wo': _L1_attn_in['Wo'], 'L1_attn_bo': _L1_attn_in['bo'], 'L1_attn_gq': _L1_attn_in['gq'], 'L1_attn_betaq': _L1_attn_in['betaq'], 'L1_attn_gk': _L1_attn_in['gk'], 'L1_attn_betak': _L1_attn_in['betak'], 'L1_attn_gv': _L1_attn_in['gv'], 'L1_attn_betav': _L1_attn_in['betav'], 'L1_attn_go': _L1_attn_in['go'], 'L1_attn_betao': _L1_attn_in['betao'], 'L1_attn_scale': _L1_attn_in['scale'], 'L1_ffn_gate_w': _L1_ffn_in['gate_w'], 'L1_ffn_gate_b': _L1_ffn_in['gate_b'], 'L1_ffn_w1': _L1_ffn_in['w1'], 'L1_ffn_b1': _L1_ffn_in['b1'], 'L1_ffn_w2': _L1_ffn_in['w2'], 'L1_ffn_b2': _L1_ffn_in['b2']}
    _x0 = _d['L0_attn_x']
    _d['L0_attn_x'] = jax.random.normal(jax.random.fold_in(jax.random.key(seed), 1), (4, 512, 128), dtype=_x0.dtype)
    del _x0
    return _d

def reference(L0_attn_x, L0_attn_W_in, L0_attn_W_out, L0_attn_W_g1, L0_attn_W_g2, L0_attn_ln_w, L0_ffn_w_gate, L0_ffn_w_g, L0_ffn_w_u, L0_ffn_w_d, L1_attn_Wq, L1_attn_bq, L1_attn_Wk, L1_attn_bk, L1_attn_Wv, L1_attn_bv, L1_attn_Wo, L1_attn_bo, L1_attn_gq, L1_attn_betaq, L1_attn_gk, L1_attn_betak, L1_attn_gv, L1_attn_betav, L1_attn_go, L1_attn_betao, L1_attn_scale, L1_ffn_gate_w, L1_ffn_gate_b, L1_ffn_w1, L1_ffn_b1, L1_ffn_w2, L1_ffn_b2):

    def _L0_attn_ref(x, W_in, W_out, W_g1, W_g2, ln_w):
        import jax, jax.numpy as jnp
        import numpy as np
        B, N, E, D = (2, 512, 128, 128)
        H = E // D
        LN_EPS = 1e-05

        def _gla_scan(q, k, v, g):

            def step(S, inp):
                qt, kt, vt, gt = inp
                S = jnp.exp(gt)[..., None] * S + kt[..., None] * vt[..., None, :]
                ot = jnp.einsum('bhd,bhde->bhe', qt, S)
                return (S, ot)
            xs = tuple((jnp.moveaxis(a, 2, 0) for a in (q, k, v, g)))
            S0 = jnp.zeros(q.shape[:2] + (q.shape[-1], v.shape[-1]), q.dtype)
            _, o = jax.lax.scan(step, S0, xs)
            return jnp.moveaxis(o, 0, 2)
        b, n, e = x.shape
        u = x @ W_in.T
        v, q, lg = jnp.split(u, 3, axis=-1)
        q = jax.nn.silu(q)
        f = jax.nn.sigmoid(lg)
        k = 1.0 - f
        g = jax.nn.log_sigmoid(lg)

        def tohead(a):
            return a.reshape(b, n, H, D).transpose(0, 2, 1, 3)
        o = _gla_scan(tohead(q), tohead(k), tohead(v), tohead(g))
        o = o.transpose(0, 2, 1, 3).reshape(b, n, e)
        gate = jax.nn.sigmoid(x @ W_g1.T @ W_g2.T)
        o = o * gate
        mu = jnp.mean(o, axis=-1, keepdims=True)
        var = jnp.var(o, axis=-1, keepdims=True)
        o = (o - mu) * jax.lax.rsqrt(var + LN_EPS) * ln_w
        return o @ W_out.T

    def _L0_ffn_ref(x, w_gate, w_g, w_u, w_d):
        import jax, jax.numpy as jnp
        import numpy as np
        B, S, D, M, E, K = (2, 256, 128, 176, 8, 2)
        scores = x @ w_gate
        topk_scores, topk_idx = jax.lax.top_k(scores, K)
        topk_probs = jax.nn.softmax(topk_scores, axis=-1)
        gating = jnp.sum(jax.nn.one_hot(topk_idx, E, dtype=topk_probs.dtype) * topk_probs[..., None], axis=-2)
        hidden = jax.nn.silu(jnp.einsum('bsd,edm->ebsm', x, w_g)) * jnp.einsum('bsd,edm->ebsm', x, w_u)
        expert_out = jnp.einsum('ebsm,emd->ebsd', hidden, w_d)
        y = jnp.einsum('bse,ebsd->bsd', gating, expert_out)
        return y

    def _L1_attn_ref(query, Wq, bq, Wk, bk, Wv, bv, Wo, bo, gq, betaq, gk, betak, gv, betav, go, betao, scale):
        import jax, jax.numpy as jnp
        import numpy as np
        D_MODEL = 128
        N_HEADS = 16
        D_HEAD = D_MODEL // N_HEADS
        EPS = 1e-05

        @jax.custom_vjp
        def spike(x):
            return (x >= 0).astype(x.dtype)

        def _spike_fwd(x):
            return (spike(x), x)

        def _spike_bwd(x, g):
            return (g / (1.0 + (jnp.pi * x) ** 2),)
        spike.defvjp(_spike_fwd, _spike_bwd)

        def lif(x, v_th):
            return spike(x - v_th)

        def layer_norm(x, g, b):
            mu = jnp.mean(x, axis=-1, keepdims=True)
            var = jnp.mean((x - mu) ** 2, axis=-1, keepdims=True)
            return (x - mu) * jax.lax.rsqrt(var + EPS) * g + b

        def log_pe_bias(n_q, n_k):
            pos_q = jnp.arange(n_q)[:, None]
            pos_k = jnp.arange(n_k)[None, :]
            dist = jnp.abs(pos_q - pos_k).astype(jnp.float32)
            max_len = max(n_q, n_k)
            bias = jnp.ceil(jnp.log2((max_len - 1) / (dist + 1.0)))
            return jnp.maximum(bias, 0.0)
        B, N, D = query.shape
        H, Dh = (N_HEADS, D_HEAD)
        Q = lif(layer_norm(query @ Wq.T + bq, gq, betaq), 1.0)
        K = lif(layer_norm(query @ Wk.T + bk, gk, betak), 1.0)
        V = lif(layer_norm(query @ Wv.T + bv, gv, betav), 1.0)
        Q = Q.reshape(B, N, H, Dh).transpose(0, 2, 1, 3)
        K = K.reshape(B, N, H, Dh).transpose(0, 2, 1, 3)
        V = V.reshape(B, N, H, Dh).transpose(0, 2, 1, 3)
        qk = jnp.einsum('bhld,bhmd->bhlm', Q, K)
        q_sum = Q.sum(-1, keepdims=True)
        k_sum = K.sum(-1, keepdims=True)
        hamming = q_sum + jnp.swapaxes(k_sum, 2, 3) - 2.0 * qk
        attn = Dh - hamming + log_pe_bias(N, N)[None, None]
        out = jnp.einsum('bhlm,bhmd->bhld', attn * scale, V)
        out = lif(out, 0.5)
        out = out.transpose(0, 2, 1, 3).reshape(B, N, D)
        out = lif(layer_norm(out @ Wo.T + bo, go, betao), 1.0)
        return out

    def _L1_ffn_ref(x, gate_w, gate_b, w1, b1, w2, b2):
        import jax, jax.numpy as jnp
        import numpy as np
        D_MODEL, HIDDEN, N_EXPERTS, TOP_K = (128, 512, 8, 2)
        orig_shape = x.shape
        flat_x = x.reshape(-1, orig_shape[-1])
        T = flat_x.shape[0]
        gate_probs = jax.nn.softmax(flat_x @ gate_w + gate_b, axis=-1)
        topk_w, topk_idx = jax.lax.top_k(gate_probs, TOP_K)
        topk_w = topk_w / jnp.maximum(topk_w.sum(-1, keepdims=True), 1e-09)
        comb = jnp.zeros((T, N_EXPERTS), flat_x.dtype).at[jnp.arange(T)[:, None], topk_idx].add(topk_w)
        h = jax.nn.silu(jnp.einsum('td,edh->eth', flat_x, w1) + b1[:, None, :])
        y = jnp.einsum('eth,ehd->etd', h, w2) + b2[:, None, :]
        flat_out = jnp.einsum('etd,te->td', y, comb)
        return flat_out.reshape(orig_shape)
    x = L0_attn_x
    x = x + 0.5 * _L0_ffn_ref(_layernorm(x, axis=-1), L0_ffn_w_gate, L0_ffn_w_g, L0_ffn_w_u, L0_ffn_w_d)
    x = x + _L0_attn_ref(_layernorm(x, axis=-1), L0_attn_W_in, L0_attn_W_out, L0_attn_W_g1, L0_attn_W_g2, L0_attn_ln_w)
    x = x + 0.5 * _L0_ffn_ref(_layernorm(x, axis=-1), L0_ffn_w_gate, L0_ffn_w_g, L0_ffn_w_u, L0_ffn_w_d)
    x = x + 0.5 * _L1_ffn_ref(_layernorm(x, axis=-1), L1_ffn_gate_w, L1_ffn_gate_b, L1_ffn_w1, L1_ffn_b1, L1_ffn_w2, L1_ffn_b2)
    x = x + _L1_attn_ref(_layernorm(x, axis=-1), L1_attn_Wq, L1_attn_bq, L1_attn_Wk, L1_attn_bk, L1_attn_Wv, L1_attn_bv, L1_attn_Wo, L1_attn_bo, L1_attn_gq, L1_attn_betaq, L1_attn_gk, L1_attn_betak, L1_attn_gv, L1_attn_betav, L1_attn_go, L1_attn_betao, L1_attn_scale)
    x = x + 0.5 * _L1_ffn_ref(_layernorm(x, axis=-1), L1_ffn_gate_w, L1_ffn_gate_b, L1_ffn_w1, L1_ffn_b1, L1_ffn_w2, L1_ffn_b2)
    return x

_drawn_inputs = setup_inputs


def setup_inputs(seed=0):
    import zlib

    import numpy as np

    out = dict(_drawn_inputs(seed))
    spreads = {'L0_attn_ln_w': (1.0, 0.2),
     'L1_attn_bq': (0.0, 0.1),
     'L1_attn_bk': (0.0, 0.1),
     'L1_attn_bv': (0.0, 0.1),
     'L1_attn_bo': (0.0, 0.1),
     'L1_attn_gq': (1.0, 0.2),
     'L1_attn_betaq': (0.0, 0.1),
     'L1_attn_gk': (1.0, 0.2),
     'L1_attn_betak': (0.0, 0.1),
     'L1_attn_gv': (1.0, 0.2),
     'L1_attn_betav': (0.0, 0.1),
     'L1_attn_go': (1.0, 0.2),
     'L1_attn_betao': (0.0, 0.1)}
    factors = {'L0_attn_W_g1': 7.644,
     'L0_attn_W_g2': 7.704,
     'L0_ffn_w_gate': 8.0,
     'L0_ffn_w_g': 8.0,
     'L0_ffn_w_u': 8.0,
     'L0_ffn_w_d': 8.0,
     'L1_ffn_b1': 13.339,
     'L1_ffn_b2': 3.3,
     'L1_ffn_gate_b': 5.071}
    for name, (base, spread) in spreads.items():
        noise = np.random.default_rng([zlib.crc32(name.encode()), seed]).standard_normal(out[name].shape)
        drawn = base * np.exp(spread * noise) if base else spread * noise
        out[name] = jnp.asarray(drawn.astype(out[name].dtype))
    for name, factor in factors.items():
        out[name] = (out[name] * factor).astype(out[name].dtype)
    return out
```

```python
from contextlib import ExitStack

import numpy as np

import concourse.bass as bass
from concourse import mybir

F32 = mybir.dt.float32
F32R = mybir.dt.float32r
BF16 = mybir.dt.bfloat16
ALU = mybir.AluOpType
ACT = mybir.ActivationFunctionType
AX = mybir.AxisListType

P = 128
B, N = 4, 512
TT = N // P
E = 8
M0 = 176
H0 = E * M0 // P
M1 = 512
Q1 = M1 // P
H1 = E * Q1
HEADS = 16
DH = P // HEADS
EPS = 1e-5
LEVELS = [1, 2, 4, 8, 16, 32, 64]
CALLS = 2 * B

C_ID = 0
C_HEAD = C_ID + P
C_RANK = C_HEAD + P
NCONST = C_RANK + TT * E
R_BIAS, R_G, R_BETA = 0, 3 * P, 6 * P
R_BO, R_GO, R_BETAO = 9 * P, 10 * P, 11 * P
R_GB, R_SC = 12 * P, 12 * P + E
NROWS = R_SC + 1


def bf16_bits(v):
    return (v.astype(np.float32).view(np.uint32) >> 16).astype(np.uint16)


def shape_constants():
    const = np.zeros((P, NCONST), np.float32)
    const[:, C_ID:C_ID + P] = np.eye(P)
    at = np.arange(P)
    const[:, C_HEAD:C_HEAD + P] = 2.0 * (at[:, None] // DH == at[None, :] // DH)
    s, t = at[:, None], at[None, :]
    mask = np.stack([(s // (2 * h) == t // (2 * h)) & (s // h % 2 == 0) & (t // h % 2 == 1) for h in LEVELS], 1)
    const[:, C_RANK:C_RANK + TT * E] = np.tile(E - np.arange(E), TT)
    spread = np.zeros((3 * E, H0 * P + E * P), np.float32)
    spread[:, :H0 * P] = (np.arange(3 * E)[:, None] % E) == (np.arange(H0 * P)[None, :] // M0)
    spread[:, H0 * P:] = (np.arange(3 * E)[:, None] % E) == (np.arange(E * P)[None, :] // P)
    dist = np.abs(np.arange(2 * N - P)[None, :] - (N - P) - at[:, None]).astype(np.float32)
    near = np.maximum(np.ceil(np.log2(np.float32(N - 1) / (dist + np.float32(1)))), 0) + DH / 2
    return {"c_const": const, "c_mask": bf16_bits(mask), "c_spread": bf16_bits(spread), "c_near": bf16_bits(near),
            "c_ident": bf16_bits(np.eye(P))}


def macaron(nc, a, out):
    ctx = ExitStack()
    with ctx:
        def sb(name, shape, dt=F32):
            return ctx.enter_context(nc.sbuf_tensor(name, shape, dt))

        def sem(name):
            return ctx.enter_context(nc.semaphore(name))

        x = sb("x", [P, B, TT, P])
        w0_hi = sb("w0_hi", [P, 3 * H0, P], F32R)
        w0_lo = sb("w0_lo", [P, 3 * H0, P], F32R)
        w1_hi = sb("w1_hi", [P, 2 * H1, P], F32R)
        w1_lo = sb("w1_lo", [P, 2 * H1, P], F32R)
        wt_hi = sb("wt_hi", [P, 10, P], F32R)
        wt_lo = sb("wt_lo", [P, 10, P], F32R)
        mask = sb("mask", [P, len(LEVELS), P], BF16)
        ident_etc = sb("ident_etc", [P, NCONST])
        ident, head2 = ident_etc[:, C_ID:C_ID + P], ident_etc[:, C_HEAD:C_HEAD + P]
        rank = ident_etc[:, C_RANK:C_RANK + TT * E].rearrange("p (t e) -> p t e", e=E)
        spread_b = sb("spread_b", [3 * E, H0 * P + E * P], BF16)
        near_b = sb("near_b", [P, 2 * N - P], BF16)
        ident_b = sb("ident_b", [P, P], BF16)
        rows = sb("rows", [P, NROWS])
        cols = sb("cols", [P, H1 + E + 1])
        wgate = sb("wgate", [P, 2, E])
        wgate_hi = sb("wgate_hi", [P, 2, E], F32R)
        wgate_lo = sb("wgate_lo", [P, 2, E], F32R)
        small = sb("small", [P, 40])
        base_e = small[:, 0:32].rearrange("p (t e) -> p t e", e=E)
        neg_half = small[:, 32:36]
        neg_half12 = sb("neg_half12", [P, 12])
        fw = sb("fw", [P, 7, N])
        h_hi = sb("h_hi", [P, 4, N], F32R)
        h_lo = sb("h_lo", [P, 4, N], F32R)
        acc = sb("acc", [P, N])
        xT_hi = sb("xT_hi", [P, 2, N], F32R)
        xT_lo = sb("xT_lo", [P, 2, N], F32R)
        zT_hi = sb("zT_hi", [P, N], F32R)
        zT_lo = sb("zT_lo", [P, N], F32R)
        r_hi = sb("r_hi", [P, N], F32R)
        r_lo = sb("r_lo", [P, N], F32R)
        gT = sb("gT", [3 * E, 2, N], BF16)
        gw = sb("gw", [P, 11, N])
        xn = sb("xn", [P, TT, P])
        stats = sb("stats", [P, TT, 6])
        mom = sb("mom", [P, 7, TT])
        rstd = sb("rstd", [P, TT])
        rt = sb("rt", [P, 7, TT, E])
        m8 = sb("m8", [P, 6, TT])
        g3 = sb("g3", [P, TT, 3 * E])
        g3b = sb("g3b", [P, 2, TT, E], BF16)
        astats = sb("astats", [P, 3 * TT, 6])
        amom = sb("amom", [P, 7, 3 * TT])
        arstd = sb("arstd", [P, 3 * TT])

        bank = [ctx.enter_context(nc.psum_tensor(f"bank{n}", [P, N], F32)) for n in range(8)]
        side, att = bank[6], bank[7]

        stage = gw[:, :, :].rearrange("p a n -> p (a n)")
        raw0 = stage[:, 0:3 * H0 * P]
        rawt = stage[:, 3 * H0 * P:(3 * H0 + 10) * P].rearrange("p (k c) -> p k c", c=P)
        raw_cols = xn[0:H1 + E + 1, 0, :]
        PIECE, RING = 2 * N, 5
        PIECES = 2 * H1 * P // PIECE
        w1_hi_f = w1_hi[:, :, :].rearrange("p a n -> p (a n)")
        w1_lo_f = w1_lo[:, :, :].rearrange("p a n -> p (a n)")

        x_in = [sem(f"x_in{b}") for b in range(B)]
        const_in, w0_in, wt_in, rows_in, cols_in = map(sem, ["const_in", "w0_in", "wt_in", "rows_in", "cols_in"])
        w1_in = [sem(f"w1_in{n}") for n in range(RING)]
        stored = sem("stored")
        set_up, wt_ps, wt_hi_done, wt_done, cols_ps = map(sem, ["set_up", "wt_ps", "wt_hi_done", "wt_done", "cols_ps"])
        w0_hi_done, w0_done, w1_hi_done, w1_done, pool_set = map(
            sem, ["w0_hi_done", "w0_done", "w1_hi_done", "w1_done", "pool_set"])
        ln_stats, ln_rstd, ln_xn, xT_ps, xT_hi_done, xT_done = map(
            sem, ["ln_stats", "ln_rstd", "ln_xn", "xT_ps", "xT_hi_done", "xT_done"])
        logits_ps, rt_step, rt_shift, rt_exp, g3_done, gT_ps, gT_done = map(
            sem, ["logits_ps", "rt_step", "rt_shift", "rt_exp", "g3_done", "gT_ps", "gT_done"])
        f_gate, f_spread, f_up, f_silu, f_sg, f_h, f_hi, f_lo, f_down, f_y, f_yT, f_x = map(
            sem, ["f_gate", "f_spread", "f_up", "f_silu", "f_sg", "f_h", "f_hi", "f_lo", "f_down", "f_y", "f_yT", "f_x"])
        m_up, m_spread, m_silu, m_gs, m_hi, m_lo_v, m_lo_p, m_down, m_y, m_acc, m_yT, m_x = map(
            sem, ["m_up", "m_spread", "m_silu", "m_gs", "m_hi", "m_lo_v", "m_lo_p", "m_down", "m_y", "m_acc", "m_yT", "m_x"])
        a_ps, a_read, a_act, a_step, a_pool = map(sem, ["a_ps", "a_read", "a_act", "a_step", "a_pool"])

        gq, gF, gR, gk, gX0, gX1, gP, gT0, gT1, gv, gG = (gw[:, n, :] for n in range(11))
        gX, gTm = [gX0, gX1], [gT0, gT1]
        gS, gon = gk, gq
        flat = stage
        spre = flat[:, 0:3 * TT * P].rearrange("p (t c) -> p t c", c=3 * P)
        spk = flat[:, 3 * N:5 * N].bitcast(BF16)[:, 0:3 * TT * P].rearrange("p (t c) -> p t c", c=3 * P)
        so = flat[:, 5 * N:6 * N].rearrange("p (t c) -> p t c", c=P)

        block = ctx.enter_context(nc.Block())

        def mm(dst, lhsT, rhs, start=True, stop=True):
            return nc.tensor.matmul(dst, lhsT, rhs, start=start, stop=stop)

        def mm3(dst, l_hi, l_lo, r_hi_, r_lo_, start=True, stop=True):
            mm(dst, l_hi, r_hi_, start, False)
            mm(dst, l_lo, r_hi_, False, False)
            return mm(dst, l_hi, r_lo_, False, stop)

        def wide(ap, n):
            return ap.unsqueeze(2).to_broadcast([ap.shape[0], ap.shape[1], n])

        @block.sync
        def _(sp):
            for b in range(B):
                sp.dma_start(x[:, b, :, :], a["L0_attn_x"][b].rearrange("(t p) d -> p t d", p=P)).then_inc(x_in[b], 16)
                if b == 0:
                    for k, name in enumerate(["w_g", "w_u"]):
                        sp.dma_start(raw0[:, k * H0 * P:(k + 1) * H0 * P].rearrange("p (e m) -> p e m", e=E),
                                     a["L0_ffn_" + name].rearrange("e d m -> d e m")).then_inc(w0_in, 16)
                    sp.dma_start(raw0[:, 2 * H0 * P:].rearrange("p (t d) -> p t d", d=P),
                                 a["L0_ffn_w_d"].rearrange("e m d -> (e m) d").rearrange("(t p) d -> p t d", p=P)
                                 ).then_inc(w0_in, 16)
            for n in range(PIECES):
                if n < RING:
                    sp.wait_ge(w0_done, 3)
                    sp.wait_ge(wt_ps, 3)
                else:
                    sp.wait_ge(w1_done, n - RING + 1)
                    sp.wait_ge(w1_hi_done, n - RING + 1)
                dst = stage[:, (n % RING) * PIECE:(n % RING + 1) * PIECE]
                if n < PIECES // 2:
                    e = n * PIECE // M1
                    sp.dma_start(dst.rearrange("p (e h) -> p e h", h=M1),
                                 a["L1_ffn_w1"][e:e + PIECE // M1].rearrange("e d h -> d e h")).then_inc(w1_in[n % RING], 16)
                else:
                    t = (n - PIECES // 2) * PIECE
                    sp.dma_start(dst.rearrange("p (t d) -> p t d", d=P),
                                 a["L1_ffn_w2"].rearrange("e h d -> (e h) d")[t:t + PIECE].rearrange("(t p) d -> p t d", p=P)
                                 ).then_inc(w1_in[n % RING], 16)
            for b in range(B):
                sp.wait_ge(m_x, B + b + 1)
                sp.dma_start(out[b].rearrange("(t p) d -> p t d", p=P), x[:, b, :, :]).then_inc(stored, 16)
            sp.wait_ge(stored, 16 * B)

        def cut(t):
            return slice(t * P, (t + 1) * P)

        def need(eng, s, value):
            if not isinstance(value, int) or value > 0:
                eng.wait_ge(s, value)

        GLA, GLA_V, GLA_A, GLA_P = 18, 50, 2, 8
        SPK, SPK_V, SPK_P = TT + 4, 53, 2
        MOM = 7

        def first(i):
            return isinstance(i, int) and i == 0

        def last_run(i):
            return isinstance(i, int) and i == CALLS - 1

        def back(t, ring):
            if t >= ring:
                return ring
            return H0 + t - max(u for u in range(H0) if u % ring == t)

        def gla_tensor(pe, g, k):
            pe.wait_ge(a_read, g * GLA + k + 1)
            if k == 0:
                pe.wait_ge(xT_done, 2 * g + 4)
                last = mm3(att[:, :], wt_hi[:, 1, :], wt_lo[:, 1, :], zT_hi[:, :], zT_lo[:, :])
            elif k == 1:
                last = mm3(att[:, :], wt_hi[:, 2, :], wt_lo[:, 2, :], zT_hi[:, :], zT_lo[:, :])
            elif k == 2:
                last = mm3(att[:, :], wt_hi[:, 3, :], wt_lo[:, 3, :], zT_hi[:, :], zT_lo[:, :])
            elif k == 3:
                for t in range(TT):
                    last = mm3(att[:, cut(t)], zT_hi[:, cut(t)], zT_lo[:, cut(t)], wt_hi[:, 0, :], wt_lo[:, 0, :])
            elif k == 4:
                for t in range(TT):
                    last = mm3(att[:, cut(t)], r_hi[:, cut(t)], r_lo[:, cut(t)], wt_hi[:, 4, :], wt_lo[:, 4, :])
            elif k < 12:
                pe.wait_ge(a_step, 1 + g * GLA_V + 3 + 4 * (k - 5) + 2)
                xl = gX[(k - 5) % 2]
                for t in range(TT):
                    last = mm(att[:, cut(t)], xl[:, cut(t)], xl[:, cut(t)])
            elif k == 12:
                for t in range(TT):
                    last = mm(att[:, cut(t)], gk[:, cut(t)], gq[:, cut(t)])
            elif k == 13:
                pe.wait_ge(a_step, 1 + g * GLA_V + 32)
                for t in range(TT):
                    last = nc.tensor.transpose(att[:, cut(t)], gX1[:, cut(t)], ident[:, :])
            elif k == 14:
                for t in range(TT - 1):
                    last = mm(att[:, cut(t)], gT0[:, cut(t)], gv[:, cut(t)])
            elif k == 15:
                pe.wait_ge(a_step, 1 + g * GLA_V + 35)
                pe.wait_ge(a_pool, 1 + g * GLA_P + 7)
                for t in range(TT):
                    last = mm(att[:, cut(t)], gP[:, cut(t)], gv[:, cut(t)], True, t == 0)
                    if t:
                        last = mm(att[:, cut(t)], gX0[:, cut(t)], gS[:, cut(t - 1)], False, True)
            elif k == 16:
                pe.wait_ge(a_step, 1 + g * GLA_V + 50)
                for t in range(TT):
                    last = nc.tensor.transpose(att[:, cut(t)], gon[:, cut(t)], ident[:, :])
            else:
                for t in range(TT):
                    last = mm3(att[:, cut(t)], zT_hi[:, cut(t)], zT_lo[:, cut(t)], wt_hi[:, 5, :], wt_lo[:, 5, :])
            last.then_inc(a_ps, 1)

        def spike_tensor(pe, s, k):
            pe.wait_ge(a_read, B * GLA + s * SPK + k + 1)
            v0 = 1 + B * GLA_V + s * SPK_V
            if k < TT:
                if k == 0:
                    pe.wait_ge(xT_done, 2 * s + 16)
                w = wt_hi[:, 6:9, :].rearrange("p a n -> p (a n)"), wt_lo[:, 6:9, :].rearrange("p a n -> p (a n)")
                last = mm3(att[:, 0:3 * P], zT_hi[:, cut(k)], zT_lo[:, cut(k)], *w)
            elif k == TT:
                pe.wait_ge(a_step, v0 + 35)
                for t in range(TT):
                    last = mm(att[:, 0:P], spk[:, t, P:2 * P], spk[:, t, 2 * P:3 * P], t == 0, t == TT - 1)
            elif k == TT + 1:
                for t in range(TT):
                    last = mm(att[:, cut(t)], spk[:, t, 0:P], ident_b[:, :])
            elif k == TT + 2:
                last = mm(att[:, :], r_lo[:, 0:P], r_hi[:, :], True, False)
                for t in range(TT):
                    u = N - P - t * P
                    last = mm(att[:, :], spk[:, t, 2 * P:3 * P], near_b[:, u:u + N], False, t == TT - 1)
            else:
                for t in range(TT):
                    mm(att[:, cut(t)], zT_hi[:, cut(t)], wt_hi[:, 9, :], True, False)
                    last = mm(att[:, cut(t)], zT_hi[:, cut(t)], wt_lo[:, 9, :], False, True)
            last.then_inc(a_ps, 1)

        def gla_scalar(act, g, k):
            if k in (0, 1, 2, 3, 4, 13, 16):
                act.wait_ge(a_ps, 1 + g * GLA + k + 1)
            if k == 0:
                nc.scalar.activation(gq, att[:, :], ACT.Silu).then_inc(a_read, 1)
            elif k == 1:
                nc.scalar.activation(gF, att[:, :], ACT.Tanh, scale=0.5).then_inc(a_read, 1)
            elif k == 2:
                nc.scalar.activation(r_hi[:, :], att[:, :], ACT.Copy).then_inc(a_act, 1)
            elif k == 3:
                nc.scalar.activation(gv, att[:, :], ACT.Copy).then_inc(a_read, 1)
            elif k == 4:
                nc.scalar.activation(gG, att[:, :], ACT.Tanh, scale=0.5).then_inc(a_read, 1)
            elif k == 13:
                act.wait_ge(a_pool, 1 + g * GLA_P + 6)
                nc.scalar.activation(gT0, att[:, :], ACT.Copy).then_inc(a_read, 1)
            elif k == 16:
                nc.scalar.activation(zT_hi[:, :], att[:, :], ACT.Copy, scale=cols[:, H1 + E:H1 + E + 1]).then_inc(a_act, 1)

        def spike_scalar(act, s, k):
            if k == TT + 1:
                act.wait_ge(a_ps, 1 + B * GLA + s * SPK + k + 1)
                nc.scalar.activation(r_hi[:, :], att[:, :], ACT.Copy).then_inc(a_read, 1)

        def gla_gpsimd(pool, g, k):
            v0, p0 = 1 + g * GLA_V, 1 + g * GLA_P
            if 5 < k <= 12:
                pool.wait_ge(a_read, g * GLA + k + 2)
                need(pool, a_pool, p0 + k - 6)
                nc.gpsimd.tensor_tensor(gP, gP, gTm[(k - 5) % 2], ALU.add).then_inc(a_pool, 1)
            elif k == 15:
                pool.wait_ge(a_step, v0 + 46)
                nc.gpsimd.tensor_tensor(arstd[:, 0:TT], amom[:, 6, 0:TT], neg_half12[:, 0:TT], ALU.pow).then_inc(a_pool, 1)

        def spike_gpsimd(pool, s, k):
            for at, w, v in ((TT - 1, 3 * TT, 19), (TT + 3, TT, 46)):
                if k == at:
                    pool.wait_ge(a_step, 1 + B * GLA_V + s * SPK_V + v)
                    nc.gpsimd.tensor_tensor(arstd[:, 0:w], amom[:, 6, 0:w], neg_half12[:, 0:w], ALU.pow).then_inc(a_pool, 1)

        def moments(dve, s, base, st, mom, w, eps):
            me, mo, qe, qo = st[:, 0:w, 1], st[:, 0:w, 4], st[:, 0:w, 2], st[:, 0:w, 5]
            total, diff, sq, mean, diff2, v, out_ = (mom[:, q, 0:w] for q in range(MOM))
            V = nc.vector
            dve.wait_ge(s, base + w)
            V.tensor_tensor(total, me, mo, ALU.add).then_inc(s, 1)
            V.tensor_tensor(diff, me, mo, ALU.subtract).then_inc(s, 1)
            V.tensor_tensor(sq, qe, qo, ALU.add).then_inc(s, 1)
            dve.wait_ge(s, base + w + 3)
            V.tensor_scalar(mean, total, 0.5, None, ALU.mult).then_inc(s, 1)
            V.tensor_tensor(diff2, diff, diff, ALU.mult).then_inc(s, 1)
            dve.wait_ge(s, base + w + 5)
            V.scalar_tensor_tensor(out=v, in0=diff2, scalar=P / 4.0, in1=sq, op0=ALU.mult, op1=ALU.add).then_inc(s, 1)
            dve.wait_ge(s, base + w + 6)
            V.tensor_scalar(out_, v, 1.0 / P, eps, ALU.mult, ALU.add).then_inc(s, 1)

        def halves(ap, h):
            v = ap.rearrange("p (s two h) -> p s two h", two=2, h=h)
            return v[:, :, 0, :], v[:, :, 1, :]

        def last_of(ap, h):
            return ap[:, :, h - 1:h].to_broadcast([P, N // (2 * h), h])

        def gla_level(dve, g, lv):
            v0, h = 1 + g * GLA_V + 3 + 4 * lv, LEVELS[lv]
            dve.wait_ge(a_step, v0)
            if lv < 2:
                need(dve, a_ps, 1 + g * GLA)
            else:
                dve.wait_ge(a_ps, 1 + g * GLA + 5 + lv - 1)
            (xe, xo), (ke, _), (_, qo) = halves(gX[lv % 2], h), halves(gk, h), halves(gq, h)
            (re, _), (fe, fo) = halves(gR, h), halves(gF, h)
            nc.vector.tensor_tensor(xe, ke, re, ALU.mult).then_inc(a_step, 1)
            nc.vector.tensor_tensor(xo, qo, fo, ALU.mult).then_inc(a_step, 1)
            dve.wait_ge(a_step, v0 + 1)
            nc.vector.tensor_tensor(re, re, last_of(fo, h), ALU.mult).then_inc(a_step, 1)
            dve.wait_ge(a_step, v0 + 3)
            nc.vector.tensor_tensor(fo, fo, last_of(fe, h), ALU.mult).then_inc(a_step, 1)

        def gla_vector(dve, g, k, bx):
            v0, p0, r0 = 1 + g * GLA_V, 1 + g * GLA_P, g * GLA + 1
            if k == 2:
                dve.wait_ge(a_read, r0 + 2)
                need(dve, a_step, v0)
                nc.vector.tensor_scalar(gk, gF, -0.5, 0.5, ALU.mult, ALU.add).then_inc(a_step, 1)
                dve.wait_ge(a_step, v0 + 1)
                nc.vector.tensor_scalar(gF, gF, 0.5, 0.5, ALU.mult, ALU.add).then_inc(a_step, 1)
                dve.wait_ge(a_step, v0 + 2)
                nc.vector.tensor_scalar(gR, gF, 0.0, 1.0, ALU.mult, ALU.add).then_inc(a_step, 1)
                dve.wait_ge(a_act, g * GLA_A + 1)
                nc.vector.tensor_tensor(r_lo[:, :], att[:, :], r_hi[:, :].bitcast(F32), ALU.subtract).then_inc(a_read, 1)
            elif k == 3:
                gla_level(dve, g, 0)
            elif k == 4:
                gla_level(dve, g, 1)
            elif 5 <= k <= 12:
                dve.wait_ge(a_ps, 1 + g * GLA + k + 1)
                src = att[:, :].rearrange("p (t c) -> p t c", c=P)
                m = (mask[:, k - 5, :] if k < 12 else ident[:, :]).unsqueeze(1).to_broadcast([P, TT, P])
                if k > 7:
                    dve.wait_ge(a_pool, p0 + k - 7)
                if k == 5:
                    need(dve, a_pool, p0)
                dst = gP if k == 5 else gTm[(k - 5) % 2]
                nc.vector.tensor_tensor(dst.rearrange("p (t c) -> p t c", c=P), src, m, ALU.mult).then_inc(a_read, 1)
                if k < 10:
                    gla_level(dve, g, k - 3)
                if k == 11:
                    dve.wait_ge(a_step, v0 + 31)
                    nc.vector.tensor_tensor(gX1, gk, gR, ALU.mult).then_inc(a_step, 1)
                    nc.vector.tensor_tensor(gX0, gq, gF, ALU.mult).then_inc(a_step, 1)
            elif k == 14:
                dve.wait_ge(a_ps, 1 + g * GLA + k + 1)
                dve.wait_ge(a_step, v0 + 33)
                nc.vector.tensor_copy(gS[:, cut(0)], att[:, cut(0)]).then_inc(a_step, 1)
                for t in range(1, TT - 1):
                    dve.wait_ge(a_step, v0 + 33 + t)
                    nc.vector.scalar_tensor_tensor(
                        out=gS[:, cut(t)], in0=gS[:, cut(t - 1)], scalar=gF[:, (t + 1) * P - 1:(t + 1) * P],
                        in1=att[:, cut(t)], op0=ALU.mult, op1=ALU.add).then_inc(a_step if t < TT - 2 else a_read, 1)
            elif k == 15:
                dve.wait_ge(a_ps, 1 + g * GLA + k + 1)
                dve.wait_ge(a_pool, p0 + 7)
                nc.vector.scalar_tensor_tensor(out=gT1, in0=gG, scalar=1.0, in1=att[:, :],
                                               op0=ALU.add, op1=ALU.mult).then_inc(a_read, 1)
                dve.wait_ge(a_read, r0 + k + 1)
                dve.wait_ge(a_step, v0 + 35)
                for t in range(TT):
                    nc.vector.bn_stats(astats[:, t, :], gT1[:, cut(t)]).then_inc(a_step, 1)
                moments(dve, a_step, v0 + 35, astats, amom, TT, 4 * EPS)
            elif k == 16:
                dve.wait_ge(a_pool, p0 + 8)
                for t in range(TT):
                    nc.vector.tensor_scalar(gon[:, cut(t)], gT1[:, cut(t)], amom[:, 3, t:t + 1], arstd[:, t:t + 1],
                                            ALU.subtract, ALU.mult).then_inc(a_step, 1)
                dve.wait_ge(a_act, g * GLA_A + 2)
                nc.vector.scalar_tensor_tensor(
                    out=zT_lo[:, :], in0=att[:, :], scalar=cols[:, H1 + E:H1 + E + 1], in1=zT_hi[:, :].bitcast(F32),
                    op0=ALU.mult, op1=ALU.subtract).then_inc(a_read, 1)
            elif k == 17:
                dve.wait_ge(a_ps, 1 + g * GLA + k + 1)
                xb = x[:, bx, :, :].rearrange("p t d -> p (t d)")
                nc.vector.tensor_tensor(xb, att[:, :], xb, ALU.add).then_inc(a_read, 1)

        def spike_vector(dve, s, k, bx):
            v0, p0 = 1 + B * GLA_V + s * SPK_V, 1 + B * GLA_P + s * SPK_P
            r0 = B * GLA + s * SPK + 1
            if k < TT:
                if k == 0:
                    dve.wait_ge(a_step, v0)
                dve.wait_ge(a_ps, r0 + k + 1)
                nc.vector.tensor_tensor(spre[:, k, :], att[:, 0:3 * P], rows[:, R_BIAS:R_BIAS + 3 * P],
                                        ALU.add).then_inc(a_read, 1)
                if k == TT - 1:
                    dve.wait_ge(a_read, r0 + TT)
                    dve.wait_ge(a_step, v0)
                    for t in range(TT):
                        for c in range(3):
                            nc.vector.bn_stats(astats[:, 3 * t + c, :], spre[:, t, cut(c)]).then_inc(a_step, 1)
                    moments(dve, a_step, v0, astats, amom, 3 * TT, EPS)
            elif k == TT:
                dve.wait_ge(a_pool, p0 + 1)
                for t in range(TT):
                    for c in range(3):
                        n = 3 * t + c
                        nc.vector.tensor_scalar(spre[:, t, cut(c)], spre[:, t, cut(c)], amom[:, 3, n:n + 1],
                                                arstd[:, n:n + 1], ALU.subtract, ALU.mult).then_inc(a_step, 1)
                dve.wait_ge(a_step, v0 + 31)
                for n, (at, op) in enumerate(((R_G, ALU.mult), (R_BETA, ALU.add))):
                    row = rows[:, at:at + 3 * P].unsqueeze(1).to_broadcast([P, TT, 3 * P])
                    nc.vector.tensor_tensor(spre, spre, row, op).then_inc(a_step, 1)
                    dve.wait_ge(a_step, v0 + 32 + n)
                nc.vector.tensor_scalar(spk[:, :, 0:2 * P], spre[:, :, 0:2 * P], 1.0, 0.5,
                                        ALU.is_ge, ALU.subtract).then_inc(a_step, 1)
                nc.vector.tensor_scalar(spk[:, :, 2 * P:3 * P], spre[:, :, 2 * P:3 * P], 1.0, None,
                                        ALU.is_ge).then_inc(a_step, 1)
                dve.wait_ge(a_ps, r0 + k + 1)
                nc.vector.tensor_tensor(r_lo[:, 0:P], att[:, 0:P], head2[:, :], ALU.mult).then_inc(a_read, 1)
            elif k == TT + 2:
                dve.wait_ge(a_ps, r0 + k + 1)
                nc.vector.tensor_scalar(zT_hi[:, :], att[:, :], rows[:, R_SC:R_SC + 1], 0.5,
                                        ALU.mult, ALU.is_ge).then_inc(a_read, 1)
            elif k == TT + 3:
                dve.wait_ge(a_ps, r0 + k + 1)
                row = rows[:, R_BO:R_BO + P].unsqueeze(1).to_broadcast([P, TT, P])
                nc.vector.tensor_tensor(so, att[:, :].rearrange("p (t c) -> p t c", c=P), row,
                                        ALU.add).then_inc(a_read, 1)
                dve.wait_ge(a_read, r0 + k + 1)
                dve.wait_ge(a_step, v0 + 35)
                for t in range(TT):
                    nc.vector.bn_stats(astats[:, t, :], so[:, t, :]).then_inc(a_step, 1)
                moments(dve, a_step, v0 + 35, astats, amom, TT, EPS)
            elif k == TT + 4:
                dve.wait_ge(a_pool, p0 + 2)
                for t in range(TT):
                    nc.vector.tensor_scalar(so[:, t, :], so[:, t, :], amom[:, 3, t:t + 1], arstd[:, t:t + 1],
                                            ALU.subtract, ALU.mult).then_inc(a_step, 1)
                dve.wait_ge(a_step, v0 + 50)
                for n, (at, op) in enumerate(((R_GO, ALU.mult), (R_BETAO, ALU.add))):
                    row = rows[:, at:at + P].unsqueeze(1).to_broadcast([P, TT, P])
                    nc.vector.tensor_tensor(so, so, row, op).then_inc(a_step, 1)
                    dve.wait_ge(a_step, v0 + 51 + n)
                nc.vector.scalar_tensor_tensor(out=x[:, bx, :, :], in0=so, scalar=1.0, in1=x[:, bx, :, :],
                                               op0=ALU.is_ge, op1=ALU.add).then_inc(a_step, 1)

        def norm_vector(dve, n, b, part, par=None):
            if part == "stats":
                need(dve, ln_stats, (TT + MOM) * n)
                need(dve, ln_xn, TT * n)
                for t in range(TT):
                    nc.vector.bn_stats(stats[:, t, :], x[:, b, t, :]).then_inc(ln_stats, 1)
                moments(dve, ln_stats, (TT + MOM) * n, stats, mom, TT, EPS)
            elif part == "norm":
                dve.wait_ge(ln_rstd, n + 1)
                need(dve, xT_ps, n)
                for t in range(TT):
                    nc.vector.tensor_scalar(xn[:, t, :], x[:, b, t, :], mom[:, 3, t:t + 1], rstd[:, t:t + 1],
                                            ALU.subtract, ALU.mult).then_inc(ln_xn, 1)
            else:
                dve.wait_ge(xT_hi_done, n + 1)
                hi, lo = (zT_hi[:, :], zT_lo[:, :]) if par is None else (xT_hi[:, par, :], xT_lo[:, par, :])
                nc.vector.tensor_tensor(lo, side[:, :], hi.bitcast(F32), ALU.subtract).then_inc(xT_done, 1)

        def norm_gpsimd(pool, n):
            pool.wait_ge(ln_stats, (TT + MOM) * (n + 1))
            nc.gpsimd.tensor_tensor(rstd[:, :], mom[:, 6, :], neg_half, ALU.pow).then_inc(ln_rstd, 1)

        def norm_tensor(pe, n, r):
            pe.wait_ge(ln_xn, TT * n + TT)
            need(pe, xT_done, n)
            need(pe, gT_done, r)
            for t in range(TT):
                last = nc.tensor.transpose(side[:, cut(t)], xn[:, t, :], ident[:, :])
            last.then_inc(xT_ps, 1)

        def norm_scalar(act, n, par=None):
            act.wait_ge(xT_ps, n + 1)
            hi = zT_hi[:, :] if par is None else xT_hi[:, par, :]
            nc.scalar.activation(hi, side[:, :], ACT.Copy).then_inc(xT_hi_done, 1)

        RT = (24, 28)

        def rt_base(r, m):
            return r * RT[0] if m == 0 else CALLS * RT[0] + (r - CALLS) * RT[1]

        def router_tensor(pe, n, r, m, par, part):
            if part == "logits":
                pe.wait_ge(xT_done, n + 1)
                for t in range(TT):
                    last = mm3(side[:, t * E:(t + 1) * E], xT_hi[:, par, cut(t)], xT_lo[:, par, cut(t)],
                               wgate_hi[:, m, :], wgate_lo[:, m, :])
                last.then_inc(logits_ps, 1)
            else:
                pe.wait_ge(rt_step, rt_base(r, m) + RT[m])
                for t in range(TT):
                    last = nc.tensor.transpose(side[0:3 * E, cut(t)], g3[:, t, :], ident[:, :])
                last.then_inc(gT_ps, 1)

        def router_scalar(act, r, par):
            act.wait_ge(gT_ps, r + 1)
            nc.scalar.activation(gT[:, par, :], side[0:3 * E, :], ACT.Copy).then_inc(gT_done, 1)

        def router_gpsimd(pool, r, m):
            pool.wait_ge(rt_step, rt_base(r, m) + 3)
            nc.gpsimd.tensor_tensor(rt[:, 1, :, :], base_e, rt[:, 1, :, :], ALU.pow).then_inc(rt_exp, 1)

        def router_vector(dve, r, m, part):
            logit, ex, eq, pick, rest, pick2, gate = (rt[:, q, :, :] for q in range(7))
            best, key, second, total, inv = (m8[:, q, :] for q in range(5))
            V, base = nc.vector, rt_base(r, m)
            done = [0 if part == "pick" else 14]

            def link(instruction):
                done[0] += 1
                instruction.then_inc(rt_step, 1)
                if done[0] < RT[m]:
                    dve.wait_ge(rt_step, base + done[0])

            def first_of(values, value, one_hot):
                link(V.tensor_tensor(eq, values, wide(value, E), ALU.is_equal))
                link(V.tensor_tensor(eq, eq, rank[:, :, :], ALU.mult))
                link(V.reduce_max(key, eq, axis=AX.X))
                link(V.tensor_tensor(one_hot, eq, wide(key, E), ALU.is_equal))

            if part == "pick":
                dve.wait_ge(logits_ps, r + 1)
                sums = side[:, 0:TT * E].rearrange("p (t e) -> p t e", e=E)
                if m == 0:
                    link(V.tensor_copy(logit, sums))
                else:
                    link(V.tensor_tensor(logit, sums, rows[:, R_GB:R_GB + E].unsqueeze(1).to_broadcast([P, TT, E]), ALU.add))
                link(V.reduce_max(best, logit, axis=AX.X))
                link(V.tensor_tensor(ex, logit, wide(best, E), ALU.subtract))
                first_of(logit, best, pick)
                link(V.scalar_tensor_tensor(out=rest, in0=pick, scalar=-3e38, in1=logit, op0=ALU.mult, op1=ALU.add))
                link(V.reduce_max(second, rest, axis=AX.X))
                first_of(rest, second, pick2)
                link(V.tensor_tensor(pick, pick, pick2, ALU.add))
            else:
                dve.wait_ge(rt_exp, r + 1)
                if m == 1:
                    link(V.reduce_sum(total, ex, axis=AX.X))
                    link(V.reciprocal(inv, total))
                    link(V.tensor_tensor(ex, ex, wide(inv, E), ALU.mult))
                link(V.tensor_tensor(gate, ex, pick, ALU.mult))
                link(V.reduce_sum(total, gate, axis=AX.X))
                if m == 1:
                    link(V.tensor_scalar(total, total, 1e-9, None, ALU.max))
                link(V.reciprocal(inv, total))
                link(V.tensor_tensor(gate, gate, wide(inv, E), ALU.mult))
                link(V.tensor_copy(g3b[:, 0, :, :], gate))
                link(V.tensor_copy(g3[:, :, 0:E], g3b[:, 0, :, :]))
                link(V.tensor_tensor(gate, gate, g3[:, :, 0:E], ALU.subtract))
                link(V.tensor_copy(g3b[:, 1, :, :], gate))
                link(V.tensor_copy(g3[:, :, E:2 * E], g3b[:, 1, :, :]))
                link(V.tensor_tensor(g3[:, :, 2 * E:3 * E], gate, g3[:, :, E:2 * E], ALU.subtract))

        GLA_AT = {4: 0, 5: 1, 6: 2, 7: 3, 8: 4, 9: 5, 11: 6, 13: 7, 15: 8, 17: 9, 19: 10, 21: 11, 22: 12,
                  23: 13, 24: 14, 26: 15, 29: 16, 31: 17}
        SPK_AT = {6: 0, 8: 1, 10: 2, 12: 3, 15: 4, 18: 5, 20: 6, 22: 7, 25: 8}
        Z_AT = {0: "stats", 2: "norm", 3: "split"}
        NORM_AT = ({1: "stats", 4: "norm", 6: "split"}, {28: "stats", 31: "norm", 33: "split"})
        W1_AT = {4 * k + 3: k for k in range(8)}
        LOGITS_AT, PICK_AT, GATE_AT = (10, 36), (10, 36), (16, 42)
        SPREAD_AT = (18, 44)

        def side_job(m, i, par, attention):
            r = i + 1 + m * CALLS
            if attention:
                n, zn = 2 * i + 12 * m, 2 * i + 12 * m - 1
            else:
                n, zn = i + (1 if i < 2 else 5) + 12 * m, None
            return n, zn, r, (i + 1) % B, par

        def router_mixture(m, i):
            return 1 if m == 1 or last_run(i) else 0

        def side_tensor(pe, m, i, slot, par_now, attention):
            n, zn, r, b, par = side_job(m, i, 1 - par_now, attention)
            if attention:
                if slot == 2:
                    norm_tensor(pe, zn, r)
                if m == 0 and slot in GLA_AT:
                    gla_tensor(pe, i - 2, GLA_AT[slot])
                if m == 1 and slot in SPK_AT and SPK_AT[slot] < SPK:
                    spike_tensor(pe, i - 2, SPK_AT[slot])
            if m == 0 or not last_run(i):
                if NORM_AT[m].get(slot) == "split":
                    norm_tensor(pe, n, r)
                if slot == LOGITS_AT[m]:
                    router_tensor(pe, n, r, router_mixture(m, i), par, "logits")
                if slot == SPREAD_AT[m]:
                    router_tensor(pe, n, r, router_mixture(m, i), par, "gates")

        def side_scalar(act, m, i, slot, par_now, attention):
            n, zn, r, b, par = side_job(m, i, 1 - par_now, attention)
            if attention:
                if slot == 2:
                    norm_scalar(act, zn)
                if m == 0 and slot in GLA_AT:
                    gla_scalar(act, i - 2, GLA_AT[slot])
                if m == 1 and slot in SPK_AT:
                    spike_scalar(act, i - 2, SPK_AT[slot])
            if m == 0 and first(i) and slot in W1_AT:
                k = W1_AT[slot]
                piece = slice(k * PIECE, (k + 1) * PIECE)
                act.wait_ge(w1_in[k % RING], 16 * (k // RING + 1))
                nc.scalar.activation(w1_hi_f[:, piece], stage[:, (k % RING) * PIECE:(k % RING + 1) * PIECE],
                                     ACT.Copy).then_inc(w1_hi_done, 1)
            if m == 0 or not last_run(i):
                if NORM_AT[m].get(slot) == "split":
                    norm_scalar(act, n, par)
                if slot == SPREAD_AT[m]:
                    router_scalar(act, r, par)

        def side_vector(dve, m, i, slot, par_now, attention):
            n, zn, r, b, par = side_job(m, i, 1 - par_now, attention)
            if attention:
                if slot == 0:
                    dve.wait_ge(m_x if m else f_x, i - 1)
                    norm_vector(dve, zn, i - 2, "stats")
                if slot == 1:
                    norm_vector(dve, zn, i - 2, "norm")
                if slot == 3:
                    norm_vector(dve, zn, i - 2, "split")
                if m == 0 and slot in GLA_AT:
                    gla_vector(dve, i - 2, GLA_AT[slot], i - 2)
                if m == 1 and slot in SPK_AT:
                    spike_vector(dve, i - 2, SPK_AT[slot], i - 2)
            if m == 0 and first(i) and slot in W1_AT:
                k = W1_AT[slot]
                piece = slice(k * PIECE, (k + 1) * PIECE)
                dve.wait_ge(w1_hi_done, k + 1)
                nc.vector.tensor_tensor(w1_lo_f[:, piece], stage[:, (k % RING) * PIECE:(k % RING + 1) * PIECE],
                                        w1_hi_f[:, piece].bitcast(F32), ALU.subtract).then_inc(w1_done, 1)
            if m == 0 or not last_run(i):
                job = NORM_AT[m].get(slot)
                if job == "stats":
                    if attention:
                        if m == 0:
                            dve.wait_ge(a_read, (i - 2) * GLA + 1)
                        else:
                            dve.wait_ge(a_step, 1 + B * GLA_V + (i - 2) * SPK_V)
                    elif isinstance(i, int) and i == CALLS - 2:
                        dve.wait_ge(a_read, B * GLA + 1) if m == 0 else dve.wait_ge(a_step, 1 + B * (GLA_V + SPK_V))
                    elif last_run(i):
                        dve.wait_ge(f_x, i - 1)
                    norm_vector(dve, n, b, "stats")
                elif job == "norm":
                    norm_vector(dve, n, b, "norm")
                elif job == "split":
                    norm_vector(dve, n, b, "split", par)
                if slot == PICK_AT[m]:
                    router_vector(dve, r, router_mixture(m, i), "pick")
                if slot == GATE_AT[m]:
                    router_vector(dve, r, router_mixture(m, i), "gate")

        def side_gpsimd(pool, m, i, slot, par_now, attention):
            n, zn, r, b, par = side_job(m, i, 1 - par_now, attention)
            if attention:
                if slot == 0:
                    norm_gpsimd(pool, zn)
                if m == 0 and slot in GLA_AT:
                    gla_gpsimd(pool, i - 2, GLA_AT[slot])
                if m == 1 and slot in SPK_AT:
                    spike_gpsimd(pool, i - 2, SPK_AT[slot])
            if m == 0 or not last_run(i):
                if NORM_AT[m].get(slot) == "stats":
                    norm_gpsimd(pool, n)
                if slot == PICK_AT[m]:
                    router_gpsimd(pool, r, router_mixture(m, i))

        G0, U0, S0, Y0 = (0, 1), (2, 3), 4, 5
        s_buf, sg_buf, h_buf = fw[:, 0:2, :], fw[:, 2, :], fw[:, 3:7, :]

        def mix0_down(pe, T, td, i):
            pe.wait_ge(f_hi, T + 1)
            pe.wait_ge(f_lo, T + 1)
            if td == 0:
                need(pe, f_yT, i)
            mm3(bank[Y0][:, :], w0_hi[:, 2 * H0 + td, :], w0_lo[:, 2 * H0 + td, :], h_hi[:, td % 4, :], h_lo[:, td % 4, :],
                td == 0, td == H0 - 1).then_inc(f_down, 1)

        def mix0_turn(pe, i):
            pe.wait_ge(f_yT, i)
            for t in range(TT):
                last = nc.tensor.transpose(bank[S0][:, cut(t)], acc[:, cut(t)], ident[:, :])
            last.then_inc(f_y, 1)

        def mix0_tensor(pe, i, par, t, attention):
            T = H0 * i + t
            xh, xl = xT_hi[:, par, :], xT_lo[:, par, :]
            if t == 0:
                pe.wait_ge(gT_done, i + 1)
            need(pe, f_silu, T - back(t, 2) + 1)
            mm3(bank[G0[t % 2]][:, :], w0_hi[:, t, :], w0_lo[:, t, :], xh, xl).then_inc(f_gate, 1)
            side_tensor(pe, 0, i, 3 * t, par, attention)
            need(pe, f_sg, T)
            if t == 4:
                need(pe, f_x, i)
            mm(bank[S0][:, :], spread_b[:, cut(t)], gT[:, par, :]).then_inc(f_spread, 1)
            need(pe, f_h, T - back(t, 2) + 1)
            mm3(bank[U0[t % 2]][:, :], w0_hi[:, H0 + t, :], w0_lo[:, H0 + t, :], xh, xl).then_inc(f_up, 1)
            side_tensor(pe, 0, i, 3 * t + 1, par, attention)
            if t == 3 and not first(i):
                pe.wait_ge(f_sg, T + 1)
                mix0_turn(pe, i)
            if t >= 3 or not first(i):
                mix0_down(pe, T - 3, (t - 3) % H0, i)
            side_tensor(pe, 0, i, 3 * t + 2, par, attention)

        def mix0_hi(act, T, th):
            act.wait_ge(f_h, T + 1)
            need(act, f_down, T - back(th, 4) + 1)
            nc.scalar.activation(h_hi[:, th % 4, :], h_buf[:, th % 4, :], ACT.Copy).then_inc(f_hi, 1)

        def mix0_out(act, i):
            act.wait_ge(f_down, H0 * (i + 1))
            need(act, f_y, i)
            nc.scalar.activation(acc[:, :], bank[Y0][:, :], ACT.Copy).then_inc(f_yT, 1)

        def mix0_scalar(act, i, par, t, attention):
            T = H0 * i + t
            act.wait_ge(f_gate, T + 1)
            need(act, f_sg, T - back(t, 2) + 1)
            nc.scalar.activation(s_buf[:, t % 2, :], bank[G0[t % 2]][:, :], ACT.Silu).then_inc(f_silu, 1)
            side_scalar(act, 0, i, 3 * t, par, attention)
            side_scalar(act, 0, i, 3 * t + 1, par, attention)
            if t > 0 or not first(i):
                mix0_hi(act, T - 1, (t - 1) % H0)
            if t == 2 and not first(i):
                mix0_out(act, i - 1)
            side_scalar(act, 0, i, 3 * t + 2, par, attention)

        def mix0_add_prev(dve, i):
            dve.wait_ge(f_y, i)
            xb = x[:, (i + B - 1) % B, :, :].rearrange("p t d -> p (t d)")
            nc.vector.scalar_tensor_tensor(out=xb, in0=bank[S0][:, :], scalar=0.5, in1=xb,
                                           op0=ALU.mult, op1=ALU.add).then_inc(f_x, 1)

        def mix0_vector(dve, i, par, t, attention):
            T = H0 * i + t
            side_vector(dve, 0, i, 3 * t, par, attention)
            dve.wait_ge(f_silu, T + 1)
            dve.wait_ge(f_spread, T + 1)
            need(dve, f_h, T)
            nc.vector.tensor_tensor(sg_buf, bank[S0][:, :], s_buf[:, t % 2, :], ALU.mult).then_inc(f_sg, 1)
            dve.wait_ge(f_sg, T + 1)
            dve.wait_ge(f_up, T + 1)
            need(dve, f_hi, T - back(t, 4) + 1)
            need(dve, f_lo, T - back(t, 4) + 1)
            nc.vector.tensor_tensor(h_buf[:, t % 4, :], bank[U0[t % 2]][:, :], sg_buf,
                                    ALU.mult).then_inc(f_h, 1)
            side_vector(dve, 0, i, 3 * t + 1, par, attention)
            if t == 3 and not first(i):
                mix0_add_prev(dve, i)
            side_vector(dve, 0, i, 3 * t + 2, par, attention)

        def mix0_lo(pool, T, th):
            pool.wait_ge(f_hi, T + 1)
            need(pool, f_down, T - back(th, 4) + 1)
            nc.gpsimd.tensor_tensor(h_lo[:, th % 4, :], h_buf[:, th % 4, :], h_hi[:, th % 4, :].bitcast(F32),
                                    ALU.subtract).then_inc(f_lo, 1)

        def mix0_gpsimd(pool, i, par, t, attention):
            T = H0 * i + t
            side_gpsimd(pool, 0, i, 3 * t, par, attention)
            side_gpsimd(pool, 0, i, 3 * t + 1, par, attention)
            if t > 0 or not first(i):
                mix0_lo(pool, T - 1, (t - 1) % H0)
            side_gpsimd(pool, 0, i, 3 * t + 2, par, attention)

        U1, Y1, S1, O1 = (0, 1), (2, 3), 4, 5
        hid, gs_buf, y_buf = fw[:, 0:4, :], fw[:, 4:6, :], fw[:, 6, :]

        def mix1_down(pe, j, t):
            td = (t - 3) % H1
            pe.wait_ge(m_hi, H1 * j + t - 2)
            pe.wait_ge(m_lo_v if td % 2 else m_lo_p, H1 // 2 * j + (t - 3) // 2 + 1)
            if td % Q1 == 0:
                need(pe, m_y, E * j + (t - 3) // Q1 - 1)
            mm3(bank[Y1[td // Q1 % 2]][:, :], w1_hi[:, H1 + td, :], w1_lo[:, H1 + td, :],
                h_hi[:, td % 4, :], h_lo[:, td % 4, :], td % Q1 == 0, td % Q1 == Q1 - 1).then_inc(m_down, 1)

        def mix1_turn(pe, j):
            pe.wait_ge(m_acc, (E - 1) * (j + 1))
            need(pe, m_x, j)
            for t in range(TT):
                last = nc.tensor.transpose(bank[O1][:, cut(t)], acc[:, cut(t)], ident[:, :])
            last.then_inc(m_yT, 1)

        def mix1_tensor(pe, j, par, t, attention):
            T = H1 * j + t
            if t == 0:
                pe.wait_ge(gT_done, j + CALLS + 1)
            need(pe, m_silu, T - 1)
            mm3(bank[U1[t % 2]][:, :], w1_hi[:, t, :], w1_lo[:, t, :], xT_hi[:, par, :], xT_lo[:, par, :]).then_inc(m_up, 1)
            if t % Q1 == 0:
                need(pe, m_gs, E * j + t // Q1)
                mm(bank[S1][:, :], spread_b[:, cut(H0 + t // Q1)], gT[:, par, :]).then_inc(m_spread, 1)
            side_tensor(pe, 1, j, 2 * t, par, attention)
            if t >= 3 or not first(j):
                mix1_down(pe, j, t)
            if t == 5 and not first(j):
                mix1_turn(pe, j - 1)
            side_tensor(pe, 1, j, 2 * t + 1, par, attention)

        def mix1_scalar(act, j, par, t, attention):
            T = H1 * j + t
            act.wait_ge(m_up, T + 1)
            need(act, m_hi, T - 3)
            need(act, m_lo_v if t % 2 else m_lo_p, H1 // 2 * j + t // 2 - 1)
            nc.scalar.activation(hid[:, t % 4, :], bank[U1[t % 2]][:, :], ACT.Silu, bias=cols[:, t:t + 1]).then_inc(m_silu, 1)
            side_scalar(act, 1, j, 2 * t, par, attention)
            if t % Q1 == 1:
                e = t // Q1
                act.wait_ge(m_spread, E * j + e + 1)
                need(act, m_y, E * j + e - 1)
                nc.scalar.activation(gs_buf[:, e % 2, :], bank[S1][:, :], ACT.Copy).then_inc(m_gs, 1)
            side_scalar(act, 1, j, 2 * t + 1, par, attention)

        def mix1_gate(dve, j, t):
            X, e = E * j + (t - 7) // Q1, (t - 7) // Q1 % E
            run = j if t >= 7 else j - 1
            dve.wait_ge(m_down, H1 * j + t - 3)
            dve.wait_ge(m_gs, X + 1)
            if e == 0:
                need(dve, m_yT, run)
                dst = acc[:, :]
            else:
                need(dve, m_acc, (E - 1) * run + e - 1)
                dst = y_buf
            nc.vector.scalar_tensor_tensor(out=dst, in0=bank[Y1[e % 2]][:, :], scalar=cols[:, H1 + e:H1 + e + 1],
                                           in1=gs_buf[:, e % 2, :], op0=ALU.add, op1=ALU.mult).then_inc(m_y, 1)

        def mix1_add(dve, j, b):
            dve.wait_ge(m_yT, j + 1)
            xb = x[:, b, :, :].rearrange("p t d -> p (t d)")
            nc.vector.scalar_tensor_tensor(out=xb, in0=bank[O1][:, :], scalar=0.5, in1=xb,
                                           op0=ALU.mult, op1=ALU.add).then_inc(m_x, 1)

        def mix1_vector(dve, j, par, t, attention):
            T = H1 * j + t
            dve.wait_ge(m_silu, T + 1)
            need(dve, m_down, T - 3)
            nc.vector.tensor_copy(h_hi[:, t % 4, :], hid[:, t % 4, :]).then_inc(m_hi, 1)
            if t % 2:
                dve.wait_ge(m_hi, T + 1)
                nc.vector.tensor_tensor(h_lo[:, t % 4, :], hid[:, t % 4, :], h_hi[:, t % 4, :].bitcast(F32),
                                        ALU.subtract).then_inc(m_lo_v, 1)
            side_vector(dve, 1, j, 2 * t, par, attention)
            if t % Q1 == 3 and (t > 3 or not first(j)):
                mix1_gate(dve, j, t)
            if t == 5 and not first(j):
                mix1_add(dve, j - 1, (j + B - 1) % B)
            side_vector(dve, 1, j, 2 * t + 1, par, attention)

        def mix1_sum(pool, j, t):
            X, e = E * j + (t - 7) // Q1, (t - 7) // Q1 % E
            run = j if t >= 7 else j - 1
            if e > 0:
                pool.wait_ge(m_y, X + 1)
                need(pool, m_acc, (E - 1) * run + e - 1)
                nc.gpsimd.tensor_tensor(acc[:, :], acc[:, :], y_buf, ALU.add).then_inc(m_acc, 1)

        def mix1_gpsimd(pool, j, par, t, attention):
            T = H1 * j + t
            if t % 2 == 0:
                pool.wait_ge(m_hi, T + 1)
                need(pool, m_down, T - 3)
                nc.gpsimd.tensor_tensor(h_lo[:, t % 4, :], hid[:, t % 4, :], h_hi[:, t % 4, :].bitcast(F32),
                                        ALU.subtract).then_inc(m_lo_p, 1)
            side_gpsimd(pool, 1, j, 2 * t, par, attention)
            if t % Q1 == 3 and (t > 3 or not first(j)):
                mix1_sum(pool, j, t)
            side_gpsimd(pool, 1, j, 2 * t + 1, par, attention)

        def runs(eng, tiles, step):
            for i in (0, 1):
                for t in range(tiles):
                    step(eng, i, i, t, False)
            with eng.Fori(0, B // 2) as pair:
                for par in (0, 1):
                    for t in range(tiles):
                        step(eng, pair * 2 + (2 + par), par, t, True)
            for i in (CALLS - 2, CALLS - 1):
                for t in range(tiles):
                    step(eng, i, i % 2, t, False)

        @block.tensor
        def _(pe):
            pe.wait_ge(wt_in, 16 * 8)
            pe.wait_ge(const_in, 16 * 5)
            for k in range(10):
                last = nc.tensor.transpose(bank[k // 4][:, cut(k % 4)], rawt[:, k, :], ident[:, :])
                if k in (3, 7, 9):
                    last.then_inc(wt_ps, 1)
            pe.wait_ge(cols_in, 16 * 3)
            nc.tensor.transpose(bank[3][:, 0:H1 + E + 1], raw_cols, ident[0:H1 + E + 1, 0:H1 + E + 1]).then_inc(cols_ps, 1)
            norm_tensor(pe, 0, 0)
            pe.wait_ge(set_up, 4)
            router_tensor(pe, 0, 0, 0, 0, "logits")
            router_tensor(pe, 0, 0, 0, 0, "gates")
            pe.wait_ge(w0_done, 3)
            pe.wait_ge(wt_done, 3)
            runs(pe, H0, mix0_tensor)
            T = CALLS * H0
            for t in range(3):
                mix0_down(pe, T - 3 + t, H0 - 3 + t, CALLS - 1)
            pe.wait_ge(f_sg, T)
            mix0_turn(pe, CALLS)
            pe.wait_ge(f_x, CALLS)
            pe.wait_ge(w1_done, PIECES)
            runs(pe, H1, mix1_tensor)
            for t in range(3):
                mix1_down(pe, CALLS, t)
            mix1_turn(pe, CALLS - 1)

        @block.scalar
        def _(act):
            act.dma_start(ident_b[:, :], a["c_ident"].bitcast(BF16)).then_inc(const_in, 16)
            act.dma_start(ident_etc[:, :], a["c_const"]).then_inc(const_in, 16)
            act.dma_start(mask[:, :, :], a["c_mask"].bitcast(BF16)).then_inc(const_in, 16)
            act.dma_start(spread_b[:, :], a["c_spread"].bitcast(BF16)).then_inc(const_in, 16)
            act.dma_start(near_b[:, :], a["c_near"].bitcast(BF16)).then_inc(const_in, 16)
            act.dma_start(rawt[:, 0:3, :], a["L0_attn_W_in"].rearrange("(k p) c -> p k c", p=P)).then_inc(wt_in, 16)
            for k, name in enumerate(["L0_attn_W_g1", "L0_attn_W_g2", "L0_attn_W_out",
                                      "L1_attn_Wq", "L1_attn_Wk", "L1_attn_Wv", "L1_attn_Wo"]):
                act.dma_start(rawt[:, 3 + k, :], a[name]).then_inc(wt_in, 16)
            act.dma_start(raw_cols[0:H1, :], a["L1_ffn_b1"].rearrange("e (q p) -> (e q) p", p=P)).then_inc(cols_in, 16)
            act.dma_start(raw_cols[H1:H1 + E, :], a["L1_ffn_b2"]).then_inc(cols_in, 16)
            act.dma_start(raw_cols[H1 + E:H1 + E + 1, :], a["L0_attn_ln_w"].unsqueeze(0)).then_inc(cols_in, 16)
            for m, name in enumerate(["L0_ffn_w_gate", "L1_ffn_gate_w"]):
                act.dma_start(wgate[:, m, :], a[name]).then_inc(rows_in, 16)
            at = 0
            for name in ["L1_attn_bq", "L1_attn_bk", "L1_attn_bv", "L1_attn_gq", "L1_attn_gk", "L1_attn_gv",
                         "L1_attn_betaq", "L1_attn_betak", "L1_attn_betav", "L1_attn_bo", "L1_attn_go", "L1_attn_betao",
                         "L1_ffn_gate_b", "L1_attn_scale"]:
                w = int(np.prod(a[name].shape))
                act.dma_start(rows[:, at:at + w], a[name].partition_broadcast(P)).then_inc(rows_in, 16)
                at += w
            norm_scalar(act, 0, 0)
            act.wait_ge(w0_in, 16 * 3)
            for k in range(3):
                nc.scalar.activation(w0_hi[:, k * H0:(k + 1) * H0, :].rearrange("p a n -> p (a n)"),
                                     raw0[:, k * H0 * P:(k + 1) * H0 * P], ACT.Copy).then_inc(w0_hi_done, 1)
            router_scalar(act, 0, 0)
            for k in range(3):
                act.wait_ge(wt_ps, k + 1)
                w = min(4, 10 - 4 * k)
                nc.scalar.activation(wt_hi[:, 4 * k:4 * k + w, :].rearrange("p a n -> p (a n)"),
                                     bank[k][:, 0:w * P], ACT.Copy).then_inc(wt_hi_done, 1)
            runs(act, H0, mix0_scalar)
            mix0_hi(act, CALLS * H0 - 1, H0 - 1)
            mix0_out(act, CALLS - 1)
            runs(act, H1, mix1_scalar)

        @block.vector
        def _(dve):
            nc.vector.memset(base_e, float(np.e)).then_inc(set_up, 1)
            for n, count in enumerate((a_read, a_step, a_ps, a_pool)):
                nc.vector.memset(small[:, 36 + n:37 + n], 0.0).then_inc(count, 1)
            dve.wait_ge(x_in[0], 16)
            norm_vector(dve, 0, 0, "stats")
            dve.wait_ge(cols_ps, 1)
            nc.vector.tensor_copy(cols[:, :], bank[3][:, 0:H1 + E + 1]).then_inc(set_up, 1)
            norm_vector(dve, 0, 0, "norm")
            norm_vector(dve, 0, 0, "split", 0)
            dve.wait_ge(rows_in, 16 * 16)
            nc.vector.tensor_copy(wgate_hi[:, :, :], wgate[:, :, :]).then_inc(set_up, 1)
            dve.wait_ge(set_up, 3)
            nc.vector.tensor_tensor(wgate_lo[:, :, :], wgate[:, :, :], wgate_hi[:, :, :].bitcast(F32),
                                    ALU.subtract).then_inc(set_up, 1)
            for k in range(3):
                dve.wait_ge(w0_hi_done, k + 1)
                nc.vector.tensor_tensor(w0_lo[:, k * H0:(k + 1) * H0, :].rearrange("p a n -> p (a n)"),
                                        raw0[:, k * H0 * P:(k + 1) * H0 * P],
                                        w0_hi[:, k * H0:(k + 1) * H0, :].rearrange("p a n -> p (a n)").bitcast(F32),
                                        ALU.subtract).then_inc(w0_done, 1)
            router_vector(dve, 0, 0, "pick")
            router_vector(dve, 0, 0, "gate")
            for k in range(3):
                dve.wait_ge(wt_hi_done, k + 1)
                w = min(4, 10 - 4 * k)
                nc.vector.tensor_tensor(wt_lo[:, 4 * k:4 * k + w, :].rearrange("p a n -> p (a n)"), bank[k][:, 0:w * P],
                                        wt_hi[:, 4 * k:4 * k + w, :].rearrange("p a n -> p (a n)").bitcast(F32),
                                        ALU.subtract).then_inc(wt_done, 1)
            for b in range(1, B):
                dve.wait_ge(x_in[b], 16)
            runs(dve, H0, mix0_vector)
            mix0_add_prev(dve, CALLS)
            runs(dve, H1, mix1_vector)
            mix1_gate(dve, CALLS, 3)
            mix1_add(dve, CALLS - 1, B - 1)

        @block.gpsimd
        def _(pool):
            nc.gpsimd.memset(neg_half, -0.5).then_inc(pool_set, 1)
            nc.gpsimd.memset(neg_half12[:, :], -0.5).then_inc(pool_set, 1)
            pool.wait_ge(pool_set, 2)
            norm_gpsimd(pool, 0)
            router_gpsimd(pool, 0, 0)
            runs(pool, H0, mix0_gpsimd)
            mix0_lo(pool, CALLS * H0 - 1, H0 - 1)
            runs(pool, H1, mix1_gpsimd)
            mix1_sum(pool, CALLS, 3)


INPUTS = ["L0_attn_x", "L0_attn_W_in", "L0_attn_W_out", "L0_attn_W_g1", "L0_attn_W_g2", "L0_attn_ln_w",
          "L0_ffn_w_gate", "L0_ffn_w_g", "L0_ffn_w_u", "L0_ffn_w_d",
          "L1_attn_Wq", "L1_attn_bq", "L1_attn_Wk", "L1_attn_bk", "L1_attn_Wv", "L1_attn_bv", "L1_attn_Wo", "L1_attn_bo",
          "L1_attn_gq", "L1_attn_betaq", "L1_attn_gk", "L1_attn_betak", "L1_attn_gv", "L1_attn_betav",
          "L1_attn_go", "L1_attn_betao", "L1_attn_scale",
          "L1_ffn_gate_w", "L1_ffn_gate_b", "L1_ffn_w1", "L1_ffn_b1", "L1_ffn_w2", "L1_ffn_b2"]


def kernel(**inputs):
    import concourse.bacc as bacc
    from concourse.bass_utils import run_bass_kernel_spmd

    nc = bacc.Bacc("TRN2", target_bir_lowering=False, num_devices=1)
    arrays, a = {}, {}

    def give(name, array):
        arrays[f"in_{name}"] = array
        a[name] = nc.dram_tensor(f"in_{name}", array.shape, mybir.dt.from_np(array.dtype), kind="ExternalInput").ap()

    for name in INPUTS:
        array = np.ascontiguousarray(inputs[name])
        give(name, array.reshape(1) if array.ndim == 0 else array)
    for name, array in shape_constants().items():
        give(name, array)
    out = nc.dram_tensor("out_x", (B, N, P), F32, kind="ExternalOutput").ap()
    macaron(nc, a, out)
    r = run_bass_kernel_spmd(nc, [arrays], core_ids=[0])
    return r.results[0]["out_x"]
```

```python
from contextlib import ExitStack

import numpy as np

import concourse.bass as bass
from concourse import mybir

F32 = mybir.dt.float32
F32R = mybir.dt.float32r
BF16 = mybir.dt.bfloat16
ALU = mybir.AluOpType
ACT = mybir.ActivationFunctionType
AX = mybir.AxisListType

P = 128
B, N = 4, 512
TT = N // P
E = 8
M0 = 176
H0 = E * M0 // P
M1 = 512
Q1 = M1 // P
H1 = E * Q1
HEADS = 16
DH = P // HEADS
EPS = 1e-5
LEVELS = [1, 2, 4, 8, 16, 32, 64]
MASKS = 5
CALLS = 2 * B

C_ID = 0
C_HEAD = C_ID + P
C_RANK = C_HEAD + P
NCONST = C_RANK + TT * E
R_BIAS, R_G, R_BETA = 0, 3 * P, 6 * P
R_BO, R_GO, R_BETAO = 9 * P, 10 * P, 11 * P
R_GB, R_SC = 12 * P, 12 * P + E
NROWS = R_SC + 1


def bf16_bits(v):
    return (v.astype(np.float32).view(np.uint32) >> 16).astype(np.uint16)


def shape_constants():
    const = np.zeros((P, NCONST), np.float32)
    const[:, C_ID:C_ID + P] = np.eye(P)
    at = np.arange(P)
    const[:, C_HEAD:C_HEAD + P] = 2.0 * (at[:, None] // DH == at[None, :] // DH)
    s, t = at[:, None], at[None, :]
    mask = np.stack([(s // (2 * h) == t // (2 * h)) & (s // h % 2 == 0) & (t // h % 2 == 1) for h in LEVELS], 1)
    mask = np.concatenate([mask[:, :MASKS - 1], mask[:, MASKS - 1:].any(1, keepdims=True)], 1)
    const[:, C_RANK:C_RANK + TT * E] = np.tile(E - np.arange(E), TT)
    spread = np.zeros((3 * E, H0 * P + E * P), np.float32)
    spread[:, :H0 * P] = (np.arange(3 * E)[:, None] % E) == (np.arange(H0 * P)[None, :] // M0)
    spread[:, H0 * P:] = (np.arange(3 * E)[:, None] % E) == (np.arange(E * P)[None, :] // P)
    dist = np.abs(np.arange(2 * N - P)[None, :] - (N - P) - at[:, None]).astype(np.float32)
    near = np.maximum(np.ceil(np.log2(np.float32(N - 1) / (dist + np.float32(1)))), 0) + DH / 2
    return {"c_const": const, "c_mask": bf16_bits(mask), "c_spread": bf16_bits(spread), "c_near": bf16_bits(near),
            "c_ident": bf16_bits(np.eye(P))}


def macaron(nc, a, out):
    ctx = ExitStack()
    with ctx:
        def sb(name, shape, dt=F32):
            return ctx.enter_context(nc.sbuf_tensor(name, shape, dt))

        def sem(name):
            return ctx.enter_context(nc.semaphore(name))

        x = sb("x", [P, B, TT, P])
        w0_hi = sb("w0_hi", [P, 3 * H0, P], F32R)
        w0_lo = sb("w0_lo", [P, 3 * H0, P], F32R)
        w1_hi = sb("w1_hi", [P, 2 * H1, P], F32R)
        w1_lo = sb("w1_lo", [P, 2 * H1, P], F32R)
        wt_hi = sb("wt_hi", [P, 10, P], F32R)
        wt_lo = sb("wt_lo", [P, 10, P], F32R)
        mask = sb("mask", [P, MASKS, P], BF16)
        ident_etc = sb("ident_etc", [P, NCONST])
        ident, head2 = ident_etc[:, C_ID:C_ID + P], ident_etc[:, C_HEAD:C_HEAD + P]
        rank = ident_etc[:, C_RANK:C_RANK + TT * E].rearrange("p (t e) -> p t e", e=E)
        spread_b = sb("spread_b", [3 * E, H0 * P + E * P], BF16)
        near_b = sb("near_b", [P, 2 * N - P], BF16)
        ident_b = sb("ident_b", [P, P], BF16)
        rows = sb("rows", [P, NROWS])
        cols = sb("cols", [P, H1 + E + 1])
        wgate = sb("wgate", [P, 2, E])
        wgate_hi = sb("wgate_hi", [P, 2, E], F32R)
        wgate_lo = sb("wgate_lo", [P, 2, E], F32R)
        small = sb("small", [P, 40])
        base_e = small[:, 0:32].rearrange("p (t e) -> p t e", e=E)
        neg_half = small[:, 32:36]
        neg_half12 = sb("neg_half12", [P, 12])
        fw = sb("fw", [P, 7, N])
        h_hi = sb("h_hi", [P, 4, N], F32R)
        h_lo = sb("h_lo", [P, 4, N], F32R)
        acc = sb("acc", [P, N])
        xT_hi = sb("xT_hi", [P, 2, N], F32R)
        xT_lo = sb("xT_lo", [P, 2, N], F32R)
        zT_hi = sb("zT_hi", [P, N], F32R)
        zT_lo = sb("zT_lo", [P, N], F32R)
        r_hi = sb("r_hi", [P, N], F32R)
        r_lo = sb("r_lo", [P, N], F32R)
        gT = sb("gT", [3 * E, 2, N], BF16)
        gw = sb("gw", [P, 11, N])
        xn = sb("xn", [P, TT, P])
        stats = sb("stats", [P, TT, 6])
        mom = sb("mom", [P, 7, TT])
        rstd = sb("rstd", [P, TT])
        rt = sb("rt", [P, 7, TT, E])
        m8 = sb("m8", [P, 6, TT])
        g3 = sb("g3", [P, TT, 3 * E])
        g3b = sb("g3b", [P, 2, TT, E], BF16)
        astats = sb("astats", [P, 3 * TT, 6])
        amom = sb("amom", [P, 7, 3 * TT])
        arstd = sb("arstd", [P, 3 * TT])

        bank = [ctx.enter_context(nc.psum_tensor(f"bank{n}", [P, N], F32)) for n in range(8)]
        side, att = bank[6], bank[7]

        stage = gw[:, :, :].rearrange("p a n -> p (a n)")
        raw0 = stage[:, 0:3 * H0 * P]
        rawt = stage[:, 3 * H0 * P:(3 * H0 + 10) * P].rearrange("p (k c) -> p k c", c=P)
        raw_cols = xn[0:H1 + E + 1, 0, :]
        PIECE, RING = 2 * N, 5
        PIECES = 2 * H1 * P // PIECE
        w1_hi_f = w1_hi[:, :, :].rearrange("p a n -> p (a n)")
        w1_lo_f = w1_lo[:, :, :].rearrange("p a n -> p (a n)")

        x_in = [sem(f"x_in{b}") for b in range(B)]
        const_in, w0_in, wt_in, rows_in, cols_in = map(sem, ["const_in", "w0_in", "wt_in", "rows_in", "cols_in"])
        w1_in = [sem(f"w1_in{n}") for n in range(RING)]
        stored = sem("stored")
        set_up, wt_ps, wt_hi_done, wt_done, cols_ps = map(sem, ["set_up", "wt_ps", "wt_hi_done", "wt_done", "cols_ps"])
        w0_hi_done, w0_done, w1_hi_done, w1_done, pool_set = map(
            sem, ["w0_hi_done", "w0_done", "w1_hi_done", "w1_done", "pool_set"])
        ln_stats, ln_rstd, ln_xn, xT_ps, xT_hi_done, xT_done = map(
            sem, ["ln_stats", "ln_rstd", "ln_xn", "xT_ps", "xT_hi_done", "xT_done"])
        logits_ps, rt_step, rt_shift, rt_exp, g3_done, gT_ps, gT_done = map(
            sem, ["logits_ps", "rt_step", "rt_shift", "rt_exp", "g3_done", "gT_ps", "gT_done"])
        f_gate, f_spread, f_up, f_silu, f_sg, f_h, f_hi, f_lo, f_down, f_y, f_yT, f_x = map(
            sem, ["f_gate", "f_spread", "f_up", "f_silu", "f_sg", "f_h", "f_hi", "f_lo", "f_down", "f_y", "f_yT", "f_x"])
        m_up, m_spread, m_silu, m_gs, m_hi, m_lo_v, m_lo_p, m_down, m_y, m_acc, m_yT, m_x = map(
            sem, ["m_up", "m_spread", "m_silu", "m_gs", "m_hi", "m_lo_v", "m_lo_p", "m_down", "m_y", "m_acc", "m_yT", "m_x"])
        a_ps, a_read, a_act, a_step, a_pool = map(sem, ["a_ps", "a_read", "a_act", "a_step", "a_pool"])

        gq, gF, gR, gk, gX0, gX1, gP, gT0, gT1, gv, gG = (gw[:, n, :] for n in range(11))
        gX, gTm = [gX0, gX1], [gT0, gT1]
        gS, gon = gk, gq
        flat = stage
        spre = flat[:, 0:3 * TT * P].rearrange("p (t c) -> p t c", c=3 * P)
        spk = flat[:, 3 * N:5 * N].bitcast(BF16)[:, 0:3 * TT * P].rearrange("p (t c) -> p t c", c=3 * P)
        so = flat[:, 5 * N:6 * N].rearrange("p (t c) -> p t c", c=P)

        block = ctx.enter_context(nc.Block())

        def mm(dst, lhsT, rhs, start=True, stop=True):
            return nc.tensor.matmul(dst, lhsT, rhs, start=start, stop=stop)

        def mm3(dst, l_hi, l_lo, r_hi_, r_lo_, start=True, stop=True):
            mm(dst, l_hi, r_hi_, start, False)
            mm(dst, l_lo, r_hi_, False, False)
            return mm(dst, l_hi, r_lo_, False, stop)

        def wide(ap, n):
            return ap.unsqueeze(2).to_broadcast([ap.shape[0], ap.shape[1], n])

        @block.sync
        def _(sp):
            for b in range(B):
                sp.dma_start(x[:, b, :, :], a["L0_attn_x"][b].rearrange("(t p) d -> p t d", p=P)).then_inc(x_in[b], 16)
                if b == 0:
                    for k, name in enumerate(["w_g", "w_u"]):
                        sp.dma_start(raw0[:, k * H0 * P:(k + 1) * H0 * P].rearrange("p (e m) -> p e m", e=E),
                                     a["L0_ffn_" + name].rearrange("e d m -> d e m")).then_inc(w0_in, 16)
                    sp.dma_start(raw0[:, 2 * H0 * P:].rearrange("p (t d) -> p t d", d=P),
                                 a["L0_ffn_w_d"].rearrange("e m d -> (e m) d").rearrange("(t p) d -> p t d", p=P)
                                 ).then_inc(w0_in, 16)
            for n in range(PIECES):
                if n < RING:
                    sp.wait_ge(w0_done, 3)
                    sp.wait_ge(wt_ps, 3)
                else:
                    sp.wait_ge(w1_done, n - RING + 1)
                    sp.wait_ge(w1_hi_done, n - RING + 1)
                dst = stage[:, (n % RING) * PIECE:(n % RING + 1) * PIECE]
                if n < PIECES // 2:
                    e = n * PIECE // M1
                    sp.dma_start(dst.rearrange("p (e h) -> p e h", h=M1),
                                 a["L1_ffn_w1"][e:e + PIECE // M1].rearrange("e d h -> d e h")).then_inc(w1_in[n % RING], 16)
                else:
                    t = (n - PIECES // 2) * PIECE
                    sp.dma_start(dst.rearrange("p (t d) -> p t d", d=P),
                                 a["L1_ffn_w2"].rearrange("e h d -> (e h) d")[t:t + PIECE].rearrange("(t p) d -> p t d", p=P)
                                 ).then_inc(w1_in[n % RING], 16)
            for b in range(B):
                sp.wait_ge(m_x, B + b + 1)
                sp.dma_start(out[b].rearrange("(t p) d -> p t d", p=P), x[:, b, :, :]).then_inc(stored, 16)
            sp.wait_ge(stored, 16 * B)

        def cut(t):
            return slice(t * P, (t + 1) * P)

        def need(eng, s, value):
            if not isinstance(value, int) or value > 0:
                eng.wait_ge(s, value)

        GLA, GLA_V, GLA_A, GLA_P = 18, 47, 5, 6
        FIRST, LAST, SELF = 5, 5 + len(LEVELS) - 1, 5 + len(LEVELS)
        JOIN = FIRST + MASKS - 1
        GLA_R = GLA - (LAST - JOIN)
        MASKED = [*range(FIRST, JOIN), LAST, SELF]

        def reads_before(k):
            return k if k <= JOIN else max(JOIN, k - (LAST - JOIN))

        SPK, SPK_V, SPK_P = TT + 4, 53, 2
        LEVEL_PIECES = [f"level {lv}" for lv in range(len(LEVELS))]
        MOM = 7

        def first(i):
            return isinstance(i, int) and i == 0

        def last_run(i):
            return isinstance(i, int) and i == CALLS - 1

        def back(t, ring):
            if t >= ring:
                return ring
            return H0 + t - max(u for u in range(H0) if u % ring == t)

        def gla_tensor(pe, g, k):
            pe.wait_ge(a_read, g * GLA_R + reads_before(k) + 1)
            if k == 0:
                pe.wait_ge(xT_done, 2 * g + 4)
                last = mm3(att[:, :], wt_hi[:, 1, :], wt_lo[:, 1, :], zT_hi[:, :], zT_lo[:, :])
            elif k == 1:
                last = mm3(att[:, :], wt_hi[:, 2, :], wt_lo[:, 2, :], zT_hi[:, :], zT_lo[:, :])
            elif k == 2:
                last = mm3(att[:, :], wt_hi[:, 3, :], wt_lo[:, 3, :], zT_hi[:, :], zT_lo[:, :])
            elif k == 3:
                for t in range(TT):
                    last = mm3(att[:, cut(t)], zT_hi[:, cut(t)], zT_lo[:, cut(t)], wt_hi[:, 0, :], wt_lo[:, 0, :])
            elif k == 4:
                for t in range(TT):
                    last = mm3(att[:, cut(t)], r_hi[:, cut(t)], r_lo[:, cut(t)], wt_hi[:, 4, :], wt_lo[:, 4, :])
            elif k <= LAST:
                pe.wait_ge(a_step, 1 + g * GLA_V + 4 * (k - FIRST) + 2)
                xl = gX[(k - FIRST) % 2]
                h = LEVELS[k - FIRST]
                for t in range(TT):
                    if k <= JOIN:
                        last = mm(att[:, cut(t)], xl[:, cut(t)], xl[:, cut(t)])
                        continue
                    for q in range(h, P, 2 * h):
                        last = mm(att[0:q, t * P + q:t * P + q + h], xl[:, t * P:t * P + q],
                                  xl[:, t * P + q:t * P + q + h])
            elif k == SELF:
                for t in range(TT):
                    last = mm(att[:, cut(t)], gk[:, cut(t)], gq[:, cut(t)])
            elif k == 13:
                pe.wait_ge(a_step, 1 + g * GLA_V + 29)
                for t in range(TT):
                    last = nc.tensor.transpose(att[:, cut(t)], gX1[:, cut(t)], ident[:, :])
            elif k == 14:
                for t in range(TT - 1):
                    last = mm(att[:, cut(t)], gT0[:, cut(t)], gv[:, cut(t)])
            elif k == 15:
                pe.wait_ge(a_step, 1 + g * GLA_V + 32)
                pe.wait_ge(a_pool, 1 + g * GLA_P + 5)
                for t in range(TT):
                    last = mm(att[:, cut(t)], gP[:, cut(t)], gv[:, cut(t)], True, t == 0)
                    if t:
                        last = mm(att[:, cut(t)], gX0[:, cut(t)], gS[:, cut(t - 1)], False, True)
            elif k == 16:
                pe.wait_ge(a_step, 1 + g * GLA_V + 47)
                for t in range(TT):
                    last = nc.tensor.transpose(att[:, cut(t)], gon[:, cut(t)], ident[:, :])
            else:
                for t in range(TT):
                    last = mm3(att[:, cut(t)], zT_hi[:, cut(t)], zT_lo[:, cut(t)], wt_hi[:, 5, :], wt_lo[:, 5, :])
            last.then_inc(a_ps, 1)

        def spike_tensor(pe, s, k):
            pe.wait_ge(a_read, B * GLA_R + s * SPK + k + 1)
            v0 = 1 + B * GLA_V + s * SPK_V
            if k < TT:
                if k == 0:
                    pe.wait_ge(xT_done, 2 * s + 16)
                w = wt_hi[:, 6:9, :].rearrange("p a n -> p (a n)"), wt_lo[:, 6:9, :].rearrange("p a n -> p (a n)")
                last = mm3(att[:, 0:3 * P], zT_hi[:, cut(k)], zT_lo[:, cut(k)], *w)
            elif k == TT:
                pe.wait_ge(a_step, v0 + 35)
                for t in range(TT):
                    last = mm(att[:, 0:P], spk[:, t, P:2 * P], spk[:, t, 2 * P:3 * P], t == 0, t == TT - 1)
            elif k == TT + 1:
                for t in range(TT):
                    last = mm(att[:, cut(t)], spk[:, t, 0:P], ident_b[:, :])
            elif k == TT + 2:
                last = mm(att[:, :], r_lo[:, 0:P], r_hi[:, :], True, False)
                for t in range(TT):
                    u = N - P - t * P
                    last = mm(att[:, :], spk[:, t, 2 * P:3 * P], near_b[:, u:u + N], False, t == TT - 1)
            else:
                for t in range(TT):
                    mm(att[:, cut(t)], zT_hi[:, cut(t)], wt_hi[:, 9, :], True, False)
                    last = mm(att[:, cut(t)], zT_hi[:, cut(t)], wt_lo[:, 9, :], False, True)
            last.then_inc(a_ps, 1)

        def gla_scalar(act, g, k):
            if k in (0, 1, 2, 3, 4, 13, 16):
                act.wait_ge(a_ps, 1 + g * GLA + k + 1)
            if k == 0:
                nc.scalar.activation(gq, att[:, :], ACT.Silu).then_inc(a_read, 1)
            elif k == 1:
                r, c = g * GLA_R + 1, g * GLA_A
                nc.scalar.activation(gF, att[:, :], ACT.Tanh, scale=0.5).then_inc(a_read, 1)
                act.wait_ge(a_read, r + 2)
                nc.scalar.activation(gk, gF, ACT.Copy, scale=-0.5, bias=0.5).then_inc(a_act, 1)
                act.wait_ge(a_act, c + 1)
                nc.scalar.activation(gF, gF, ACT.Copy, scale=0.5, bias=0.5).then_inc(a_act, 1)
                act.wait_ge(a_act, c + 2)
                nc.scalar.activation(gR, gF, ACT.Copy, scale=0.0, bias=1.0).then_inc(a_act, 1)
            elif k == 2:
                nc.scalar.activation(r_hi[:, :], att[:, :], ACT.Copy).then_inc(a_act, 1)
            elif k == 3:
                nc.scalar.activation(gv, att[:, :], ACT.Copy).then_inc(a_read, 1)
            elif k == 4:
                nc.scalar.activation(gG, att[:, :], ACT.Tanh, scale=0.5).then_inc(a_read, 1)
            elif k == 13:
                act.wait_ge(a_pool, 1 + g * GLA_P + 4)
                nc.scalar.activation(gT0, att[:, :], ACT.Copy).then_inc(a_read, 1)
            elif k == 16:
                nc.scalar.activation(zT_hi[:, :], att[:, :], ACT.Copy, scale=cols[:, H1 + E:H1 + E + 1]).then_inc(a_act, 1)

        def spike_scalar(act, s, k):
            if k == TT + 1:
                act.wait_ge(a_ps, 1 + B * GLA + s * SPK + k + 1)
                nc.scalar.activation(r_hi[:, :], att[:, :], ACT.Copy).then_inc(a_read, 1)

        def gla_gpsimd(pool, g, k):
            v0, p0 = 1 + g * GLA_V, 1 + g * GLA_P
            if k in MASKED[1:]:
                n = MASKED.index(k)
                pool.wait_ge(a_read, g * GLA_R + reads_before(k) + 2)
                need(pool, a_pool, p0 + n - 1)
                nc.gpsimd.tensor_tensor(gP, gP, gTm[n % 2], ALU.add).then_inc(a_pool, 1)
            elif k == "moments":
                pool.wait_ge(a_step, v0 + 43)
                nc.gpsimd.tensor_tensor(arstd[:, 0:TT], amom[:, 6, 0:TT], neg_half12[:, 0:TT], ALU.pow).then_inc(a_pool, 1)

        def spike_gpsimd(pool, s, k):
            for at, w, v in (("moments", 3 * TT, 19), ("moments 2", TT, 46)):
                if k == at:
                    pool.wait_ge(a_step, 1 + B * GLA_V + s * SPK_V + v)
                    nc.gpsimd.tensor_tensor(arstd[:, 0:w], amom[:, 6, 0:w], neg_half12[:, 0:w], ALU.pow).then_inc(a_pool, 1)

        def moments(dve, s, base, st, mom, w, eps):
            me, mo, qe, qo = st[:, 0:w, 1], st[:, 0:w, 4], st[:, 0:w, 2], st[:, 0:w, 5]
            total, diff, sq, mean, diff2, v, out_ = (mom[:, q, 0:w] for q in range(MOM))
            V = nc.vector
            dve.wait_ge(s, base + w)
            V.tensor_tensor(total, me, mo, ALU.add).then_inc(s, 1)
            V.tensor_tensor(diff, me, mo, ALU.subtract).then_inc(s, 1)
            V.tensor_tensor(sq, qe, qo, ALU.add).then_inc(s, 1)
            dve.wait_ge(s, base + w + 3)
            V.tensor_scalar(mean, total, 0.5, None, ALU.mult).then_inc(s, 1)
            V.tensor_tensor(diff2, diff, diff, ALU.mult).then_inc(s, 1)
            dve.wait_ge(s, base + w + 5)
            V.scalar_tensor_tensor(out=v, in0=diff2, scalar=P / 4.0, in1=sq, op0=ALU.mult, op1=ALU.add).then_inc(s, 1)
            dve.wait_ge(s, base + w + 6)
            V.tensor_scalar(out_, v, 1.0 / P, eps, ALU.mult, ALU.add).then_inc(s, 1)

        def halves(ap, h):
            v = ap.rearrange("p (s two h) -> p s two h", two=2, h=h)
            return v[:, :, 0, :], v[:, :, 1, :]

        def last_of(ap, h):
            return ap[:, :, h - 1:h].to_broadcast([P, N // (2 * h), h])

        def gla_level(dve, g, lv):
            v0, h = 1 + g * GLA_V + 4 * lv, LEVELS[lv]
            dve.wait_ge(a_step, v0)
            if lv == 0:
                dve.wait_ge(a_act, g * GLA_A + 3)
            if lv < 2:
                need(dve, a_ps, 1 + g * GLA)
            else:
                dve.wait_ge(a_ps, 1 + g * GLA + 5 + lv - 1)
            (xe, xo), (ke, _), (_, qo) = halves(gX[lv % 2], h), halves(gk, h), halves(gq, h)
            (re, _), (fe, fo) = halves(gR, h), halves(gF, h)
            nc.vector.tensor_tensor(xe, ke, re, ALU.mult).then_inc(a_step, 1)
            nc.vector.tensor_tensor(xo, qo, fo, ALU.mult).then_inc(a_step, 1)
            dve.wait_ge(a_step, v0 + 1)
            nc.vector.tensor_tensor(re, re, last_of(fo, h), ALU.mult).then_inc(a_step, 1)
            dve.wait_ge(a_step, v0 + 3)
            nc.vector.tensor_tensor(fo, fo, last_of(fe, h), ALU.mult).then_inc(a_step, 1)

        def gla_vector(dve, g, k, bx):
            v0, p0, r0 = 1 + g * GLA_V, 1 + g * GLA_P, g * GLA_R + 1
            if k == 2:
                dve.wait_ge(a_act, g * GLA_A + 4)
                nc.vector.tensor_tensor(r_lo[:, :], att[:, :], r_hi[:, :].bitcast(F32), ALU.subtract).then_inc(a_read, 1)
            elif k in LEVEL_PIECES:
                gla_level(dve, g, LEVEL_PIECES.index(k))
            elif k in MASKED:
                n = MASKED.index(k)
                dve.wait_ge(a_ps, 1 + g * GLA + k + 1)
                src = att[:, :].rearrange("p (t c) -> p t c", c=P)
                m = (mask[:, n, :] if k != SELF else ident[:, :]).unsqueeze(1).to_broadcast([P, TT, P])
                if n > 2:
                    dve.wait_ge(a_pool, p0 + n - 2)
                if n == 0:
                    need(dve, a_pool, p0)
                dst = gP if n == 0 else gTm[n % 2]
                nc.vector.tensor_tensor(dst.rearrange("p (t c) -> p t c", c=P), src, m, ALU.mult).then_inc(a_read, 1)
            elif k == "decay":
                dve.wait_ge(a_step, v0 + 28)
                dve.wait_ge(a_ps, 1 + g * GLA + LAST + 1)
                nc.vector.tensor_tensor(gX1, gk, gR, ALU.mult).then_inc(a_step, 1)
                nc.vector.tensor_tensor(gX0, gq, gF, ALU.mult).then_inc(a_step, 1)
            elif k == 14:
                dve.wait_ge(a_ps, 1 + g * GLA + k + 1)
                dve.wait_ge(a_step, v0 + 30)
                nc.vector.tensor_copy(gS[:, cut(0)], att[:, cut(0)]).then_inc(a_step, 1)
                for t in range(1, TT - 1):
                    dve.wait_ge(a_step, v0 + 30 + t)
                    nc.vector.scalar_tensor_tensor(
                        out=gS[:, cut(t)], in0=gS[:, cut(t - 1)], scalar=gF[:, (t + 1) * P - 1:(t + 1) * P],
                        in1=att[:, cut(t)], op0=ALU.mult, op1=ALU.add).then_inc(a_step if t < TT - 2 else a_read, 1)
            elif k == 15:
                dve.wait_ge(a_ps, 1 + g * GLA + k + 1)
                dve.wait_ge(a_pool, p0 + 5)
                nc.vector.scalar_tensor_tensor(out=gT1, in0=gG, scalar=1.0, in1=att[:, :],
                                               op0=ALU.add, op1=ALU.mult).then_inc(a_read, 1)
                dve.wait_ge(a_read, r0 + reads_before(k) + 1)
                dve.wait_ge(a_step, v0 + 32)
                for t in range(TT):
                    nc.vector.bn_stats(astats[:, t, :], gT1[:, cut(t)]).then_inc(a_step, 1)
            elif k == "moments":
                moments(dve, a_step, v0 + 32, astats, amom, TT, 4 * EPS)
            elif k == "norm":
                dve.wait_ge(a_pool, p0 + 6)
                for t in range(TT):
                    nc.vector.tensor_scalar(gon[:, cut(t)], gT1[:, cut(t)], amom[:, 3, t:t + 1], arstd[:, t:t + 1],
                                            ALU.subtract, ALU.mult).then_inc(a_step, 1)
            elif k == 16:
                dve.wait_ge(a_act, g * GLA_A + 5)
                nc.vector.scalar_tensor_tensor(
                    out=zT_lo[:, :], in0=att[:, :], scalar=cols[:, H1 + E:H1 + E + 1], in1=zT_hi[:, :].bitcast(F32),
                    op0=ALU.mult, op1=ALU.subtract).then_inc(a_read, 1)
            elif k == 17:
                dve.wait_ge(a_ps, 1 + g * GLA + k + 1)
                xb = x[:, bx, :, :].rearrange("p t d -> p (t d)")
                nc.vector.tensor_tensor(xb, att[:, :], xb, ALU.add).then_inc(a_read, 1)

        def spike_vector(dve, s, k, bx):
            v0, p0 = 1 + B * GLA_V + s * SPK_V, 1 + B * GLA_P + s * SPK_P
            r0, s0 = B * GLA_R + s * SPK + 1, B * GLA + s * SPK + 1

            def row(at, w):
                return rows[:, at:at + w].unsqueeze(1).to_broadcast([P, TT, w])

            if k in range(SPK):
                dve.wait_ge(a_ps, s0 + k + 1)
            if k in range(TT):
                if k == 0:
                    dve.wait_ge(a_step, v0)
                nc.vector.tensor_tensor(spre[:, k, :], att[:, 0:3 * P], rows[:, R_BIAS:R_BIAS + 3 * P],
                                        ALU.add).then_inc(a_read, 1)
                dve.wait_ge(a_read, r0 + k + 1)
                for c in range(3):
                    nc.vector.bn_stats(astats[:, 3 * k + c, :], spre[:, k, cut(c)]).then_inc(a_step, 1)
            elif k == "moments":
                moments(dve, a_step, v0, astats, amom, 3 * TT, EPS)
            elif k in ("norm 0", "norm 1"):
                if k == "norm 0":
                    dve.wait_ge(a_pool, p0 + 1)
                for t in (0, 1) if k == "norm 0" else (2, 3):
                    for c in range(3):
                        n = 3 * t + c
                        nc.vector.tensor_scalar(spre[:, t, cut(c)], spre[:, t, cut(c)], amom[:, 3, n:n + 1],
                                                arstd[:, n:n + 1], ALU.subtract, ALU.mult).then_inc(a_step, 1)
            elif k == "scale":
                dve.wait_ge(a_step, v0 + 31)
                nc.vector.tensor_tensor(spre, spre, row(R_G, 3 * P), ALU.mult).then_inc(a_step, 1)
            elif k == "shift":
                dve.wait_ge(a_step, v0 + 32)
                nc.vector.tensor_tensor(spre, spre, row(R_BETA, 3 * P), ALU.add).then_inc(a_step, 1)
            elif k == "spikes":
                dve.wait_ge(a_step, v0 + 33)
                nc.vector.tensor_scalar(spk[:, :, 0:2 * P], spre[:, :, 0:2 * P], 1.0, 0.5,
                                        ALU.is_ge, ALU.subtract).then_inc(a_step, 1)
                nc.vector.tensor_scalar(spk[:, :, 2 * P:3 * P], spre[:, :, 2 * P:3 * P], 1.0, None,
                                        ALU.is_ge).then_inc(a_step, 1)
            elif k == TT:
                nc.vector.tensor_tensor(r_lo[:, 0:P], att[:, 0:P], head2, ALU.mult).then_inc(a_read, 1)
            elif k == TT + 2:
                nc.vector.tensor_scalar(zT_hi[:, :], att[:, :], rows[:, R_SC:R_SC + 1], 0.5,
                                        ALU.mult, ALU.is_ge).then_inc(a_read, 1)
            elif k == TT + 3:
                nc.vector.tensor_tensor(so, att[:, :].rearrange("p (t c) -> p t c", c=P), row(R_BO, P),
                                        ALU.add).then_inc(a_read, 1)
                dve.wait_ge(a_read, r0 + k + 1)
                dve.wait_ge(a_step, v0 + 35)
                for t in range(TT):
                    nc.vector.bn_stats(astats[:, t, :], so[:, t, :]).then_inc(a_step, 1)
            elif k == "moments 2":
                moments(dve, a_step, v0 + 35, astats, amom, TT, EPS)
            elif k == "norm 2":
                dve.wait_ge(a_pool, p0 + 2)
                for t in range(TT):
                    nc.vector.tensor_scalar(so[:, t, :], so[:, t, :], amom[:, 3, t:t + 1], arstd[:, t:t + 1],
                                            ALU.subtract, ALU.mult).then_inc(a_step, 1)
            elif k == "scale 2":
                dve.wait_ge(a_step, v0 + 50)
                nc.vector.tensor_tensor(so, so, row(R_GO, P), ALU.mult).then_inc(a_step, 1)
            elif k == "shift 2":
                dve.wait_ge(a_step, v0 + 51)
                nc.vector.tensor_tensor(so, so, row(R_BETAO, P), ALU.add).then_inc(a_step, 1)
            elif k == "spikes 2":
                dve.wait_ge(a_step, v0 + 52)
                nc.vector.scalar_tensor_tensor(out=x[:, bx, :, :], in0=so, scalar=1.0, in1=x[:, bx, :, :],
                                               op0=ALU.is_ge, op1=ALU.add).then_inc(a_step, 1)

        def norm_vector(dve, n, b, part, par=None):
            if part == "stats":
                need(dve, ln_stats, (TT + MOM) * n)
                need(dve, ln_xn, TT * n)
                for t in range(TT):
                    nc.vector.bn_stats(stats[:, t, :], x[:, b, t, :]).then_inc(ln_stats, 1)
            elif part == "moments":
                moments(dve, ln_stats, (TT + MOM) * n, stats, mom, TT, EPS)
            elif part == "norm":
                dve.wait_ge(ln_rstd, n + 1)
                need(dve, xT_ps, n)
                for t in range(TT):
                    nc.vector.tensor_scalar(xn[:, t, :], x[:, b, t, :], mom[:, 3, t:t + 1], rstd[:, t:t + 1],
                                            ALU.subtract, ALU.mult).then_inc(ln_xn, 1)
            else:
                dve.wait_ge(xT_hi_done, n + 1)
                hi, lo = (zT_hi[:, :], zT_lo[:, :]) if par is None else (xT_hi[:, par, :], xT_lo[:, par, :])
                nc.vector.tensor_tensor(lo, side[:, :], hi.bitcast(F32), ALU.subtract).then_inc(xT_done, 1)

        def norm_gpsimd(pool, n):
            pool.wait_ge(ln_stats, (TT + MOM) * (n + 1))
            nc.gpsimd.tensor_tensor(rstd[:, :], mom[:, 6, :], neg_half, ALU.pow).then_inc(ln_rstd, 1)

        def norm_tensor(pe, n, r):
            pe.wait_ge(ln_xn, TT * n + TT)
            need(pe, xT_done, n)
            need(pe, gT_done, r)
            for t in range(TT):
                last = nc.tensor.transpose(side[:, cut(t)], xn[:, t, :], ident[:, :])
            last.then_inc(xT_ps, 1)

        def norm_scalar(act, n, par=None):
            act.wait_ge(xT_ps, n + 1)
            hi = zT_hi[:, :] if par is None else xT_hi[:, par, :]
            nc.scalar.activation(hi, side[:, :], ACT.Copy).then_inc(xT_hi_done, 1)

        RT = (24, 28)

        def rt_base(r, m):
            return r * RT[0] if m == 0 else CALLS * RT[0] + (r - CALLS) * RT[1]

        def router_tensor(pe, n, r, m, par, part):
            if part == "logits":
                pe.wait_ge(xT_done, n + 1)
                for t in range(TT):
                    last = mm3(side[:, t * E:(t + 1) * E], xT_hi[:, par, cut(t)], xT_lo[:, par, cut(t)],
                               wgate_hi[:, m, :], wgate_lo[:, m, :])
                last.then_inc(logits_ps, 1)
            else:
                pe.wait_ge(rt_step, rt_base(r, m) + RT[m])
                for t in range(TT):
                    last = nc.tensor.transpose(side[0:3 * E, cut(t)], g3[:, t, :], ident[:, :])
                last.then_inc(gT_ps, 1)

        def router_scalar(act, r, par):
            act.wait_ge(gT_ps, r + 1)
            nc.scalar.activation(gT[:, par, :], side[0:3 * E, :], ACT.Copy).then_inc(gT_done, 1)

        def router_gpsimd(pool, r, m, t):
            pool.wait_ge(rt_step, rt_base(r, m) + 3)
            nc.gpsimd.tensor_tensor(rt[:, 1, t, :], base_e[:, t, :], rt[:, 1, t, :], ALU.pow).then_inc(rt_exp, 1)

        def router_vector(dve, r, m, part):
            logit, ex, eq, pick, rest, pick2, gate = (rt[:, q, :, :] for q in range(7))
            best, key, second, total, inv = (m8[:, q, :] for q in range(5))
            V, base = nc.vector, rt_base(r, m)
            done = [{"pick 0": 0, "pick 1": 3, "pick 2": 8, "gate 0": 14, "gate 1": RT[m] - 6}[part]]

            def link(instruction):
                done[0] += 1
                instruction.then_inc(rt_step, 1)
                if done[0] < RT[m]:
                    dve.wait_ge(rt_step, base + done[0])

            def first_of(values, value, one_hot):
                link(V.tensor_tensor(eq, values, wide(value, E), ALU.is_equal))
                link(V.tensor_tensor(eq, eq, rank[:, :, :], ALU.mult))
                link(V.reduce_max(key, eq, axis=AX.X))
                link(V.tensor_tensor(one_hot, eq, wide(key, E), ALU.is_equal))

            if part == "pick 0":
                dve.wait_ge(logits_ps, r + 1)
                sums = side[:, 0:TT * E].rearrange("p (t e) -> p t e", e=E)
                if m == 0:
                    link(V.tensor_copy(logit, sums))
                else:
                    link(V.tensor_tensor(logit, sums, rows[:, R_GB:R_GB + E].unsqueeze(1).to_broadcast([P, TT, E]), ALU.add))
                link(V.reduce_max(best, logit, axis=AX.X))
                link(V.tensor_tensor(ex, logit, wide(best, E), ALU.subtract))
            elif part == "pick 1":
                first_of(logit, best, pick)
                link(V.scalar_tensor_tensor(out=rest, in0=pick, scalar=-3e38, in1=logit, op0=ALU.mult, op1=ALU.add))
            elif part == "pick 2":
                link(V.reduce_max(second, rest, axis=AX.X))
                first_of(rest, second, pick2)
                link(V.tensor_tensor(pick, pick, pick2, ALU.add))
            elif part == "gate 0":
                dve.wait_ge(rt_exp, TT * (r + 1))
                if m == 1:
                    link(V.reduce_sum(total, ex, axis=AX.X))
                    link(V.reciprocal(inv, total))
                    link(V.tensor_tensor(ex, ex, wide(inv, E), ALU.mult))
                link(V.tensor_tensor(gate, ex, pick, ALU.mult))
                link(V.reduce_sum(total, gate, axis=AX.X))
                if m == 1:
                    link(V.tensor_scalar(total, total, 1e-9, None, ALU.max))
                link(V.reciprocal(inv, total))
                link(V.tensor_tensor(gate, gate, wide(inv, E), ALU.mult))
            else:
                link(V.tensor_copy(g3b[:, 0, :, :], gate))
                link(V.tensor_copy(g3[:, :, 0:E], g3b[:, 0, :, :]))
                link(V.tensor_tensor(gate, gate, g3[:, :, 0:E], ALU.subtract))
                link(V.tensor_copy(g3b[:, 1, :, :], gate))
                link(V.tensor_copy(g3[:, :, E:2 * E], g3b[:, 1, :, :]))
                link(V.tensor_tensor(g3[:, :, 2 * E:3 * E], gate, g3[:, :, E:2 * E], ALU.subtract))

        Z_AT = ({"stats": 0, "moments": 0, "rstd": 0, "norm": 1, "turn": 3, "split": 3},
                {"stats": 0, "moments": 1, "rstd": 1, "norm": 3, "turn": 7, "split": 8})
        R_AT = ({"stats": 4, "moments": 5, "rstd": 5, "norm": 7, "turn": 9, "split": 9, "logits": 12, "pick 0": 12,
                 "exp 0": 13, "exp 1": 14, "exp 2": 15, "exp 3": 16,
                 "pick 1": 14, "pick 2": 16, "gate 0": 20, "gate 1": 22, "spread": 26},
                {"stats": 5, "moments": 9, "rstd": 9, "norm": 11, "turn": 15, "split": 16, "logits": 20, "pick 0": 20,
                 "exp 0": 21, "exp 1": 23, "exp 2": 25, "exp 3": 27,
                 "pick 1": 22, "pick 2": 24, "gate 0": 29, "gate 1": 31, "spread": 38})
        GLA_PE = dict(zip([5, 6, 7, 8, 10, 11, 13, 15, 17, 19, 20, 21, 23, 24, 25, 27, 31, 32], range(GLA)))
        GLA_DVE = {7: [2], 8: ["level 0"], 9: ["level 1"], 11: [5, "level 2"], 13: [6, "level 3"], 15: [7, "level 4"],
                   17: [8, "level 5"], 19: ["level 6"], 21: [LAST], 22: ["decay"], 23: [SELF], 25: [14], 27: [15],
                   28: ["moments"], 29: ["norm"], 31: [16], 32: [17]}
        SPK_PE = dict(zip([12, 17, 21, 25, 41, 44, 47, 51], range(SPK)))
        SPK_DVE = {13: [0], 18: [1], 22: [2], 26: [3], 27: ["moments"], 30: ["norm 0"], 32: ["norm 1"], 33: ["scale"],
                   35: ["shift"], 37: ["spikes"], 41: [4], 47: [6], 51: [7], 52: ["moments 2"], 55: ["norm 2"],
                   56: ["scale 2"], 57: ["shift 2"], 58: ["spikes 2"]}
        W1_AT = {4 * k + 3: k for k in range(8)}

        def side_job(m, i, par, attention):
            r = i + 1 + m * CALLS
            if attention:
                n, zn = 2 * i + 12 * m, 2 * i + 12 * m - 1
            else:
                n, zn = i + (1 if i < 2 else 5) + 12 * m, None
            return n, zn, r, (i + 1) % B, par

        def router_mixture(m, i):
            return 1 if m == 1 or last_run(i) else 0

        def side_tensor(pe, m, i, slot, par_now, attention):
            n, zn, r, b, par = side_job(m, i, 1 - par_now, attention)
            if attention:
                if slot == Z_AT[m]["turn"]:
                    norm_tensor(pe, zn, r)
                if m == 0 and slot in GLA_PE:
                    gla_tensor(pe, i - 2, GLA_PE[slot])
                if m == 1 and slot in SPK_PE:
                    spike_tensor(pe, i - 2, SPK_PE[slot])
            if m == 0 or not last_run(i):
                at, to = R_AT[m], router_mixture(m, i)
                if slot == at["turn"]:
                    norm_tensor(pe, n, r)
                if slot == at["logits"]:
                    router_tensor(pe, n, r, to, par, "logits")
                if slot == at["spread"]:
                    router_tensor(pe, n, r, to, par, "gates")

        def side_scalar(act, m, i, slot, par_now, attention):
            n, zn, r, b, par = side_job(m, i, 1 - par_now, attention)
            if attention:
                if slot == Z_AT[m]["turn"]:
                    norm_scalar(act, zn)
                if m == 0 and slot in GLA_PE:
                    gla_scalar(act, i - 2, GLA_PE[slot])
                if m == 1 and slot in SPK_PE:
                    spike_scalar(act, i - 2, SPK_PE[slot])
            if m == 0 and first(i) and slot in W1_AT:
                k = W1_AT[slot]
                piece = slice(k * PIECE, (k + 1) * PIECE)
                act.wait_ge(w1_in[k % RING], 16 * (k // RING + 1))
                nc.scalar.activation(w1_hi_f[:, piece], stage[:, (k % RING) * PIECE:(k % RING + 1) * PIECE],
                                     ACT.Copy).then_inc(w1_hi_done, 1)
            if m == 0 or not last_run(i):
                if slot == R_AT[m]["turn"]:
                    norm_scalar(act, n, par)
                if slot == R_AT[m]["spread"]:
                    router_scalar(act, r, par)

        def side_vector(dve, m, i, slot, par_now, attention):
            n, zn, r, b, par = side_job(m, i, 1 - par_now, attention)
            if attention:
                for part in ("stats", "moments", "norm", "split"):
                    if slot == Z_AT[m][part]:
                        if part == "stats":
                            dve.wait_ge(m_x if m else f_x, i - 1)
                        norm_vector(dve, zn, i - 2, part)
                for part in (GLA_DVE, SPK_DVE)[m].get(slot, []):
                    (gla_vector, spike_vector)[m](dve, i - 2, part, i - 2)
            if m == 0 and first(i) and slot in W1_AT:
                k = W1_AT[slot]
                piece = slice(k * PIECE, (k + 1) * PIECE)
                dve.wait_ge(w1_hi_done, k + 1)
                nc.vector.tensor_tensor(w1_lo_f[:, piece], stage[:, (k % RING) * PIECE:(k % RING + 1) * PIECE],
                                        w1_hi_f[:, piece].bitcast(F32), ALU.subtract).then_inc(w1_done, 1)
            if m == 0 or not last_run(i):
                if slot == R_AT[m]["stats"]:
                    if attention:
                        if m == 0:
                            dve.wait_ge(a_read, (i - 2) * GLA_R + 1)
                        else:
                            dve.wait_ge(a_step, 1 + B * GLA_V + (i - 2) * SPK_V)
                    elif last_run(i):
                        dve.wait_ge(f_x, i - 1)
                    elif i > 1:
                        dve.wait_ge(a_read, B * GLA_R + 1) if m == 0 else dve.wait_ge(a_step, 1 + B * (GLA_V + SPK_V))
                for part in ("stats", "moments", "norm", "split"):
                    if slot == R_AT[m][part]:
                        norm_vector(dve, n, b, part, par)
                for part in ("pick 0", "pick 1", "pick 2", "gate 0", "gate 1"):
                    if slot == R_AT[m][part]:
                        router_vector(dve, r, router_mixture(m, i), part)

        def side_gpsimd(pool, m, i, slot, par_now, attention):
            n, zn, r, b, par = side_job(m, i, 1 - par_now, attention)
            if attention:
                if slot == Z_AT[m]["rstd"]:
                    norm_gpsimd(pool, zn)
                for part in (GLA_DVE, SPK_DVE)[m].get(slot, []):
                    (gla_gpsimd, spike_gpsimd)[m](pool, i - 2, part)
            if m == 0 or not last_run(i):
                if slot == R_AT[m]["rstd"]:
                    norm_gpsimd(pool, n)
                for t in range(TT):
                    if slot == R_AT[m][f"exp {t}"]:
                        router_gpsimd(pool, r, router_mixture(m, i), t)

        G0, U0, S0, Y0 = (0, 1), (2, 3), 4, 5
        s_buf, sg_buf, h_buf = fw[:, 0:2, :], fw[:, 2, :], fw[:, 3:7, :]

        def mix0_down(pe, T, td, i):
            pe.wait_ge(f_hi, T + 1)
            pe.wait_ge(f_lo, T + 1)
            if td == 0:
                need(pe, f_yT, i)
            mm3(bank[Y0][:, :], w0_hi[:, 2 * H0 + td, :], w0_lo[:, 2 * H0 + td, :], h_hi[:, td % 4, :], h_lo[:, td % 4, :],
                td == 0, td == H0 - 1).then_inc(f_down, 1)

        def mix0_turn(pe, i):
            pe.wait_ge(f_yT, i)
            for t in range(TT):
                last = nc.tensor.transpose(bank[S0][:, cut(t)], acc[:, cut(t)], ident[:, :])
            last.then_inc(f_y, 1)

        def mix0_tensor(pe, i, par, t, attention):
            T = H0 * i + t
            xh, xl = xT_hi[:, par, :], xT_lo[:, par, :]
            if t == 0:
                pe.wait_ge(gT_done, i + 1)
            need(pe, f_silu, T - back(t, 2) + 1)
            mm3(bank[G0[t % 2]][:, :], w0_hi[:, t, :], w0_lo[:, t, :], xh, xl).then_inc(f_gate, 1)
            side_tensor(pe, 0, i, 3 * t, par, attention)
            need(pe, f_sg, T)
            if t == 4:
                need(pe, f_x, i)
            mm(bank[S0][:, :], spread_b[:, cut(t)], gT[:, par, :]).then_inc(f_spread, 1)
            need(pe, f_h, T - back(t, 2) + 1)
            mm3(bank[U0[t % 2]][:, :], w0_hi[:, H0 + t, :], w0_lo[:, H0 + t, :], xh, xl).then_inc(f_up, 1)
            side_tensor(pe, 0, i, 3 * t + 1, par, attention)
            if t == 3 and not first(i):
                pe.wait_ge(f_sg, T + 1)
                mix0_turn(pe, i)
            if t >= 3 or not first(i):
                mix0_down(pe, T - 3, (t - 3) % H0, i)
            side_tensor(pe, 0, i, 3 * t + 2, par, attention)

        def mix0_hi(act, T, th):
            act.wait_ge(f_h, T + 1)
            need(act, f_down, T - back(th, 4) + 1)
            nc.scalar.activation(h_hi[:, th % 4, :], h_buf[:, th % 4, :], ACT.Copy).then_inc(f_hi, 1)

        def mix0_out(act, i):
            act.wait_ge(f_down, H0 * (i + 1))
            need(act, f_y, i)
            nc.scalar.activation(acc[:, :], bank[Y0][:, :], ACT.Copy).then_inc(f_yT, 1)

        def mix0_scalar(act, i, par, t, attention):
            T = H0 * i + t
            act.wait_ge(f_gate, T + 1)
            need(act, f_sg, T - back(t, 2) + 1)
            nc.scalar.activation(s_buf[:, t % 2, :], bank[G0[t % 2]][:, :], ACT.Silu).then_inc(f_silu, 1)
            side_scalar(act, 0, i, 3 * t, par, attention)
            side_scalar(act, 0, i, 3 * t + 1, par, attention)
            if t > 0 or not first(i):
                mix0_hi(act, T - 1, (t - 1) % H0)
            if t == 2 and not first(i):
                mix0_out(act, i - 1)
            side_scalar(act, 0, i, 3 * t + 2, par, attention)

        def mix0_add_prev(dve, i):
            dve.wait_ge(f_y, i)
            xb = x[:, (i + B - 1) % B, :, :].rearrange("p t d -> p (t d)")
            nc.vector.scalar_tensor_tensor(out=xb, in0=bank[S0][:, :], scalar=0.5, in1=xb,
                                           op0=ALU.mult, op1=ALU.add).then_inc(f_x, 1)

        def mix0_vector(dve, i, par, t, attention):
            T = H0 * i + t
            side_vector(dve, 0, i, 3 * t, par, attention)
            dve.wait_ge(f_silu, T + 1)
            dve.wait_ge(f_spread, T + 1)
            need(dve, f_h, T)
            nc.vector.tensor_tensor(sg_buf, bank[S0][:, :], s_buf[:, t % 2, :], ALU.mult).then_inc(f_sg, 1)
            dve.wait_ge(f_sg, T + 1)
            dve.wait_ge(f_up, T + 1)
            need(dve, f_hi, T - back(t, 4) + 1)
            need(dve, f_lo, T - back(t, 4) + 1)
            nc.vector.tensor_tensor(h_buf[:, t % 4, :], bank[U0[t % 2]][:, :], sg_buf,
                                    ALU.mult).then_inc(f_h, 1)
            side_vector(dve, 0, i, 3 * t + 1, par, attention)
            if t == 3 and not first(i):
                mix0_add_prev(dve, i)
            side_vector(dve, 0, i, 3 * t + 2, par, attention)

        def mix0_lo(pool, T, th):
            pool.wait_ge(f_hi, T + 1)
            need(pool, f_down, T - back(th, 4) + 1)
            nc.gpsimd.tensor_tensor(h_lo[:, th % 4, :], h_buf[:, th % 4, :], h_hi[:, th % 4, :].bitcast(F32),
                                    ALU.subtract).then_inc(f_lo, 1)

        def mix0_gpsimd(pool, i, par, t, attention):
            T = H0 * i + t
            side_gpsimd(pool, 0, i, 3 * t, par, attention)
            side_gpsimd(pool, 0, i, 3 * t + 1, par, attention)
            if t > 0 or not first(i):
                mix0_lo(pool, T - 1, (t - 1) % H0)
            side_gpsimd(pool, 0, i, 3 * t + 2, par, attention)

        U1, Y1, S1, O1 = (0, 1), (2, 3), 4, 5
        hid, gs_buf, y_buf = fw[:, 0:4, :], fw[:, 4:6, :], fw[:, 6, :]

        def mix1_down(pe, j, t):
            td = (t - 3) % H1
            pe.wait_ge(m_hi, H1 * j + t - 2)
            pe.wait_ge(m_lo_v if td % 2 else m_lo_p, H1 // 2 * j + (t - 3) // 2 + 1)
            if td % Q1 == 0:
                need(pe, m_y, E * j + (t - 3) // Q1 - 1)
            mm3(bank[Y1[td // Q1 % 2]][:, :], w1_hi[:, H1 + td, :], w1_lo[:, H1 + td, :],
                h_hi[:, td % 4, :], h_lo[:, td % 4, :], td % Q1 == 0, td % Q1 == Q1 - 1).then_inc(m_down, 1)

        def mix1_turn(pe, j):
            pe.wait_ge(m_acc, (E - 1) * (j + 1))
            need(pe, m_x, j)
            for t in range(TT):
                last = nc.tensor.transpose(bank[O1][:, cut(t)], acc[:, cut(t)], ident[:, :])
            last.then_inc(m_yT, 1)

        def mix1_tensor(pe, j, par, t, attention):
            T = H1 * j + t
            if t == 0:
                pe.wait_ge(gT_done, j + CALLS + 1)
            need(pe, m_hi, T - 1)
            mm3(bank[U1[t % 2]][:, :], w1_hi[:, t, :], w1_lo[:, t, :], xT_hi[:, par, :], xT_lo[:, par, :]).then_inc(m_up, 1)
            if t % Q1 == 0:
                need(pe, m_gs, E * j + t // Q1)
                mm(bank[S1][:, :], spread_b[:, cut(H0 + t // Q1)], gT[:, par, :]).then_inc(m_spread, 1)
            side_tensor(pe, 1, j, 2 * t, par, attention)
            if t >= 3 or not first(j):
                mix1_down(pe, j, t)
            if t == 5 and not first(j):
                mix1_turn(pe, j - 1)
            side_tensor(pe, 1, j, 2 * t + 1, par, attention)

        def mix1_scalar(act, j, par, t, attention):
            T = H1 * j + t
            act.wait_ge(m_up, T + 1)
            need(act, m_lo_v if t % 2 else m_lo_p, H1 // 2 * j + t // 2 - 1)
            nc.scalar.activation(hid[:, t % 4, :], bank[U1[t % 2]][:, :], ACT.Silu, bias=cols[:, t:t + 1]).then_inc(m_silu, 1)
            need(act, m_down, T - 3)
            nc.scalar.activation(h_hi[:, t % 4, :], bank[U1[t % 2]][:, :], ACT.Silu, bias=cols[:, t:t + 1]).then_inc(m_hi, 1)
            side_scalar(act, 1, j, 2 * t, par, attention)
            if t % Q1 == 1:
                e = t // Q1
                act.wait_ge(m_spread, E * j + e + 1)
                need(act, m_y, E * j + e - 1)
                nc.scalar.activation(gs_buf[:, e % 2, :], bank[S1][:, :], ACT.Copy).then_inc(m_gs, 1)
            side_scalar(act, 1, j, 2 * t + 1, par, attention)

        def mix1_gate(dve, j, t):
            X, e = E * j + (t - 7) // Q1, (t - 7) // Q1 % E
            run = j if t >= 7 else j - 1
            dve.wait_ge(m_down, H1 * j + t - 3)
            dve.wait_ge(m_gs, X + 1)
            if e == 0:
                need(dve, m_yT, run)
                dst = acc[:, :]
            else:
                need(dve, m_acc, (E - 1) * run + e - 1)
                dst = y_buf
            nc.vector.scalar_tensor_tensor(out=dst, in0=bank[Y1[e % 2]][:, :], scalar=cols[:, H1 + e:H1 + e + 1],
                                           in1=gs_buf[:, e % 2, :], op0=ALU.add, op1=ALU.mult).then_inc(m_y, 1)

        def mix1_add(dve, j, b):
            dve.wait_ge(m_yT, j + 1)
            xb = x[:, b, :, :].rearrange("p t d -> p (t d)")
            nc.vector.scalar_tensor_tensor(out=xb, in0=bank[O1][:, :], scalar=0.5, in1=xb,
                                           op0=ALU.mult, op1=ALU.add).then_inc(m_x, 1)

        def mix1_vector(dve, j, par, t, attention):
            T = H1 * j + t
            if t % 2:
                dve.wait_ge(m_hi, T + 1)
                need(dve, m_down, T - 3)
                nc.vector.tensor_tensor(h_lo[:, t % 4, :], hid[:, t % 4, :], h_hi[:, t % 4, :].bitcast(F32),
                                        ALU.subtract).then_inc(m_lo_v, 1)
            side_vector(dve, 1, j, 2 * t, par, attention)
            if t % Q1 == 3 and (t > 3 or not first(j)):
                mix1_gate(dve, j, t)
            if t == 5 and not first(j):
                mix1_add(dve, j - 1, (j + B - 1) % B)
            side_vector(dve, 1, j, 2 * t + 1, par, attention)

        def mix1_sum(pool, j, t):
            X, e = E * j + (t - 7) // Q1, (t - 7) // Q1 % E
            run = j if t >= 7 else j - 1
            if e > 0:
                pool.wait_ge(m_y, X + 1)
                need(pool, m_acc, (E - 1) * run + e - 1)
                nc.gpsimd.tensor_tensor(acc[:, :], acc[:, :], y_buf, ALU.add).then_inc(m_acc, 1)

        def mix1_gpsimd(pool, j, par, t, attention):
            T = H1 * j + t
            if t % 2 == 0:
                pool.wait_ge(m_hi, T + 1)
                need(pool, m_down, T - 3)
                nc.gpsimd.tensor_tensor(h_lo[:, t % 4, :], hid[:, t % 4, :], h_hi[:, t % 4, :].bitcast(F32),
                                        ALU.subtract).then_inc(m_lo_p, 1)
            side_gpsimd(pool, 1, j, 2 * t, par, attention)
            if t % Q1 == 3 and (t > 3 or not first(j)):
                mix1_sum(pool, j, t)
            side_gpsimd(pool, 1, j, 2 * t + 1, par, attention)

        def runs(eng, tiles, step):
            for i in (0, 1):
                for t in range(tiles):
                    step(eng, i, i, t, False)
            with eng.Fori(0, B // 2) as pair:
                for par in (0, 1):
                    for t in range(tiles):
                        step(eng, pair * 2 + (2 + par), par, t, True)
            for i in (CALLS - 2, CALLS - 1):
                for t in range(tiles):
                    step(eng, i, i % 2, t, False)

        @block.tensor
        def _(pe):
            pe.wait_ge(wt_in, 16 * 8)
            pe.wait_ge(const_in, 16 * 5)
            for k in range(10):
                last = nc.tensor.transpose(bank[k // 4][:, cut(k % 4)], rawt[:, k, :], ident[:, :])
                if k in (3, 7, 9):
                    last.then_inc(wt_ps, 1)
            pe.wait_ge(cols_in, 16 * 3)
            nc.tensor.transpose(bank[3][:, 0:H1 + E + 1], raw_cols, ident[0:H1 + E + 1, 0:H1 + E + 1]).then_inc(cols_ps, 1)
            norm_tensor(pe, 0, 0)
            pe.wait_ge(set_up, 4)
            router_tensor(pe, 0, 0, 0, 0, "logits")
            router_tensor(pe, 0, 0, 0, 0, "gates")
            pe.wait_ge(w0_done, 3)
            pe.wait_ge(wt_done, 3)
            runs(pe, H0, mix0_tensor)
            T = CALLS * H0
            for t in range(3):
                mix0_down(pe, T - 3 + t, H0 - 3 + t, CALLS - 1)
            pe.wait_ge(f_sg, T)
            mix0_turn(pe, CALLS)
            pe.wait_ge(f_x, CALLS)
            pe.wait_ge(w1_done, PIECES)
            runs(pe, H1, mix1_tensor)
            for t in range(3):
                mix1_down(pe, CALLS, t)
            mix1_turn(pe, CALLS - 1)

        @block.scalar
        def _(act):
            act.dma_start(ident_b[:, :], a["c_ident"].bitcast(BF16)).then_inc(const_in, 16)
            act.dma_start(ident_etc[:, :], a["c_const"]).then_inc(const_in, 16)
            act.dma_start(mask[:, :, :], a["c_mask"].bitcast(BF16)).then_inc(const_in, 16)
            act.dma_start(spread_b[:, :], a["c_spread"].bitcast(BF16)).then_inc(const_in, 16)
            act.dma_start(near_b[:, :], a["c_near"].bitcast(BF16)).then_inc(const_in, 16)
            act.dma_start(rawt[:, 0:3, :], a["L0_attn_W_in"].rearrange("(k p) c -> p k c", p=P)).then_inc(wt_in, 16)
            for k, name in enumerate(["L0_attn_W_g1", "L0_attn_W_g2", "L0_attn_W_out",
                                      "L1_attn_Wq", "L1_attn_Wk", "L1_attn_Wv", "L1_attn_Wo"]):
                act.dma_start(rawt[:, 3 + k, :], a[name]).then_inc(wt_in, 16)
            act.dma_start(raw_cols[0:H1, :], a["L1_ffn_b1"].rearrange("e (q p) -> (e q) p", p=P)).then_inc(cols_in, 16)
            act.dma_start(raw_cols[H1:H1 + E, :], a["L1_ffn_b2"]).then_inc(cols_in, 16)
            act.dma_start(raw_cols[H1 + E:H1 + E + 1, :], a["L0_attn_ln_w"].unsqueeze(0)).then_inc(cols_in, 16)
            for m, name in enumerate(["L0_ffn_w_gate", "L1_ffn_gate_w"]):
                act.dma_start(wgate[:, m, :], a[name]).then_inc(rows_in, 16)
            at = 0
            for name in ["L1_attn_bq", "L1_attn_bk", "L1_attn_bv", "L1_attn_gq", "L1_attn_gk", "L1_attn_gv",
                         "L1_attn_betaq", "L1_attn_betak", "L1_attn_betav", "L1_attn_bo", "L1_attn_go", "L1_attn_betao",
                         "L1_ffn_gate_b", "L1_attn_scale"]:
                w = int(np.prod(a[name].shape))
                act.dma_start(rows[:, at:at + w], a[name].partition_broadcast(P)).then_inc(rows_in, 16)
                at += w
            norm_scalar(act, 0, 0)
            act.wait_ge(w0_in, 16 * 3)
            for k in range(3):
                nc.scalar.activation(w0_hi[:, k * H0:(k + 1) * H0, :].rearrange("p a n -> p (a n)"),
                                     raw0[:, k * H0 * P:(k + 1) * H0 * P], ACT.Copy).then_inc(w0_hi_done, 1)
            router_scalar(act, 0, 0)
            for k in range(3):
                act.wait_ge(wt_ps, k + 1)
                w = min(4, 10 - 4 * k)
                nc.scalar.activation(wt_hi[:, 4 * k:4 * k + w, :].rearrange("p a n -> p (a n)"),
                                     bank[k][:, 0:w * P], ACT.Copy).then_inc(wt_hi_done, 1)
            runs(act, H0, mix0_scalar)
            mix0_hi(act, CALLS * H0 - 1, H0 - 1)
            mix0_out(act, CALLS - 1)
            runs(act, H1, mix1_scalar)

        @block.vector
        def _(dve):
            nc.vector.memset(base_e, float(np.e)).then_inc(set_up, 1)
            for n, count in enumerate((a_read, a_step, a_ps, a_pool)):
                nc.vector.memset(small[:, 36 + n:37 + n], 0.0).then_inc(count, 1)
            dve.wait_ge(x_in[0], 16)
            norm_vector(dve, 0, 0, "stats")
            norm_vector(dve, 0, 0, "moments")
            dve.wait_ge(cols_ps, 1)
            nc.vector.tensor_copy(cols[:, :], bank[3][:, 0:H1 + E + 1]).then_inc(set_up, 1)
            norm_vector(dve, 0, 0, "norm")
            norm_vector(dve, 0, 0, "split", 0)
            dve.wait_ge(rows_in, 16 * 16)
            nc.vector.tensor_copy(wgate_hi[:, :, :], wgate[:, :, :]).then_inc(set_up, 1)
            dve.wait_ge(set_up, 3)
            nc.vector.tensor_tensor(wgate_lo[:, :, :], wgate[:, :, :], wgate_hi[:, :, :].bitcast(F32),
                                    ALU.subtract).then_inc(set_up, 1)
            for k in range(3):
                dve.wait_ge(w0_hi_done, k + 1)
                nc.vector.tensor_tensor(w0_lo[:, k * H0:(k + 1) * H0, :].rearrange("p a n -> p (a n)"),
                                        raw0[:, k * H0 * P:(k + 1) * H0 * P],
                                        w0_hi[:, k * H0:(k + 1) * H0, :].rearrange("p a n -> p (a n)").bitcast(F32),
                                        ALU.subtract).then_inc(w0_done, 1)
            for part in ("pick 0", "pick 1", "pick 2", "gate 0", "gate 1"):
                router_vector(dve, 0, 0, part)
            for k in range(3):
                dve.wait_ge(wt_hi_done, k + 1)
                w = min(4, 10 - 4 * k)
                nc.vector.tensor_tensor(wt_lo[:, 4 * k:4 * k + w, :].rearrange("p a n -> p (a n)"), bank[k][:, 0:w * P],
                                        wt_hi[:, 4 * k:4 * k + w, :].rearrange("p a n -> p (a n)").bitcast(F32),
                                        ALU.subtract).then_inc(wt_done, 1)
            for b in range(1, B):
                dve.wait_ge(x_in[b], 16)
            runs(dve, H0, mix0_vector)
            mix0_add_prev(dve, CALLS)
            runs(dve, H1, mix1_vector)
            mix1_gate(dve, CALLS, 3)
            mix1_add(dve, CALLS - 1, B - 1)

        @block.gpsimd
        def _(pool):
            nc.gpsimd.memset(neg_half, -0.5).then_inc(pool_set, 1)
            nc.gpsimd.memset(neg_half12[:, :], -0.5).then_inc(pool_set, 1)
            pool.wait_ge(pool_set, 2)
            norm_gpsimd(pool, 0)
            for t in range(TT):
                router_gpsimd(pool, 0, 0, t)
            runs(pool, H0, mix0_gpsimd)
            mix0_lo(pool, CALLS * H0 - 1, H0 - 1)
            runs(pool, H1, mix1_gpsimd)
            mix1_sum(pool, CALLS, 3)


INPUTS = ["L0_attn_x", "L0_attn_W_in", "L0_attn_W_out", "L0_attn_W_g1", "L0_attn_W_g2", "L0_attn_ln_w",
          "L0_ffn_w_gate", "L0_ffn_w_g", "L0_ffn_w_u", "L0_ffn_w_d",
          "L1_attn_Wq", "L1_attn_bq", "L1_attn_Wk", "L1_attn_bk", "L1_attn_Wv", "L1_attn_bv", "L1_attn_Wo", "L1_attn_bo",
          "L1_attn_gq", "L1_attn_betaq", "L1_attn_gk", "L1_attn_betak", "L1_attn_gv", "L1_attn_betav",
          "L1_attn_go", "L1_attn_betao", "L1_attn_scale",
          "L1_ffn_gate_w", "L1_ffn_gate_b", "L1_ffn_w1", "L1_ffn_b1", "L1_ffn_w2", "L1_ffn_b2"]


def kernel(**inputs):
    import concourse.bacc as bacc
    from concourse.bass_utils import run_bass_kernel_spmd

    nc = bacc.Bacc("TRN2", target_bir_lowering=False, num_devices=1)
    arrays, a = {}, {}

    def give(name, array):
        arrays[f"in_{name}"] = array
        a[name] = nc.dram_tensor(f"in_{name}", array.shape, mybir.dt.from_np(array.dtype), kind="ExternalInput").ap()

    for name in INPUTS:
        array = np.ascontiguousarray(inputs[name])
        give(name, array.reshape(1) if array.ndim == 0 else array)
    for name, array in shape_constants().items():
        give(name, array)
    out = nc.dram_tensor("out_x", (B, N, P), F32, kind="ExternalOutput").ap()
    macaron(nc, a, out)
    r = run_bass_kernel_spmd(nc, [arrays], core_ids=[0])
    return r.results[0]["out_x"]
```

```python
from contextlib import ExitStack

import numpy as np

import concourse.bass as bass
from concourse import mybir

F32 = mybir.dt.float32
F32R = mybir.dt.float32r
BF16 = mybir.dt.bfloat16
ALU = mybir.AluOpType
ACT = mybir.ActivationFunctionType
AX = mybir.AxisListType

P = 128
B, N = 4, 512
TT = N // P
E = 8
M0 = 176
H0 = E * M0 // P
M1 = 512
Q1 = M1 // P
H1 = E * Q1
HEADS = 16
DH = P // HEADS
EPS = 1e-5
LEVELS = [1, 2, 4, 8, 16, 32, 64]
MASKS = 5
CALLS = 2 * B

C_ID = 0
C_HEAD = C_ID + P
C_RANK = C_HEAD + P
NCONST = C_RANK + TT * E
R_BIAS, R_G, R_BETA = 0, 3 * P, 6 * P
R_BO, R_GO, R_BETAO = 9 * P, 10 * P, 11 * P
R_GB, R_SC = 12 * P, 12 * P + E
NROWS = R_SC + 1


def bf16_bits(v):
    return (v.astype(np.float32).view(np.uint32) >> 16).astype(np.uint16)


def shape_constants():
    const = np.zeros((P, NCONST), np.float32)
    const[:, C_ID:C_ID + P] = np.eye(P)
    at = np.arange(P)
    const[:, C_HEAD:C_HEAD + P] = 2.0 * (at[:, None] // DH == at[None, :] // DH)
    s, t = at[:, None], at[None, :]
    mask = np.stack([(s // (2 * h) == t // (2 * h)) & (s // h % 2 == 0) & (t // h % 2 == 1) for h in LEVELS], 1)
    mask = np.concatenate([mask[:, :MASKS - 1], (mask[:, MASKS - 1:].any(1) | (s == t))[:, None]], 1)
    const[:, C_RANK:C_RANK + TT * E] = np.tile(E - np.arange(E), TT)
    spread = np.zeros((3 * E, H0 * P + E * P), np.float32)
    spread[:, :H0 * P] = (np.arange(3 * E)[:, None] % E) == (np.arange(H0 * P)[None, :] // M0)
    spread[:, H0 * P:] = (np.arange(3 * E)[:, None] % E) == (np.arange(E * P)[None, :] // P)
    dist = np.abs(np.arange(2 * N - P)[None, :] - (N - P) - at[:, None]).astype(np.float32)
    near = np.maximum(np.ceil(np.log2(np.float32(N - 1) / (dist + np.float32(1)))), 0) + DH / 2
    return {"c_const": const, "c_mask": bf16_bits(mask), "c_spread": bf16_bits(spread), "c_near": bf16_bits(near),
            "c_ident": bf16_bits(np.eye(P))}


def macaron(nc, a, out):
    ctx = ExitStack()
    with ctx:
        def sb(name, shape, dt=F32):
            return ctx.enter_context(nc.sbuf_tensor(name, shape, dt))

        def sem(name):
            return ctx.enter_context(nc.semaphore(name))

        x = sb("x", [P, B, TT, P])
        w0_hi = sb("w0_hi", [P, 3 * H0, P], F32R)
        w0_lo = sb("w0_lo", [P, 3 * H0, P], F32R)
        w1_hi = sb("w1_hi", [P, 2 * H1, P], F32R)
        w1_lo = sb("w1_lo", [P, 2 * H1, P], F32R)
        wt_hi = sb("wt_hi", [P, 10, P], F32R)
        wt_lo = sb("wt_lo", [P, 10, P], F32R)
        wt_all = sb("wt_all", [P, 2, P])
        mask = sb("mask", [P, MASKS, P], BF16)
        ident_etc = sb("ident_etc", [P, NCONST])
        ident, head2 = ident_etc[:, C_ID:C_ID + P], ident_etc[:, C_HEAD:C_HEAD + P]
        rank = ident_etc[:, C_RANK:C_RANK + TT * E].rearrange("p (t e) -> p t e", e=E)
        spread_b = sb("spread_b", [3 * E, H0 * P + E * P], BF16)
        near_b = sb("near_b", [P, 2 * N - P], BF16)
        ident_b = sb("ident_b", [P, P], BF16)
        rows = sb("rows", [P, NROWS])
        cols = sb("cols", [P, H1 + E + 1])
        wgate = sb("wgate", [P, 2, E])
        wgate_hi = sb("wgate_hi", [P, 2, E], F32R)
        wgate_lo = sb("wgate_lo", [P, 2, E], F32R)
        small = sb("small", [P, 41])
        base_e = small[:, 0:32].rearrange("p (t e) -> p t e", e=E)
        neg_half = small[:, 32:36]
        neg_half12 = sb("neg_half12", [P, 12])
        fw = sb("fw", [P, 7, N])
        h_hi = sb("h_hi", [P, 4, N], F32R)
        h_lo = sb("h_lo", [P, 4, N], F32R)
        acc = sb("acc", [P, N])
        xT_hi = sb("xT_hi", [P, 2, N], F32R)
        xT_lo = sb("xT_lo", [P, 2, N], F32R)
        zT_hi = sb("zT_hi", [P, N], F32R)
        zT_lo = sb("zT_lo", [P, N], F32R)
        r_hi = sb("r_hi", [P, N], F32R)
        r_lo = sb("r_lo", [P, P], F32R)
        gT = sb("gT", [3 * E, 2, N], BF16)
        gw = sb("gw", [P, 11, N])
        xn = sb("xn", [P, TT, P])
        stats = sb("stats", [P, TT, 6])
        mom = sb("mom", [P, 7, TT])
        rstd = sb("rstd", [P, TT])
        rt = sb("rt", [P, 7, TT, E])
        m8 = sb("m8", [P, 5, TT])
        g3 = sb("g3", [P, TT, 3 * E])
        g3b = sb("g3b", [P, 2, TT, E], BF16)
        astats = sb("astats", [P, 3 * TT, 6])
        amom = sb("amom", [P, 7, 3 * TT])
        arstd = sb("arstd", [P, 3 * TT])

        bank = [ctx.enter_context(nc.psum_tensor(f"bank{n}", [P, N], F32)) for n in range(8)]
        side, att, att2 = bank[6], bank[7], bank[1]

        stage = gw[:, :, :].rearrange("p a n -> p (a n)")
        raw0 = stage[:, 0:3 * H0 * P]
        rawt = stage[:, 3 * H0 * P:(3 * H0 + 10) * P].rearrange("p (k c) -> p k c", c=P)
        raw_cols = stage[0:H1 + E + 1, (3 * H0 + 10) * P:(3 * H0 + 11) * P]
        PIECE, RING = 2 * N, 5
        PIECES = 2 * H1 * P // PIECE
        w1_hi_f = w1_hi[:, :, :].rearrange("p a n -> p (a n)")
        w1_lo_f = w1_lo[:, :, :].rearrange("p a n -> p (a n)")

        WHOLE = (4, 5)

        x_in = [sem(f"x_in{b}") for b in range(B)]
        const_in, spread_in, wgate_in, wt_in, late_in, rows_in, cols_in, warm = map(
            sem, ["const_in", "spread_in", "wgate_in", "wt_in", "late_in", "rows_in", "cols_in", "warm"])
        w0_in = [sem(f"w0_in{k}") for k in range(3)]
        w1_in = [sem(f"w1_in{n}") for n in range(RING)]
        stored = sem("stored")
        set_up, wt_ps, wt_hi_done, wt_done, cols_ps = map(sem, ["set_up", "wt_ps", "wt_hi_done", "wt_done", "cols_ps"])
        w0_hi_done, w0_done, w1_hi_done, w1_done, pool_set = map(
            sem, ["w0_hi_done", "w0_done", "w1_hi_done", "w1_done", "pool_set"])
        ln_stats, ln_rstd, ln_xn, xT_ps, xT_hi_done, xT_done = map(
            sem, ["ln_stats", "ln_rstd", "ln_xn", "xT_ps", "xT_hi_done", "xT_done"])
        logits_ps, rt_step, rt_exp, gT_ps, gT_done = map(sem, ["logits_ps", "rt_step", "rt_exp", "gT_ps", "gT_done"])
        f_gate, f_spread, f_up, f_silu, f_sg, f_h, f_hi, f_lo, f_down, f_y, f_yT, f_x = map(
            sem, ["f_gate", "f_spread", "f_up", "f_silu", "f_sg", "f_h", "f_hi", "f_lo", "f_down", "f_y", "f_yT", "f_x"])
        m_up, m_spread, m_silu, m_gs, m_hi, m_lo_v, m_lo_p, m_down, m_y, m_acc, m_yT, m_x = map(
            sem, ["m_up", "m_spread", "m_silu", "m_gs", "m_hi", "m_lo_v", "m_lo_p", "m_down", "m_y", "m_acc", "m_yT", "m_x"])
        a_ps, a_read, a_act, a_step, a_pool = map(sem, ["a_ps", "a_read", "a_act", "a_step", "a_pool"])

        gq, gF, gR, gk, gX0, gX1, gP, gT0, gT1, gv, gG = (gw[:, n, :] for n in range(11))
        gX, gTm = [gX0, gX1], [gT0, gT1]
        gS, gon = gk, gq
        spre = stage[:, 0:3 * TT * P].rearrange("p (t c) -> p t c", c=3 * P)
        spk = stage[:, 3 * N:5 * N].bitcast(BF16)[:, 0:3 * TT * P].rearrange("p (t c) -> p t c", c=3 * P)
        so = stage[:, 5 * N:6 * N].rearrange("p (t c) -> p t c", c=P)

        block = ctx.enter_context(nc.Block())

        def mm(dst, lhsT, rhs, start=True, stop=True):
            return nc.tensor.matmul(dst, lhsT, rhs, start=start, stop=stop)

        def mm3(dst, l_hi, l_lo, r_hi_, r_lo_, start=True, stop=True):
            mm(dst, l_hi, r_hi_, start, False)
            mm(dst, l_lo, r_hi_, False, False)
            return mm(dst, l_hi, r_lo_, False, stop)

        def wide(ap, n):
            return ap.unsqueeze(2).to_broadcast([ap.shape[0], ap.shape[1], n])

        @block.sync
        def _(sp):
            for b in range(B):
                sp.dma_start(x[:, b, :, :], a["L0_attn_x"][b].rearrange("(t p) d -> p t d", p=P)).then_inc(x_in[b], 16)
                if b == 0:
                    for k, name in enumerate(["w_g", "w_u"]):
                        sp.dma_start(raw0[:, k * H0 * P:(k + 1) * H0 * P].rearrange("p (e m) -> p e m", e=E),
                                     a["L0_ffn_" + name].rearrange("e d m -> d e m")).then_inc(w0_in[k], 16)
                    sp.dma_start(raw0[:, 2 * H0 * P:].rearrange("p (t d) -> p t d", d=P),
                                 a["L0_ffn_w_d"].rearrange("e m d -> (e m) d").rearrange("(t p) d -> p t d", p=P)
                                 ).then_inc(w0_in[2], 16)
                    sp.dma_start(rawt[:, 0:3, :], a["L0_attn_W_in"].rearrange("(k p) c -> p k c", p=P)).then_inc(wt_in, 16)
                    for k, name in enumerate(["L0_attn_W_g1", "L0_attn_W_g2", "L0_attn_W_out",
                                              "L1_attn_Wq", "L1_attn_Wk", "L1_attn_Wv", "L1_attn_Wo"]):
                        sp.dma_start(rawt[:, 3 + k, :], a[name]).then_inc(wt_in, 16)
                    sp.dma_start(raw_cols[0:H1, :], a["L1_ffn_b1"].rearrange("e (q p) -> (e q) p", p=P)).then_inc(cols_in, 16)
                    sp.dma_start(raw_cols[H1:H1 + E, :], a["L1_ffn_b2"]).then_inc(cols_in, 16)
                    sp.dma_start(raw_cols[H1 + E:H1 + E + 1, :], a["L0_attn_ln_w"].unsqueeze(0)).then_inc(cols_in, 16)
            sp.dma_start(mask[:, :, :], a["c_mask"].bitcast(BF16)).then_inc(late_in, 16)
            sp.dma_start(near_b[:, :], a["c_near"].bitcast(BF16)).then_inc(late_in, 16)
            sp.dma_start(ident_b[:, :], a["c_ident"].bitcast(BF16)).then_inc(late_in, 16)
            at = 0
            for name in ["L1_attn_bq", "L1_attn_bk", "L1_attn_bv", "L1_attn_gq", "L1_attn_gk", "L1_attn_gv",
                         "L1_attn_betaq", "L1_attn_betak", "L1_attn_betav", "L1_attn_bo", "L1_attn_go", "L1_attn_betao",
                         "L1_ffn_gate_b", "L1_attn_scale"]:
                w = int(np.prod(a[name].shape))
                sp.dma_start(rows[:, at:at + w], a[name].partition_broadcast(P)).then_inc(rows_in, 16)
                at += w
            for n in range(PIECES):
                if n < RING:
                    sp.wait_ge(w0_done, 3)
                    sp.wait_ge(wt_ps, 3)
                else:
                    sp.wait_ge(w1_done, n - RING + 1)
                    sp.wait_ge(w1_hi_done, n - RING + 1)
                dst = stage[:, (n % RING) * PIECE:(n % RING + 1) * PIECE]
                if n < PIECES // 2:
                    e = n * PIECE // M1
                    sp.dma_start(dst.rearrange("p (e h) -> p e h", h=M1),
                                 a["L1_ffn_w1"][e:e + PIECE // M1].rearrange("e d h -> d e h")).then_inc(w1_in[n % RING], 16)
                else:
                    t = (n - PIECES // 2) * PIECE
                    sp.dma_start(dst.rearrange("p (t d) -> p t d", d=P),
                                 a["L1_ffn_w2"].rearrange("e h d -> (e h) d")[t:t + PIECE].rearrange("(t p) d -> p t d", p=P)
                                 ).then_inc(w1_in[n % RING], 16)
            for b in range(B):
                sp.wait_ge(m_x, B + b + 1)
                sp.dma_start(out[b].rearrange("(t p) d -> p t d", p=P), x[:, b, :, :]).then_inc(stored, 16)
            sp.wait_ge(stored, 16 * B)

        def cut(t):
            return slice(t * P, (t + 1) * P)

        def need(eng, s, value):
            if not isinstance(value, int) or value > 0:
                eng.wait_ge(s, value)

        GLA, GLA_V, GLA_A, GLA_P = 18, 45, 5, 5
        FIRST, LAST, OWN = 5, 5 + len(LEVELS), MASKS - 1
        SELF = FIRST + OWN
        GLA_R = GLA - (LAST - SELF)
        MASKED = [*range(FIRST, SELF), LAST]

        def level_step(lv):
            return FIRST + lv + (lv >= OWN)

        def level_base(lv):
            return 4 * lv - 2 if lv else 0

        def reads_before(k):
            return k if k <= SELF else max(SELF, k - (LAST - SELF))

        SPK, SPK_V, SPK_P = TT + 4, 55, 2
        LEVEL_PIECES = [f"level {lv}" for lv in range(len(LEVELS))]
        AFTER_PIECES = [f"after {lv}" for lv in range(len(LEVELS))]
        MOM = 7

        IN_TURN = (1, 2, 3, 4, 5, *range(7, LAST + 1))

        def gla_bank(k):
            return att2 if k <= LAST and reads_before(k) % 2 else att

        def first(i):
            return isinstance(i, int) and i == 0

        def last_run(i):
            return isinstance(i, int) and i == CALLS - 1

        def back(t, ring):
            if t >= ring:
                return ring
            return H0 + t - max(u for u in range(H0) if u % ring == t)

        def gla_tensor(pe, g, k):
            pe.wait_ge(a_read, g * GLA_R + reads_before(k) + (1 if k not in IN_TURN else 0))
            att = gla_bank(k)
            if k == 0:
                pe.wait_ge(xT_done, 2 * g + 4)
                last = mm3(att[:, :], wt_hi[:, 1, :], wt_lo[:, 1, :], zT_hi[:, :], zT_lo[:, :])
            elif k == 1:
                last = mm3(att[:, :], wt_hi[:, 2, :], wt_lo[:, 2, :], zT_hi[:, :], zT_lo[:, :])
            elif k == 2:
                last = mm3(att[:, :], wt_hi[:, 3, :], wt_lo[:, 3, :], zT_hi[:, :], zT_lo[:, :])
            elif k == 3:
                for t in range(TT):
                    last = mm3(att[:, cut(t)], zT_hi[:, cut(t)], zT_lo[:, cut(t)], wt_hi[:, 0, :], wt_lo[:, 0, :])
            elif k == 4:
                for t in range(TT):
                    last = mm(att[:, cut(t)], gG[:, cut(t)], wt_all[:, 0, :])
            elif k <= LAST and k != SELF:
                lv = k - FIRST - (k > SELF)
                pe.wait_ge(a_step, 1 + g * GLA_V + level_base(lv) + (2 if lv else 1))
                xl, h = gX[lv % 2], LEVELS[lv]
                for t in range(TT):
                    if k < SELF:
                        last = mm(att[:, cut(t)], xl[:, cut(t)], xl[:, cut(t)])
                        continue
                    for q in range(h, P, 2 * h):
                        last = mm(att[0:q, t * P + q:t * P + q + h], xl[:, t * P:t * P + q],
                                  xl[:, t * P + q:t * P + q + h])
            elif k == SELF:
                for t in range(TT):
                    last = mm(att[:, cut(t)], gk[:, cut(t)], gq[:, cut(t)])
            elif k == 13:
                pe.wait_ge(a_step, 1 + g * GLA_V + 27)
                for t in range(TT):
                    last = nc.tensor.transpose(att[:, cut(t)], gX1[:, cut(t)], ident[:, :])
            elif k == 14:
                for t in range(TT - 1):
                    last = mm(att[:, cut(t)], gT0[:, cut(t)], gv[:, cut(t)])
            elif k == 15:
                pe.wait_ge(a_step, 1 + g * GLA_V + 30)
                pe.wait_ge(a_pool, 1 + g * GLA_P + 4)
                for t in range(TT):
                    last = mm(att[:, cut(t)], gP[:, cut(t)], gv[:, cut(t)], True, t == 0)
                    if t:
                        last = mm(att[:, cut(t)], gX0[:, cut(t)], gS[:, cut(t - 1)], False, True)
            elif k == 16:
                pe.wait_ge(a_step, 1 + g * GLA_V + 45)
                for t in range(TT):
                    last = nc.tensor.transpose(att[:, cut(t)], gon[:, cut(t)], ident[:, :])
            else:
                for t in range(TT):
                    last = mm(att[:, cut(t)], gG[:, cut(t)], wt_all[:, 1, :])
            last.then_inc(a_ps, 1)

        def spike_tensor(pe, s, k):
            pe.wait_ge(a_read, B * GLA_R + s * SPK + k + 1)
            v0 = 1 + B * GLA_V + s * SPK_V
            if k < TT:
                if k == 0:
                    pe.wait_ge(xT_done, 2 * s + 17)
                w = wt_hi[:, 6:9, :].rearrange("p a n -> p (a n)"), wt_lo[:, 6:9, :].rearrange("p a n -> p (a n)")
                last = mm3(att[:, 0:3 * P], zT_hi[:, cut(k)], zT_lo[:, cut(k)], *w)
            elif k == TT:
                pe.wait_ge(a_step, v0 + 37)
                for t in range(TT):
                    last = mm(att[:, 0:P], spk[:, t, P:2 * P], spk[:, t, 2 * P:3 * P], t == 0, t == TT - 1)
            elif k == TT + 1:
                for t in range(TT):
                    last = mm(att[:, cut(t)], spk[:, t, 0:P], ident_b[:, :])
            elif k == TT + 2:
                last = mm(att[:, :], r_lo[:, :], r_hi[:, :], True, False)
                for t in range(TT):
                    u = N - P - t * P
                    last = mm(att[:, :], spk[:, t, 2 * P:3 * P], near_b[:, u:u + N], False, t == TT - 1)
            else:
                for t in range(TT):
                    mm(att[:, cut(t)], r_hi[:, cut(t)], wt_hi[:, 9, :], True, False)
                    last = mm(att[:, cut(t)], r_hi[:, cut(t)], wt_lo[:, 9, :], False, True)
            last.then_inc(a_ps, 1)

        def gla_scalar(act, g, k):
            att = gla_bank(k) if k in range(GLA) else None
            if k in (0, 1, 2, 3, 4, 13, 16):
                act.wait_ge(a_ps, 1 + g * GLA + k + 1)
            if k == 0:
                nc.scalar.activation(gq, att[:, :], ACT.Silu).then_inc(a_read, 1)
            elif k == 1:
                r, c = g * GLA_R + 1, g * GLA_A
                nc.scalar.activation(gF, att[:, :], ACT.Tanh, scale=0.5).then_inc(a_read, 1)
                act.wait_ge(a_read, r + 2)
                (fe, fo), (re, ro), (xe, _) = halves(gF, 1), halves(gR, 1), halves(gX0, 1)
                nc.scalar.activation(xe, fe, ACT.Copy, scale=-0.5, bias=0.5).then_inc(a_act, 1)
                nc.scalar.activation(re, fo, ACT.Copy, scale=0.5, bias=0.5).then_inc(a_act, 1)
                nc.scalar.activation(gk, gF, ACT.Copy, scale=-0.5, bias=0.5).then_inc(a_act, 1)
                nc.scalar.activation(ro, fo, ACT.Copy, scale=0.0, bias=1.0).then_inc(a_act, 1)
                act.wait_ge(a_act, c + 4)
                nc.scalar.activation(gF, gF, ACT.Copy, scale=0.5, bias=0.5).then_inc(a_act, 1)
            elif k == 2:
                nc.scalar.activation(gG, att[:, :], ACT.Copy).then_inc(a_read, 1)
            elif k == 3:
                nc.scalar.activation(gv, att[:, :], ACT.Copy).then_inc(a_read, 1)
            elif k == 4:
                nc.scalar.activation(gG, att[:, :], ACT.Tanh, scale=0.5).then_inc(a_read, 1)
            elif k == 13:
                act.wait_ge(a_pool, 1 + g * GLA_P + 3)
                nc.scalar.activation(gT0, att[:, :], ACT.Copy).then_inc(a_read, 1)
            elif k == 16:
                nc.scalar.activation(gG, att[:, :], ACT.Copy, scale=cols[:, H1 + E:H1 + E + 1]).then_inc(a_read, 1)

        def spike_scalar(act, s, k):
            if k == TT + 1:
                act.wait_ge(a_ps, 1 + B * GLA + s * SPK + k + 1)
                nc.scalar.activation(r_hi[:, :], att[:, :], ACT.Copy).then_inc(a_read, 1)

        def gla_gpsimd(pool, g, k):
            v0, p0 = 1 + g * GLA_V, 1 + g * GLA_P
            if k in MASKED[1:]:
                n = MASKED.index(k)
                pool.wait_ge(a_read, g * GLA_R + reads_before(k) + 2)
                need(pool, a_pool, p0 + n - 1)
                nc.gpsimd.tensor_tensor(gP, gP, gTm[(n + 1) % 2], ALU.add).then_inc(a_pool, 1)
            elif k == "moments":
                pool.wait_ge(a_step, v0 + 41)
                nc.gpsimd.tensor_tensor(arstd[:, 0:TT], amom[:, 6, 0:TT], neg_half12[:, 0:TT], ALU.pow).then_inc(a_pool, 1)

        def spike_gpsimd(pool, s, k):
            for at, w, v in (("moments", 3 * TT, 19), ("moments 2", TT, 48)):
                if k == at:
                    pool.wait_ge(a_step, 1 + B * GLA_V + s * SPK_V + v)
                    nc.gpsimd.tensor_tensor(arstd[:, 0:w], amom[:, 6, 0:w], neg_half12[:, 0:w], ALU.pow).then_inc(a_pool, 1)

        def moments(dve, k, s, base, st, mom, w, eps):
            me, mo, qe, qo = st[:, 0:w, 1], st[:, 0:w, 4], st[:, 0:w, 2], st[:, 0:w, 5]
            total, diff, sq, mean, diff2, v, out_ = (mom[:, q, 0:w] for q in range(MOM))
            V = nc.vector
            dve.wait_ge(s, base + w + (0, 0, 0, 1, 2, 5, 6)[k])
            if k == 0:
                V.tensor_tensor(total, me, mo, ALU.add).then_inc(s, 1)
            elif k == 1:
                V.tensor_tensor(diff, me, mo, ALU.subtract).then_inc(s, 1)
            elif k == 2:
                V.tensor_tensor(sq, qe, qo, ALU.add).then_inc(s, 1)
            elif k == 3:
                V.tensor_scalar(mean, total, 0.5, None, ALU.mult).then_inc(s, 1)
            elif k == 4:
                V.tensor_tensor(diff2, diff, diff, ALU.mult).then_inc(s, 1)
            elif k == 5:
                V.scalar_tensor_tensor(out=v, in0=diff2, scalar=P / 4.0, in1=sq, op0=ALU.mult, op1=ALU.add).then_inc(s, 1)
            else:
                V.tensor_scalar(out_, v, 1.0 / P, eps, ALU.mult, ALU.add).then_inc(s, 1)

        def halves(ap, h):
            v = ap.rearrange("p (s two h) -> p s two h", two=2, h=h)
            return v[:, :, 0, :], v[:, :, 1, :]

        def last_of(ap, h):
            return ap[:, :, h - 1:h].to_broadcast([P, N // (2 * h), h])

        def gla_level(dve, g, lv, after):
            v0, h = 1 + g * GLA_V + level_base(lv), LEVELS[lv]
            (xe, xo), (ke, _), (_, qo) = halves(gX[lv % 2], h), halves(gk, h), halves(gq, h)
            (re, _), (fe, fo) = halves(gR, h), halves(gF, h)
            if not after:
                need(dve, a_step, v0)
                if lv == 0:
                    dve.wait_ge(a_act, g * GLA_A + 5)
                else:
                    need(dve, a_ps, 1 + g * GLA + (0 if lv < 2 else level_step(lv - 2) + 1))
                    nc.vector.tensor_tensor(xe, ke, re, ALU.mult).then_inc(a_step, 1)
                nc.vector.tensor_tensor(xo, qo, fo, ALU.mult).then_inc(a_step, 1)
            else:
                if lv > 0:
                    dve.wait_ge(a_step, v0 + 1)
                    nc.vector.tensor_tensor(re, re, last_of(fo, h), ALU.mult).then_inc(a_step, 1)
                dve.wait_ge(a_step, v0 + (3 if lv else 1))
                nc.vector.tensor_tensor(fo, fo, last_of(fe, h), ALU.mult).then_inc(a_step, 1)

        def gla_vector(dve, g, k, bx):
            v0, p0, r0 = 1 + g * GLA_V, 1 + g * GLA_P, g * GLA_R + 1
            att = gla_bank(k) if k in range(GLA) else None
            if k in LEVEL_PIECES or k in AFTER_PIECES:
                after = k in AFTER_PIECES
                gla_level(dve, g, (AFTER_PIECES if after else LEVEL_PIECES).index(k), after)
            elif k in MASKED:
                n = MASKED.index(k)
                dve.wait_ge(a_ps, 1 + g * GLA + k + 1)
                src = att[:, :].rearrange("p (t c) -> p t c", c=P)
                m = mask[:, n, :].unsqueeze(1).to_broadcast([P, TT, P])
                if n > 2:
                    dve.wait_ge(a_pool, p0 + n - 2)
                if n == 0:
                    need(dve, a_pool, p0)
                dst = gP if n == 0 else gTm[(n + 1) % 2]
                nc.vector.tensor_tensor(dst.rearrange("p (t c) -> p t c", c=P), src, m, ALU.mult).then_inc(a_read, 1)
            elif k == "decay":
                dve.wait_ge(a_step, v0 + 26)
                dve.wait_ge(a_ps, 1 + g * GLA + LAST + 1)
                nc.vector.tensor_tensor(gX1, gk, gR, ALU.mult).then_inc(a_step, 1)
                nc.vector.tensor_tensor(gX0, gq, gF, ALU.mult).then_inc(a_step, 1)
            elif k == 14:
                dve.wait_ge(a_ps, 1 + g * GLA + k + 1)
                dve.wait_ge(a_step, v0 + 28)
                nc.vector.tensor_copy(gS[:, cut(0)], att[:, cut(0)]).then_inc(a_step, 1)
                for t in range(1, TT - 1):
                    dve.wait_ge(a_step, v0 + 28 + t)
                    nc.vector.scalar_tensor_tensor(
                        out=gS[:, cut(t)], in0=gS[:, cut(t - 1)], scalar=gF[:, (t + 1) * P - 1:(t + 1) * P],
                        in1=att[:, cut(t)], op0=ALU.mult, op1=ALU.add).then_inc(a_step if t < TT - 2 else a_read, 1)
            elif k == 15:
                dve.wait_ge(a_ps, 1 + g * GLA + k + 1)
                dve.wait_ge(a_pool, p0 + 4)
                nc.vector.scalar_tensor_tensor(out=gT1, in0=gG, scalar=1.0, in1=att[:, :],
                                               op0=ALU.add, op1=ALU.mult).then_inc(a_read, 1)
                dve.wait_ge(a_read, r0 + reads_before(k) + 1)
                dve.wait_ge(a_step, v0 + 30)
                for t in range(TT):
                    nc.vector.bn_stats(astats[:, t, :], gT1[:, cut(t)]).then_inc(a_step, 1)
            elif k == "norm":
                dve.wait_ge(a_pool, p0 + 5)
                for t in range(TT):
                    nc.vector.tensor_scalar(gon[:, cut(t)], gT1[:, cut(t)], amom[:, 3, t:t + 1], arstd[:, t:t + 1],
                                            ALU.subtract, ALU.mult).then_inc(a_step, 1)
            elif k == 17:
                dve.wait_ge(a_ps, 1 + g * GLA + k + 1)
                xb = x[:, bx, :, :].rearrange("p t d -> p (t d)")
                nc.vector.tensor_tensor(xb, att[:, :], xb, ALU.add).then_inc(a_read, 1)

        def spike_vector(dve, s, k, bx):
            v0, p0 = 1 + B * GLA_V + s * SPK_V, 1 + B * GLA_P + s * SPK_P
            r0, s0 = B * GLA_R + s * SPK + 1, B * GLA + s * SPK + 1

            def row(at, w):
                return rows[:, at:at + w].unsqueeze(1).to_broadcast([P, TT, w])

            if k in range(SPK):
                dve.wait_ge(a_ps, s0 + k + 1)
            if k in range(TT):
                if k == 0:
                    dve.wait_ge(a_step, v0)
                nc.vector.tensor_tensor(spre[:, k, :], att[:, 0:3 * P], rows[:, R_BIAS:R_BIAS + 3 * P],
                                        ALU.add).then_inc(a_read, 1)
                dve.wait_ge(a_read, r0 + k + 1)
                for c in range(3):
                    nc.vector.bn_stats(astats[:, 3 * k + c, :], spre[:, k, cut(c)]).then_inc(a_step, 1)
            elif k in ("norm 0", "norm 1"):
                if k == "norm 0":
                    dve.wait_ge(a_pool, p0 + 1)
                for t in (0, 1) if k == "norm 0" else (2, 3):
                    for c in range(3):
                        n = 3 * t + c
                        nc.vector.tensor_scalar(spre[:, t, cut(c)], spre[:, t, cut(c)], amom[:, 3, n:n + 1],
                                                arstd[:, n:n + 1], ALU.subtract, ALU.mult).then_inc(a_step, 1)
            elif k in ("scale 0", "scale 1", "shift 0", "shift 1"):
                at = int(k[-1])
                op, half = k[:-2], spre[:, 2 * at:2 * at + 2, :]
                r = R_G if op == "scale" else R_BETA
                dve.wait_ge(a_step, v0 + (31 if op == "scale" else 32 + at))
                nc.vector.tensor_tensor(half, half, row(r, 3 * P)[:, 0:2, :],
                                        ALU.mult if op == "scale" else ALU.add).then_inc(a_step, 1)
            elif k == "spikes":
                dve.wait_ge(a_step, v0 + 35)
                nc.vector.tensor_scalar(spk[:, :, 0:2 * P], spre[:, :, 0:2 * P], 1.0, 0.5,
                                        ALU.is_ge, ALU.subtract).then_inc(a_step, 1)
                nc.vector.tensor_scalar(spk[:, :, 2 * P:3 * P], spre[:, :, 2 * P:3 * P], 1.0, None,
                                        ALU.is_ge).then_inc(a_step, 1)
            elif k == TT:
                nc.vector.tensor_tensor(r_lo[:, :], att[:, 0:P], head2, ALU.mult).then_inc(a_read, 1)
            elif k == TT + 2:
                nc.vector.tensor_scalar(r_hi[:, :], att[:, :], rows[:, R_SC:R_SC + 1], 0.5,
                                        ALU.mult, ALU.is_ge).then_inc(a_read, 1)
            elif k == TT + 3:
                nc.vector.tensor_tensor(so, att[:, :].rearrange("p (t c) -> p t c", c=P), row(R_BO, P),
                                        ALU.add).then_inc(a_read, 1)
                dve.wait_ge(a_read, r0 + k + 1)
                dve.wait_ge(a_step, v0 + 37)
                for t in range(TT):
                    nc.vector.bn_stats(astats[:, t, :], so[:, t, :]).then_inc(a_step, 1)
            elif k == "norm 2":
                dve.wait_ge(a_pool, p0 + 2)
                for t in range(TT):
                    nc.vector.tensor_scalar(so[:, t, :], so[:, t, :], amom[:, 3, t:t + 1], arstd[:, t:t + 1],
                                            ALU.subtract, ALU.mult).then_inc(a_step, 1)
            elif k == "scale 2":
                dve.wait_ge(a_step, v0 + 52)
                nc.vector.tensor_tensor(so, so, row(R_GO, P), ALU.mult).then_inc(a_step, 1)
            elif k == "shift 2":
                dve.wait_ge(a_step, v0 + 53)
                nc.vector.tensor_tensor(so, so, row(R_BETAO, P), ALU.add).then_inc(a_step, 1)
            elif k == "spikes 2":
                dve.wait_ge(a_step, v0 + 54)
                nc.vector.scalar_tensor_tensor(out=x[:, bx, :, :], in0=so, scalar=1.0, in1=x[:, bx, :, :],
                                               op0=ALU.is_ge, op1=ALU.add).then_inc(a_step, 1)

        def norm_vector(dve, n, b, part, par=None):
            if part == "stats":
                need(dve, ln_stats, (TT + MOM) * n)
                need(dve, ln_xn, TT * n)
                dve.nop(nofuse=True)
                for t in range(TT):
                    nc.vector.bn_stats(stats[:, t, :], x[:, b, t, :]).then_inc(ln_stats, 1)
            elif part == "norm":
                dve.wait_ge(ln_rstd, n + 1)
                need(dve, xT_ps, n)
                for t in range(TT):
                    nc.vector.tensor_scalar(xn[:, t, :], x[:, b, t, :], mom[:, 3, t:t + 1], rstd[:, t:t + 1],
                                            ALU.subtract, ALU.mult).then_inc(ln_xn, 1)
            else:
                dve.wait_ge(xT_hi_done, n + 1)
                hi, lo = (zT_hi[:, :], zT_lo[:, :]) if par is None else (xT_hi[:, par, :], xT_lo[:, par, :])
                nc.vector.tensor_tensor(lo, side[:, :], hi.bitcast(F32), ALU.subtract).then_inc(xT_done, 1)

        def norm_moments(dve, n, k):
            moments(dve, k, ln_stats, (TT + MOM) * n, stats, mom, TT, EPS)

        def gla_moments(dve, g, k):
            moments(dve, k, a_step, 1 + g * GLA_V + 30, astats, amom, TT, 4 * EPS)

        def spike_moments(dve, s, k, second):
            moments(dve, k, a_step, 1 + B * GLA_V + s * SPK_V + (37 if second else 0), astats, amom,
                    TT if second else 3 * TT, EPS)

        def norm_gpsimd(pool, n):
            pool.wait_ge(ln_stats, (TT + MOM) * (n + 1))
            nc.gpsimd.tensor_tensor(rstd[:, :], mom[:, 6, :], neg_half, ALU.pow).then_inc(ln_rstd, 1)

        def norm_tensor(pe, n, r, m=None):
            pe.wait_ge(ln_xn, TT * n + TT)
            need(pe, xT_done, n)
            if m is None:
                need(pe, gT_done, r)
            else:
                pe.wait_ge(rt_step, rt_base(r, m) + 1)
            for t in range(TT):
                last = nc.tensor.transpose(side[:, cut(t)], xn[:, t, :], ident[:, :])
            last.then_inc(xT_ps, 1)

        def norm_scalar(act, n, par=None):
            act.wait_ge(xT_ps, n + 1)
            hi = zT_hi[:, :] if par is None else xT_hi[:, par, :]
            nc.scalar.activation(hi, side[:, :], ACT.Copy).then_inc(xT_hi_done, 1)

        PICK = ["logits", "best", "shifted", "best's places", "their ranks", "highest rank", "pick", "rest",
                "second", "second's places", "their ranks", "highest rank", "pick 2", "both picks"]
        GATE = (["picked", "sum", "inverse", "gates"],
                ["sum of all", "inverse", "probabilities", "picked", "sum", "guard", "inverse", "gates"])
        SPLIT = ["part 0", "part 0 out", "less 0", "part 1", "part 1 out", "less 1"]
        ROUTER = [PICK + GATE[m] + SPLIT for m in (0, 1)]
        RT = [len(ROUTER[m]) for m in (0, 1)]

        def rt_base(r, m):
            return r * RT[0] if m == 0 else CALLS * RT[0] + (r - CALLS) * RT[1]

        def router_tensor(pe, n, r, m, par, part):
            if part == "logits":
                pe.wait_ge(xT_done, n + 1)
                for t in range(TT):
                    last = mm3(side[:, t * E:(t + 1) * E], xT_hi[:, par, cut(t)], xT_lo[:, par, cut(t)],
                               wgate_hi[:, m, :], wgate_lo[:, m, :])
                last.then_inc(logits_ps, 1)
            else:
                pe.wait_ge(rt_step, rt_base(r, m) + RT[m])
                pe.wait_ge(xT_done, n + 1)
                for t in range(TT):
                    last = nc.tensor.transpose(side[0:3 * E, cut(t)], g3[:, t, :], ident[:, :])
                last.then_inc(gT_ps, 1)

        def router_scalar(act, r, par):
            act.wait_ge(gT_ps, r + 1)
            nc.scalar.activation(gT[:, par, :], side[0:3 * E, :], ACT.Copy).then_inc(gT_done, 1)

        def router_gpsimd(pool, r, m, t):
            pool.wait_ge(rt_step, rt_base(r, m) + 3)
            nc.gpsimd.tensor_tensor(rt[:, 1, t, :], base_e[:, t, :], rt[:, 1, t, :], ALU.pow).then_inc(rt_exp, 1)

        def router_vector(dve, r, m, k):
            logit, ex, eq, pick, rest, pick2, gate = (rt[:, q, :, :] for q in range(7))
            best, key, second, total, inv = (m8[:, q, :] for q in range(5))
            V, base, step = nc.vector, rt_base(r, m), ROUTER[m][k]
            need(dve, rt_step, base + k)
            values, value, one_hot = (logit, best, pick) if k < 8 else (rest, second, pick2)
            if step == "logits":
                dve.wait_ge(logits_ps, r + 1)
                sums = side[:, 0:TT * E].rearrange("p (t e) -> p t e", e=E)
                if m == 0:
                    ins = V.tensor_copy(logit, sums)
                else:
                    ins = V.tensor_tensor(logit, sums, rows[:, R_GB:R_GB + E].unsqueeze(1).to_broadcast([P, TT, E]), ALU.add)
            elif step == "best":
                ins = V.reduce_max(best, logit, axis=AX.X)
            elif step == "shifted":
                ins = V.tensor_tensor(ex, logit, wide(best, E), ALU.subtract)
            elif step in ("best's places", "second's places"):
                ins = V.tensor_tensor(eq, values, wide(value, E), ALU.is_equal)
            elif step == "their ranks":
                ins = V.tensor_tensor(eq, eq, rank[:, :, :], ALU.mult)
            elif step == "highest rank":
                ins = V.reduce_max(key, eq, axis=AX.X)
            elif step in ("pick", "pick 2"):
                ins = V.tensor_tensor(one_hot, eq, wide(key, E), ALU.is_equal)
            elif step == "rest":
                ins = V.scalar_tensor_tensor(out=rest, in0=pick, scalar=-3e38, in1=logit, op0=ALU.mult, op1=ALU.add)
            elif step == "second":
                ins = V.reduce_max(second, rest, axis=AX.X)
            elif step == "both picks":
                ins = V.tensor_tensor(pick, pick, pick2, ALU.add)
            elif step == "sum of all":
                dve.wait_ge(rt_exp, TT * (r + 1))
                ins = V.reduce_sum(total, ex, axis=AX.X)
            elif step == "probabilities":
                ins = V.tensor_tensor(ex, ex, wide(inv, E), ALU.mult)
            elif step == "picked":
                if m == 0:
                    dve.wait_ge(rt_exp, TT * (r + 1))
                ins = V.tensor_tensor(gate, ex, pick, ALU.mult)
            elif step == "sum":
                ins = V.reduce_sum(total, gate, axis=AX.X)
            elif step == "guard":
                ins = V.tensor_scalar(total, total, 1e-9, None, ALU.max)
            elif step == "inverse":
                ins = V.reciprocal(inv, total)
            elif step == "gates":
                ins = V.tensor_tensor(gate, gate, wide(inv, E), ALU.mult)
            elif step == "part 0":
                ins = V.tensor_copy(g3b[:, 0, :, :], gate)
            elif step == "part 0 out":
                ins = V.tensor_copy(g3[:, :, 0:E], g3b[:, 0, :, :])
            elif step == "less 0":
                ins = V.tensor_tensor(gate, gate, g3[:, :, 0:E], ALU.subtract)
            elif step == "part 1":
                ins = V.tensor_copy(g3b[:, 1, :, :], gate)
            elif step == "part 1 out":
                ins = V.tensor_copy(g3[:, :, E:2 * E], g3b[:, 1, :, :])
            else:
                ins = V.tensor_tensor(g3[:, :, 2 * E:3 * E], gate, g3[:, :, E:2 * E], ALU.subtract)
            ins.then_inc(rt_step, 1)

        Z_AT = ({"stats": 14, "rstd": 19, "norm": 22, "turn": 24, "split": 24},
                {"stats": 36, "rstd": 42, "norm": 42, "turn": 52, "split": 55})
        R_AT = ({"stats": 0, "rstd": 6, "norm": 7, "turn": 10, "split": 10, "logits": 13, "exp 0": 15, "exp 1": 17,
                 "exp 2": 18, "exp 3": 20, "spread": 30},
                {"stats": 0, "rstd": 4, "norm": 7, "turn": 15, "split": 14, "logits": 22, "exp 0": 35, "exp 1": 38,
                 "exp 2": 44, "exp 3": 44, "spread": 62})
        GLA_PE = dict(zip([0, 1, 2, 4, 6, 7, 8, 10, 13, 15, 16, 17, 18, 21, 22, 25, 30, 31], range(GLA)))
        GLA_DVE = {3: ["level 0", "after 0"], 4: ["level 1"], 5: ["after 1"], 7: [5, "level 2"], 8: ["after 2"],
                   9: [6, "level 3"], 11: ["after 3", 7, "level 4"], 12: ["after 4"], 13: [8, "level 5"],
                   14: ["after 5"], 16: ["level 6"], 17: ["after 6"], 18: [LAST], 19: ["decay"], 23: [14], 24: [15],
                   27: ["moments", "norm"], 31: [17]}
        SPK_PE = dict(zip([0, 4, 8, 13, 37, 40, 43, 47], range(SPK)))
        SPK_DVE = {0: [0], 5: [1], 10: [2], 13: [3], 19: ["moments"], 20: ["norm 0"], 22: ["norm 1"],
                   23: ["scale 0"], 25: ["scale 1"], 27: ["shift 0"], 28: ["shift 1"], 30: ["spikes"], 35: [4],
                   41: [6], 45: [7], 53: ["moments 2"], 55: ["norm 2", "scale 2"], 56: ["shift 2"], 59: ["spikes 2"]}
        STEPS_AT = ({"Z moments": (20, 1, 0, MOM), "R moments": (2, 1, 0, MOM), "pick": (18, 1, 0, len(PICK)),
                     "gate": (32, 2, len(PICK), len(GATE[0] + SPLIT)), "attention": (33, 3, 0, MOM)},
                    {"Z moments": (77, 1, 0, MOM), "R moments": (2, 1, 0, MOM), "pick": (45, 1, 0, len(PICK)),
                     "gate": (96, 1, len(PICK), len(GATE[1] + SPLIT)), "attention": (33, 2, 0, MOM),
                     "attention 2": (94, 1, 0, MOM)})

        def due(m, what, point):
            at, each, first_step, count = STEPS_AT[m][what]
            return range(first_step + min(count, max(0, point - at) * each),
                         first_step + min(count, max(0, point - at + 1) * each))

        W1_AT = ({4: 0, 11: 1, 15: 2, 20: 3, 25: 4, 30: 5}, {15: 6, 26: 7})

        def w1_pieces(i):
            return W1_AT[i] if i < len(W1_AT) else {}

        def side_job(m, i, par, attention):
            r = i + 1 + m * CALLS
            if attention or first(i - 1):
                n, zn = 2 * i + 13 * m, 2 * i + 13 * m + 1
            else:
                n, zn = i + (1 if i < 1 else 6) + 13 * m, None
            return n, zn, r, (i + 1) % B, (i + B - 1) % B, par

        def router_mixture(m, i):
            return 1 if m == 1 or last_run(i) else 0

        def side_tensor(pe, m, i, slot, par_now, attention):
            n, zn, r, b, zb, par = side_job(m, i, 1 - par_now, attention)
            if zn is not None and slot == Z_AT[m]["turn"]:
                norm_tensor(pe, zn, r, router_mixture(m, i))
            if attention:
                if m == 0 and slot in GLA_PE:
                    gla_tensor(pe, i - 2, GLA_PE[slot])
                if m == 1 and slot in SPK_PE:
                    spike_tensor(pe, i - 2, SPK_PE[slot])
            if m == 0 or not last_run(i):
                at, to = R_AT[m], router_mixture(m, i)
                if slot == at["turn"]:
                    norm_tensor(pe, n, r)
                if slot == at["logits"]:
                    router_tensor(pe, n, r, to, par, "logits")
                if slot == at["spread"]:
                    router_tensor(pe, n if zn is None else zn, r, to, par, "gates")

        def side_scalar(act, m, i, slot, par_now, attention):
            n, zn, r, b, zb, par = side_job(m, i, 1 - par_now, attention)
            if zn is not None and slot == Z_AT[m]["turn"]:
                norm_scalar(act, zn)
            if attention:
                if m == 0 and slot in GLA_PE:
                    gla_scalar(act, i - 2, GLA_PE[slot])
                if m == 1 and slot in SPK_PE:
                    spike_scalar(act, i - 2, SPK_PE[slot])
            if m == 0 and not attention and slot in w1_pieces(i):
                k = w1_pieces(i)[slot]
                piece = slice(k * PIECE, (k + 1) * PIECE)
                act.wait_ge(w1_in[k % RING], 16 * (k // RING + 1))
                nc.scalar.activation(w1_hi_f[:, piece], stage[:, (k % RING) * PIECE:(k % RING + 1) * PIECE],
                                     ACT.Copy).then_inc(w1_hi_done, 1)
            if m == 0 or not last_run(i):
                if slot == R_AT[m]["turn"]:
                    norm_scalar(act, n, par)
                if slot == R_AT[m]["spread"]:
                    router_scalar(act, r, par)

        def side_vector(dve, m, i, slot, par_now, attention):
            n, zn, r, b, zb, par = side_job(m, i, 1 - par_now, attention)
            if zn is not None:
                for part in ("stats", "norm", "split"):
                    if slot == Z_AT[m][part]:
                        if part == "stats":
                            dve.wait_ge(m_x if m else f_x, i)
                        norm_vector(dve, zn, zb, part)
            if attention:
                for part in (GLA_DVE, SPK_DVE)[m].get(slot, []):
                    (gla_vector, spike_vector)[m](dve, i - 2, part, i - 2)
            if m == 0 and not attention and slot in w1_pieces(i):
                k = w1_pieces(i)[slot]
                piece = slice(k * PIECE, (k + 1) * PIECE)
                dve.wait_ge(w1_hi_done, k + 1)
                nc.vector.tensor_tensor(w1_lo_f[:, piece], stage[:, (k % RING) * PIECE:(k % RING + 1) * PIECE],
                                        w1_hi_f[:, piece].bitcast(F32), ALU.subtract).then_inc(w1_done, 1)
            if m == 0 or not last_run(i):
                if slot == R_AT[m]["stats"]:
                    if attention:
                        if m == 0:
                            dve.wait_ge(a_read, (i - 2) * GLA_R + 1)
                        else:
                            dve.wait_ge(a_step, 1 + B * GLA_V + (i - 2) * SPK_V)
                    elif last_run(i):
                        dve.wait_ge(f_x, i - 1)
                    elif i > 1:
                        dve.wait_ge(a_read, B * GLA_R + 1) if m == 0 else dve.wait_ge(a_step, 1 + B * (GLA_V + SPK_V))
                for part in ("stats", "norm", "split"):
                    if slot == R_AT[m][part]:
                        norm_vector(dve, n, b, part, par)

        def small_vector(dve, m, i, point, par_now, attention):
            n, zn, r, b, zb, par = side_job(m, i, 1 - par_now, attention)
            if zn is not None:
                for k in due(m, "Z moments", point):
                    norm_moments(dve, zn, k)
            if attention:
                for k in due(m, "attention", point):
                    if m == 0:
                        gla_moments(dve, i - 2, k)
                    else:
                        spike_moments(dve, i - 2, k, False)
                if m == 1:
                    for k in due(m, "attention 2", point):
                        spike_moments(dve, i - 2, k, True)
            if m == 0 or not last_run(i):
                for k in due(m, "R moments", point):
                    norm_moments(dve, n, k)
                for k in due(m, "pick", point):
                    router_vector(dve, r, router_mixture(m, i), k)
                to = router_mixture(m, i)
                for k in due(m, "gate", point):
                    router_vector(dve, r, to, k)
                at, each, _, count = STEPS_AT[m]["gate"]
                if to != m and point == at + (count - 1) // each:
                    for k in range(RT[m], RT[to]):
                        router_vector(dve, r, to, k)

        def side_gpsimd(pool, m, i, slot, par_now, attention):
            n, zn, r, b, zb, par = side_job(m, i, 1 - par_now, attention)
            if zn is not None and slot == Z_AT[m]["rstd"]:
                norm_gpsimd(pool, zn)
            if attention:
                for part in (GLA_DVE, SPK_DVE)[m].get(slot, []):
                    (gla_gpsimd, spike_gpsimd)[m](pool, i - 2, part)
            if m == 0 or not last_run(i):
                if slot == R_AT[m]["rstd"]:
                    norm_gpsimd(pool, n)
                for t in range(TT):
                    if slot == R_AT[m][f"exp {t}"]:
                        router_gpsimd(pool, r, router_mixture(m, i), t)

        G0, U0, S0, Y0 = 0, (2, 3), 4, 5
        s_buf, sg_buf, h_buf = fw[:, 0:2, :], fw[:, 2, :], fw[:, 3:7, :]

        def mix0_down(pe, T, td, i):
            pe.wait_ge(f_hi, T + 1)
            pe.wait_ge(f_lo, T + 1)
            if td == 0:
                need(pe, f_yT, i)
            mm3(bank[Y0][:, :], w0_hi[:, 2 * H0 + td, :], w0_lo[:, 2 * H0 + td, :], h_hi[:, td % 4, :], h_lo[:, td % 4, :],
                td == 0, td == H0 - 1).then_inc(f_down, 1)

        def mix0_turn(pe, i):
            pe.wait_ge(f_yT, i)
            for t in range(TT):
                last = nc.tensor.transpose(bank[S0][:, cut(t)], acc[:, cut(t)], ident[:, :])
            last.then_inc(f_y, 1)

        def mix0_tensor(pe, i, par, t, attention):
            T = H0 * i + t
            xh, xl = xT_hi[:, par, :], xT_lo[:, par, :]
            if t == 0:
                pe.wait_ge(gT_done, i + 1)
            need(pe, f_silu, T)
            mm3(bank[G0][:, :], w0_hi[:, t, :], w0_lo[:, t, :], xh, xl).then_inc(f_gate, 1)
            side_tensor(pe, 0, i, 3 * t, par, attention)
            need(pe, f_sg, T)
            if t == 4:
                need(pe, f_x, i)
            mm(bank[S0][:, :], spread_b[:, cut(t)], gT[:, par, :]).then_inc(f_spread, 1)
            need(pe, f_h, T - back(t, 2) + 1)
            mm3(bank[U0[t % 2]][:, :], w0_hi[:, H0 + t, :], w0_lo[:, H0 + t, :], xh, xl).then_inc(f_up, 1)
            side_tensor(pe, 0, i, 3 * t + 1, par, attention)
            if t == 3 and not first(i):
                pe.wait_ge(f_sg, T + 1)
                mix0_turn(pe, i)
            if t >= 3 or not first(i):
                mix0_down(pe, T - 3, (t - 3) % H0, i)
            side_tensor(pe, 0, i, 3 * t + 2, par, attention)
            if first(i - 1) and t == H0 - 1:
                pe.wait_ge(w1_done, PIECES)

        def mix0_hi(act, T, th):
            act.wait_ge(f_h, T + 1)
            need(act, f_down, T - back(th, 4) + 1)
            nc.scalar.activation(h_hi[:, th % 4, :], h_buf[:, th % 4, :], ACT.Copy).then_inc(f_hi, 1)

        def mix0_out(act, i):
            act.wait_ge(f_down, H0 * (i + 1))
            need(act, f_y, i)
            nc.scalar.activation(acc[:, :], bank[Y0][:, :], ACT.Copy).then_inc(f_yT, 1)

        def mix0_scalar(act, i, par, t, attention):
            T = H0 * i + t
            act.wait_ge(f_gate, T + 1)
            need(act, f_sg, T - back(t, 2) + 1)
            nc.scalar.activation(s_buf[:, t % 2, :], bank[G0][:, :], ACT.Silu).then_inc(f_silu, 1)
            side_scalar(act, 0, i, 3 * t, par, attention)
            side_scalar(act, 0, i, 3 * t + 1, par, attention)
            if t > 0 or not first(i):
                mix0_hi(act, T - 1, (t - 1) % H0)
            if t == 2 and not first(i):
                mix0_out(act, i - 1)
            side_scalar(act, 0, i, 3 * t + 2, par, attention)

        def mix0_add_prev(dve, i):
            dve.wait_ge(f_y, i)
            xb = x[:, (i + B - 1) % B, :, :].rearrange("p t d -> p (t d)")
            nc.vector.scalar_tensor_tensor(out=xb, in0=bank[S0][:, :], scalar=0.5, in1=xb,
                                           op0=ALU.mult, op1=ALU.add).then_inc(f_x, 1)

        def mix0_vector(dve, i, par, t, attention):
            T = H0 * i + t
            small_vector(dve, 0, i, 4 * t, par, attention)
            side_vector(dve, 0, i, 3 * t, par, attention)
            dve.wait_ge(f_silu, T + 1)
            dve.wait_ge(f_spread, T + 1)
            need(dve, f_h, T)
            nc.vector.tensor_tensor(sg_buf, bank[S0][:, :], s_buf[:, t % 2, :], ALU.mult).then_inc(f_sg, 1)
            small_vector(dve, 0, i, 4 * t + 1, par, attention)
            dve.wait_ge(f_sg, T + 1)
            dve.wait_ge(f_up, T + 1)
            need(dve, f_hi, T - back(t, 4) + 1)
            need(dve, f_lo, T - back(t, 4) + 1)
            nc.vector.tensor_tensor(h_buf[:, t % 4, :], bank[U0[t % 2]][:, :], sg_buf,
                                    ALU.mult).then_inc(f_h, 1)
            small_vector(dve, 0, i, 4 * t + 2, par, attention)
            side_vector(dve, 0, i, 3 * t + 1, par, attention)
            if t == 3 and not first(i):
                mix0_add_prev(dve, i)
            small_vector(dve, 0, i, 4 * t + 3, par, attention)
            side_vector(dve, 0, i, 3 * t + 2, par, attention)

        def mix0_lo(pool, T, th):
            pool.wait_ge(f_hi, T + 1)
            need(pool, f_down, T - back(th, 4) + 1)
            nc.gpsimd.tensor_tensor(h_lo[:, th % 4, :], h_buf[:, th % 4, :], h_hi[:, th % 4, :].bitcast(F32),
                                    ALU.subtract).then_inc(f_lo, 1)

        def mix0_gpsimd(pool, i, par, t, attention):
            T = H0 * i + t
            side_gpsimd(pool, 0, i, 3 * t, par, attention)
            side_gpsimd(pool, 0, i, 3 * t + 1, par, attention)
            if t > 0 or not first(i):
                mix0_lo(pool, T - 1, (t - 1) % H0)
            side_gpsimd(pool, 0, i, 3 * t + 2, par, attention)

        U1, Y1, S1, O1 = (0, 1), (2, 3), 4, 5
        hid, gs_buf, y_buf = fw[:, 0:4, :], fw[:, 4:6, :], fw[:, 6, :]
        LOW_POOL = (0, 6, 8, 11, 12, 14, 25, 26, 28, 30, 31)

        def low_half(j, t):
            j, t = (j - 1, t + H1) if t < 0 else (j, t)
            if t in LOW_POOL:
                return m_lo_p, len(LOW_POOL) * j + LOW_POOL.index(t) + 1
            return m_lo_v, (H1 - len(LOW_POOL)) * j + sum(u not in LOW_POOL for u in range(t)) + 1

        def mix1_down(pe, j, t):
            td = (t - 3) % H1
            pe.wait_ge(m_hi, H1 * j + t - 2)
            pe.wait_ge(*low_half(j, t - 3))
            if td % Q1 == 0:
                need(pe, m_y, E * j + (t - 3) // Q1 - 1)
            mm3(bank[Y1[td // Q1 % 2]][:, :], w1_hi[:, H1 + td, :], w1_lo[:, H1 + td, :],
                h_hi[:, td % 4, :], h_lo[:, td % 4, :], td % Q1 == 0, td % Q1 == Q1 - 1).then_inc(m_down, 1)

        def mix1_spread(pe, j, par, t):
            X = E * j + (t - 5) // Q1
            if t == 5:
                pe.wait_ge(gT_done, j + CALLS + 1)
            need(pe, m_gs, X)
            e = (t - 5) // Q1 % E
            mm(bank[S1][:, :], spread_b[:, cut(H0 + e)], gT[:, par if t >= 5 else 1 - par, :]).then_inc(m_spread, 1)

        def mix1_turn(pe, j):
            pe.wait_ge(m_acc, (E - 1) * (j + 1))
            need(pe, m_x, j)
            for t in range(TT):
                last = nc.tensor.transpose(bank[O1][:, cut(t)], acc[:, cut(t)], ident[:, :])
            last.then_inc(m_yT, 1)

        def mix1_tensor(pe, j, par, t, attention):
            T = H1 * j + t
            need(pe, m_hi, T - 1)
            mm3(bank[U1[t % 2]][:, :], w1_hi[:, t, :], w1_lo[:, t, :], xT_hi[:, par, :], xT_lo[:, par, :]).then_inc(m_up, 1)
            if t % Q1 == 1 and (t > 1 or not first(j)):
                mix1_spread(pe, j, par, t)
            side_tensor(pe, 1, j, 2 * t, par, attention)
            if t >= 3 or not first(j):
                mix1_down(pe, j, t)
            if t == 6 and not first(j):
                mix1_turn(pe, j - 1)
            side_tensor(pe, 1, j, 2 * t + 1, par, attention)

        def mix1_scalar(act, j, par, t, attention):
            T = H1 * j + t
            act.wait_ge(m_up, T + 1)
            need(act, *low_half(j, t - 4))
            nc.scalar.activation(hid[:, t % 4, :], bank[U1[t % 2]][:, :], ACT.Silu, bias=cols[:, t:t + 1]).then_inc(m_silu, 1)
            need(act, m_down, T - 3)
            nc.scalar.activation(h_hi[:, t % 4, :], bank[U1[t % 2]][:, :], ACT.Silu, bias=cols[:, t:t + 1]).then_inc(m_hi, 1)
            side_scalar(act, 1, j, 2 * t, par, attention)
            if t % Q1 == 1 and (t > 1 or not first(j)):
                mix1_move(act, j, t)
            side_scalar(act, 1, j, 2 * t + 1, par, attention)

        def mix1_move(act, j, t):
            X = E * j + (t - 5) // Q1
            act.wait_ge(m_spread, X + 1)
            need(act, m_y, X - 1)
            nc.scalar.activation(gs_buf[:, (t - 5) // Q1 % 2, :], bank[S1][:, :], ACT.Copy).then_inc(m_gs, 1)

        def mix1_gate(dve, j, t):
            X, e = E * j + (t - 7) // Q1, (t - 7) // Q1 % E
            run = j if t >= 7 else j - 1
            dve.wait_ge(m_down, H1 * j + t - 3)
            dve.wait_ge(m_gs, X + 1)
            if e == 0:
                need(dve, m_yT, run)
                dst = acc[:, :]
            else:
                need(dve, m_acc, (E - 1) * run + e - 1)
                dst = y_buf
            nc.vector.scalar_tensor_tensor(out=dst, in0=bank[Y1[e % 2]][:, :], scalar=cols[:, H1 + e:H1 + e + 1],
                                           in1=gs_buf[:, e % 2, :], op0=ALU.add, op1=ALU.mult).then_inc(m_y, 1)

        def mix1_add(dve, j, b):
            dve.wait_ge(m_yT, j + 1)
            xb = x[:, b, :, :].rearrange("p t d -> p (t d)")
            nc.vector.scalar_tensor_tensor(out=xb, in0=bank[O1][:, :], scalar=0.5, in1=xb,
                                           op0=ALU.mult, op1=ALU.add).then_inc(m_x, 1)

        def mix1_vector(dve, j, par, t, attention):
            T = H1 * j + t
            small_vector(dve, 1, j, 4 * t, par, attention)
            if t not in LOW_POOL:
                dve.wait_ge(m_hi, T + 1)
                need(dve, m_down, T - 3)
                nc.vector.tensor_tensor(h_lo[:, t % 4, :], hid[:, t % 4, :], h_hi[:, t % 4, :].bitcast(F32),
                                        ALU.subtract).then_inc(m_lo_v, 1)
            small_vector(dve, 1, j, 4 * t + 1, par, attention)
            side_vector(dve, 1, j, 2 * t, par, attention)
            small_vector(dve, 1, j, 4 * t + 2, par, attention)
            if t % Q1 == 3 and (t > 3 or not first(j)):
                mix1_gate(dve, j, t)
            if t == 6 and not first(j):
                mix1_add(dve, j - 1, (j + B - 1) % B)
            small_vector(dve, 1, j, 4 * t + 3, par, attention)
            side_vector(dve, 1, j, 2 * t + 1, par, attention)

        def mix1_sum(pool, j, t):
            X, e = E * j + (t - 7) // Q1, (t - 7) // Q1 % E
            run = j if t >= 7 else j - 1
            if e > 0:
                pool.wait_ge(m_y, X + 1)
                need(pool, m_acc, (E - 1) * run + e - 1)
                nc.gpsimd.tensor_tensor(acc[:, :], acc[:, :], y_buf, ALU.add).then_inc(m_acc, 1)

        def mix1_gpsimd(pool, j, par, t, attention):
            T = H1 * j + t
            if t in LOW_POOL:
                pool.wait_ge(m_hi, T + 1)
                need(pool, m_down, T - 3)
                nc.gpsimd.tensor_tensor(h_lo[:, t % 4, :], hid[:, t % 4, :], h_hi[:, t % 4, :].bitcast(F32),
                                        ALU.subtract).then_inc(m_lo_p, 1)
            side_gpsimd(pool, 1, j, 2 * t, par, attention)
            if t % Q1 == 0 and (t > 4 or not first(j)):
                mix1_sum(pool, j, t - 1)
            side_gpsimd(pool, 1, j, 2 * t + 1, par, attention)

        def runs(eng, tiles, step):
            for i in (0, 1):
                for t in range(tiles):
                    step(eng, i, i, t, False)
            with eng.Fori(0, B // 2) as pair:
                for par in (0, 1):
                    for t in range(tiles):
                        step(eng, pair * 2 + (2 + par), par, t, True)
            for i in (CALLS - 2, CALLS - 1):
                for t in range(tiles):
                    step(eng, i, i % 2, t, False)

        @block.tensor
        def _(pe):
            pe.wait_ge(const_in, 16)
            norm_tensor(pe, 0, 0)
            pe.wait_ge(set_up, 3)
            router_tensor(pe, 0, 0, 0, 0, "logits")
            pe.wait_ge(wt_in, 16 * 8)
            for k in range(10):
                last = nc.tensor.transpose(bank[k // 4][:, cut(k % 4)], rawt[:, k, :], ident[:, :])
                if k in (3, 7, 9):
                    last.then_inc(wt_ps, 1)
            pe.wait_ge(cols_in, 16 * 3)
            nc.tensor.transpose(bank[3][:, 0:H1 + E + 1], raw_cols, ident[0:H1 + E + 1, 0:H1 + E + 1]).then_inc(cols_ps, 1)
            router_tensor(pe, 0, 0, 0, 0, "gates")
            pe.wait_ge(w0_done, 3)
            pe.wait_ge(wt_done, 4)
            pe.wait_ge(set_up, 4)
            pe.wait_ge(spread_in, 16)
            runs(pe, H0, mix0_tensor)
            T = CALLS * H0
            for t in range(3):
                mix0_down(pe, T - 3 + t, H0 - 3 + t, CALLS - 1)
            pe.wait_ge(f_sg, T)
            mix0_turn(pe, CALLS)
            pe.wait_ge(f_x, CALLS)
            runs(pe, H1, mix1_tensor)
            for t in range(3):
                if t == 1:
                    mix1_spread(pe, CALLS, 0, t)
                mix1_down(pe, CALLS, t)
            mix1_turn(pe, CALLS - 1)

        @block.scalar
        def _(act):
            act.dma_start(ident_etc[:, :], a["c_const"]).then_inc(const_in, 16)
            for m, name in enumerate(["L0_ffn_w_gate", "L1_ffn_gate_w"]):
                act.dma_start(wgate[:, m, :], a[name]).then_inc(wgate_in, 16)
            act.dma_start(spread_b[:, :], a["c_spread"].bitcast(BF16)).then_inc(spread_in, 16)
            act.wait_ge(set_up, 1)
            nc.scalar.activation(small[:, 40:41], small[:, 0:1], ACT.Silu).then_inc(warm, 1)
            norm_scalar(act, 0, 0)
            for k in range(3):
                act.wait_ge(w0_in[k], 16)
                nc.scalar.activation(w0_hi[:, k * H0:(k + 1) * H0, :].rearrange("p a n -> p (a n)"),
                                     raw0[:, k * H0 * P:(k + 1) * H0 * P], ACT.Copy).then_inc(w0_hi_done, 1)
            for k in range(3):
                act.wait_ge(wt_ps, k + 1)
                w = min(4, 10 - 4 * k)
                nc.scalar.activation(wt_hi[:, 4 * k:4 * k + w, :].rearrange("p a n -> p (a n)"),
                                     bank[k][:, 0:w * P], ACT.Copy).then_inc(wt_hi_done, 1)
            router_scalar(act, 0, 0)
            runs(act, H0, mix0_scalar)
            mix0_hi(act, CALLS * H0 - 1, H0 - 1)
            mix0_out(act, CALLS - 1)
            runs(act, H1, mix1_scalar)
            mix1_move(act, CALLS, 1)

        @block.vector
        def _(dve):
            nc.vector.memset(base_e, float(np.e)).then_inc(set_up, 1)
            for n, count in enumerate((a_read, a_step, a_ps, a_pool)):
                nc.vector.memset(small[:, 36 + n:37 + n], 0.0).then_inc(count, 1)
            dve.wait_ge(x_in[0], 16)
            norm_vector(dve, 0, 0, "stats")
            for k in range(MOM):
                norm_moments(dve, 0, k)
            norm_vector(dve, 0, 0, "norm")
            dve.wait_ge(wgate_in, 16 * 2)
            nc.vector.tensor_copy(wgate_hi[:, :, :], wgate[:, :, :]).then_inc(set_up, 1)
            dve.wait_ge(set_up, 2)
            nc.vector.tensor_tensor(wgate_lo[:, :, :], wgate[:, :, :], wgate_hi[:, :, :].bitcast(F32),
                                    ALU.subtract).then_inc(set_up, 1)
            norm_vector(dve, 0, 0, "split", 0)
            for k in range(len(PICK)):
                if k in (0, 3, 7):
                    w = (0, 3, 7).index(k)
                    dve.wait_ge(w0_hi_done, w + 1)
                    nc.vector.tensor_tensor(w0_lo[:, w * H0:(w + 1) * H0, :].rearrange("p a n -> p (a n)"),
                                            raw0[:, w * H0 * P:(w + 1) * H0 * P],
                                            w0_hi[:, w * H0:(w + 1) * H0, :].rearrange("p a n -> p (a n)").bitcast(F32),
                                            ALU.subtract).then_inc(w0_done, 1)
                router_vector(dve, 0, 0, k)
                if k in (9, 11, 13):
                    w = (9, 11, 13).index(k)
                    dve.wait_ge(wt_hi_done, w + 1)
                    low, end = 4 * w, min(4 * w + 4, 10)
                    if low == WHOLE[0]:
                        low += len(WHOLE)
                        nc.vector.tensor_copy(wt_all[:, :, :].rearrange("p a n -> p (a n)"),
                                              bank[w][:, 0:(low - 4 * w) * P]).then_inc(wt_done, 1)
                    nc.vector.tensor_tensor(wt_lo[:, low:end, :].rearrange("p a n -> p (a n)"),
                                            bank[w][:, (low - 4 * w) * P:(end - 4 * w) * P],
                                            wt_hi[:, low:end, :].rearrange("p a n -> p (a n)").bitcast(F32),
                                            ALU.subtract).then_inc(wt_done, 1)
            dve.wait_ge(cols_ps, 1)
            nc.vector.tensor_copy(cols[:, :], bank[3][:, 0:H1 + E + 1]).then_inc(set_up, 1)
            for k in range(len(PICK), RT[0]):
                router_vector(dve, 0, 0, k)
            dve.wait_ge(late_in, 16 * 3)
            dve.wait_ge(rows_in, 16 * 14)
            for b in range(1, B):
                dve.wait_ge(x_in[b], 16)
            runs(dve, H0, mix0_vector)
            mix0_add_prev(dve, CALLS)
            runs(dve, H1, mix1_vector)
            mix1_gate(dve, CALLS, 3)
            mix1_add(dve, CALLS - 1, B - 1)

        @block.gpsimd
        def _(pool):
            nc.gpsimd.memset(neg_half, -0.5).then_inc(pool_set, 1)
            nc.gpsimd.memset(neg_half12[:, :], -0.5).then_inc(pool_set, 1)
            pool.wait_ge(pool_set, 2)
            norm_gpsimd(pool, 0)
            for t in range(TT):
                router_gpsimd(pool, 0, 0, t)
            runs(pool, H0, mix0_gpsimd)
            mix0_lo(pool, CALLS * H0 - 1, H0 - 1)
            runs(pool, H1, mix1_gpsimd)
            mix1_sum(pool, CALLS, -1)
            mix1_sum(pool, CALLS, 3)


INPUTS = ["L0_attn_x", "L0_attn_W_in", "L0_attn_W_out", "L0_attn_W_g1", "L0_attn_W_g2", "L0_attn_ln_w",
          "L0_ffn_w_gate", "L0_ffn_w_g", "L0_ffn_w_u", "L0_ffn_w_d",
          "L1_attn_Wq", "L1_attn_bq", "L1_attn_Wk", "L1_attn_bk", "L1_attn_Wv", "L1_attn_bv", "L1_attn_Wo", "L1_attn_bo",
          "L1_attn_gq", "L1_attn_betaq", "L1_attn_gk", "L1_attn_betak", "L1_attn_gv", "L1_attn_betav",
          "L1_attn_go", "L1_attn_betao", "L1_attn_scale",
          "L1_ffn_gate_w", "L1_ffn_gate_b", "L1_ffn_w1", "L1_ffn_b1", "L1_ffn_w2", "L1_ffn_b2"]


def kernel(**inputs):
    import concourse.bacc as bacc
    from concourse.bass_utils import run_bass_kernel_spmd

    nc = bacc.Bacc("TRN2", target_bir_lowering=False, num_devices=1)
    arrays, a = {}, {}

    def give(name, array):
        arrays[f"in_{name}"] = array
        a[name] = nc.dram_tensor(f"in_{name}", array.shape, mybir.dt.from_np(array.dtype), kind="ExternalInput").ap()

    for name in INPUTS:
        array = np.ascontiguousarray(inputs[name])
        give(name, array.reshape(1) if array.ndim == 0 else array)
    for name, array in shape_constants().items():
        give(name, array)
    out = nc.dram_tensor("out_x", (B, N, P), F32, kind="ExternalOutput").ap()
    macaron(nc, a, out)
    r = run_bass_kernel_spmd(nc, [arrays], core_ids=[0])
    return r.results[0]["out_x"]
```
